# Optimizing a Trainium2 kernel written in Bass

```python
import numpy as np
import jax
import jax.numpy as jnp

def _softmax(x, axis=-1):
    return jax.nn.softmax(x, axis=axis)

def _gelu(x):
    return jax.nn.gelu(x, approximate=True)

def _silu(x):
    return jax.nn.silu(x)

def _sigmoid(x):
    return jax.nn.sigmoid(x)

def _layernorm(x, axis=-1, eps=1e-05):
    m = jnp.mean(x, axis=axis, keepdims=True)
    v = jnp.var(x, axis=axis, keepdims=True)
    return (x - m) / jnp.sqrt(v + eps)

def _scatter_add(tgt, idx, src, axis=0):
    return tgt.at[idx].add(src)

def _segment_sum(src, seg, n):
    return jax.ops.segment_sum(src, seg, n)
kernel_name = 'mk_gnn_preln_d4_gnn_r32_79510f'

def setup_inputs(seed: int=0):
    np.random.seed(seed)
    _w = jnp.asarray

    def _rec_inputs():
        import jax
        import jax.numpy as jnp
        _gk = jax.random.key(seed)
        x = -8.776e-05 + 1 * jax.random.normal(jax.random.fold_in(_gk, 1), (3125, 256), jnp.float32)
        _s = jax.random.randint(jax.random.fold_in(_gk, 2), (25000,), 0, 3125, jnp.int32)
        _d = jax.random.randint(jax.random.fold_in(_gk, 3), (25000,), 0, 3125, jnp.int32)
        _loop = jnp.arange(3125, dtype=jnp.int32)
        src = jnp.concatenate([_s, _d, _loop])
        dst = jnp.concatenate([_d, _s, _loop])
        _o = jnp.argsort(dst, stable=True)
        src = src[_o]
        dst = dst[_o]
        edge_attr_64 = 1.36993e-05 + 0.999972 * jax.random.normal(jax.random.fold_in(_gk, 12), (53125, 64), jnp.float32)
        edge_weight = jax.random.uniform(jax.random.fold_in(_gk, 14), (53125,), jnp.float32, 0.0, 0.999998)
        return (x, src, dst, edge_attr_64, edge_weight)
    x, src, dst, edge_attr_64, edge_weight = _rec_inputs()

    def _L0_gnn_setup():
        import jax, jax.numpy as jnp
        import numpy as np
        N = 625
        E = 10000
        D = 256
        H = 8
        DH = D // H
        ED = 64
        FF = 4 * D
        EPS = 1e-05

        def _layernorm(x, g, b):
            m = jnp.mean(x, axis=-1, keepdims=True)
            v = jnp.var(x, axis=-1, keepdims=True)
            return (x - m) * jax.lax.rsqrt(v + EPS) * g + b

        def _edge_attention(xn, edge_index, ef, ew, Wq, bq, Wk, bk, Wv, bv, We, be, Wo, bo):
            n = xn.shape[0]
            scale = DH ** (-0.5)
            q = (xn @ Wq + bq).reshape(n, H, DH)
            k = (xn @ Wk + bk).reshape(n, H, DH)
            v = (xn @ Wv + bv).reshape(n, H, DH)
            src, dst = (edge_index[0], edge_index[1])
            ep = ef @ We + be
            scores = jnp.einsum('ehd,ehd->eh', q[dst], k[src] + ep[:, None, :]) * scale
            scores = scores * ew[:, None]
            m = jax.ops.segment_max(scores, dst, num_segments=n)
            m = jnp.where(jnp.isfinite(m), m, 0.0)
            ex = jnp.exp(scores - m[dst])
            s = jax.ops.segment_sum(ex, dst, num_segments=n)
            attn = ex / s[dst]
            out = jax.ops.segment_sum(attn[:, :, None] * v[src], dst, num_segments=n)
            out = out.reshape(n, D) @ Wo + bo
            return out
        key = jax.random.key(seed)
        ks = jax.random.split(key, 32)

        def lin_w(k, i, o):
            return (jax.random.normal(k, (i, o), jnp.float32) / np.sqrt(i)).astype(jnp.float32)
        return {'x': jax.random.normal(ks[0], (N, D), jnp.float32), 'edge_features': jax.random.normal(ks[1], (E, ED), jnp.float32), 'edge_weights': jax.random.uniform(ks[2], (E,), jnp.float32), 'edge_index': jax.random.randint(ks[3], (2, E), 0, N, dtype=jnp.int32), 'Wq': lin_w(ks[4], D, D), 'bq': jnp.zeros((D,), jnp.float32), 'Wk': lin_w(ks[5], D, D), 'bk': jnp.zeros((D,), jnp.float32), 'Wv': lin_w(ks[6], D, D), 'bv': jnp.zeros((D,), jnp.float32), 'We': lin_w(ks[7], ED, DH), 'be': jnp.zeros((DH,), jnp.float32), 'Wo': lin_w(ks[8], D, D), 'bo': jnp.zeros((D,), jnp.float32), 'ln1_g': jnp.ones((D,), jnp.float32), 'ln1_b': jnp.zeros((D,), jnp.float32), 'ln2_g': jnp.ones((D,), jnp.float32), 'ln2_b': jnp.zeros((D,), jnp.float32), 'W1': lin_w(ks[9], D, FF), 'b1': jnp.zeros((FF,), jnp.float32), 'W2': lin_w(ks[10], FF, D), 'b2': jnp.zeros((D,), jnp.float32), 'alpha': jnp.ones((1,), jnp.float32), 'beta': jnp.ones((1,), jnp.float32)}
    _L0_gnn_all = _L0_gnn_setup()
    _L0_gnn_in = {k: v for k, v in _L0_gnn_all.items() if k in ('Wq', 'bq', 'Wk', 'bk', 'Wv', 'bv', 'We', 'be', 'Wo', 'bo', 'ln1_g', 'ln1_b', 'ln2_g', 'ln2_b', 'W1', 'b1', 'W2', 'b2', 'alpha', 'beta')}
    del _L0_gnn_all

    def _L1_gnn_setup():
        import jax, jax.numpy as jnp
        import numpy as np
        C = 1.0
        SQC = 1.0
        MIN_NORM = 1e-15
        PROJ_EPS = 0.004

        def _norm(x):
            return jnp.clip(jnp.linalg.norm(x, axis=-1, keepdims=True), MIN_NORM)

        def logmap0(x):
            n = _norm(x)
            return jnp.arctanh(jnp.minimum(SQC * n, 1.0 - 1e-07)) * x / (SQC * n)

        def expmap0(u):
            n = _norm(u)
            return jnp.tanh(SQC * n) * u / (SQC * n)

        def proj(x):
            n = _norm(x)
            maxn = (1.0 - PROJ_EPS) / SQC
            return jnp.where(n > maxn, x / n * maxn, x)

        def mobius_add(x, y):
            x2 = jnp.sum(x * x, -1, keepdims=True)
            y2 = jnp.sum(y * y, -1, keepdims=True)
            xy = jnp.sum(x * y, -1, keepdims=True)
            num = (1.0 + 2.0 * C * xy + C * y2) * x + (1.0 - C * x2) * y
            den = 1.0 + 2.0 * C * xy + C * C * x2 * y2
            return num / jnp.clip(den, MIN_NORM)
        N, E, DIN, H, DH = (50000, 25000, 256, 4, 64)
        key = jax.random.key(seed)
        k1, k2, k3, k4, k5, k6, k7 = jax.random.split(key, 7)
        x = proj(0.01 * jax.random.normal(k1, (N, DIN), jnp.float32))
        src = jax.random.randint(k2, (E,), 0, N)
        off = jax.random.randint(k3, (E,), 1, N)
        dst = (src + off) % N
        edge_index = jnp.stack([src, dst]).astype(jnp.int64)
        glorot = float(np.sqrt(2.0 / (DIN + H * DH)))
        W = glorot * jax.random.normal(k4, (H * DH, DIN), jnp.float32)
        b_lin = 0.01 * jax.random.normal(k5, (H * DH,), jnp.float32)
        ga = float(np.sqrt(6.0 / (1 + 2 * DH)))
        att = jax.random.uniform(k6, (H, 2 * DH), jnp.float32, -ga, ga)
        b_conv = jnp.zeros((H * DH,), jnp.float32)
        return {'x': x, 'edge_index': edge_index, 'W': W, 'b_lin': b_lin, 'att': att, 'b_conv': b_conv}
    _L1_gnn_all = _L1_gnn_setup()
    _L1_gnn_in = {k: v for k, v in _L1_gnn_all.items() if k in ('W', 'b_lin', 'att', 'b_conv')}
    del _L1_gnn_all

    def _L2_gnn_setup():
        import jax, jax.numpy as jnp
        import numpy as np
        BLOCK_DIMS = [8] * 32

        def _mask_indices():
            d = sum(BLOCK_DIMS)
            mask = np.ones((d, d), dtype=np.int8)
            off = 0
            for b in BLOCK_DIMS:
                mask[off:off + b, off:off + b] = 0
                off += b
            rows, cols = np.nonzero(mask)
            return (d, rows.astype(np.int32), cols.astype(np.int32))
        key = jax.random.key(seed)
        k1, k2 = jax.random.split(key)
        d, rows, cols = _mask_indices()
        N = 15625
        X = jax.random.normal(k1, (N, d), dtype=jnp.float32)
        w_est = 0.1 * jax.random.normal(k2, (rows.shape[0],), dtype=jnp.float32)
        return {'X': X, 'w_est': w_est, 'rows': jnp.asarray(rows), 'cols': jnp.asarray(cols)}
    _L2_gnn_all = _L2_gnn_setup()
    _L2_gnn_in = {k: v for k, v in _L2_gnn_all.items() if k in ()}
    del _L2_gnn_all

    def _L3_gnn_setup():
        import jax, jax.numpy as jnp
        import numpy as np
        N_NODES = 50000
        N_EDGES = 25000
        IN_FEATS = 256
        HID = 64
        HEADS = 4
        OUT = 64

        def _gat_layer(x, src, dst, W, a_s, a_d, b, num_nodes):
            H, F = a_s.shape
            h = (x @ W).reshape(num_nodes, H, F)
            al_s = jnp.einsum('nhf,hf->nh', h, a_s)
            al_d = jnp.einsum('nhf,hf->nh', h, a_d)
            e = jax.nn.leaky_relu(al_s[src] + al_d[dst], 0.2)
            emax = jax.ops.segment_max(e, dst, num_segments=num_nodes)
            emax = jnp.where(jnp.isfinite(emax), emax, 0.0)
            ee = jnp.exp(e - emax[dst])
            denom = jax.ops.segment_sum(ee, dst, num_segments=num_nodes)
            alpha = ee / (denom[dst] + 1e-16)
            out = jax.ops.segment_sum(alpha[:, :, None] * h[src], dst, num_segments=num_nodes)
            return out.reshape(num_nodes, H * F) + b
        key = jax.random.key(seed)
        ks = jax.random.split(key, 16)
        p = lambda k, shape: jax.random.normal(k, shape, dtype=jnp.float32) * 0.05
        return {'x': jax.random.normal(ks[0], (N_NODES, IN_FEATS), dtype=jnp.float32), 'edge_index': jax.random.randint(ks[1], (2, N_EDGES), 0, N_NODES), 'W0': p(ks[2], (IN_FEATS, HEADS * HID)), 'as0': p(ks[3], (HEADS, HID)), 'ad0': p(ks[4], (HEADS, HID)), 'b0': jnp.zeros((HEADS * HID,), jnp.float32), 'W1': p(ks[5], (HEADS * HID, HEADS * HID)), 'as1': p(ks[6], (HEADS, HID)), 'ad1': p(ks[7], (HEADS, HID)), 'b1': jnp.zeros((HEADS * HID,), jnp.float32), 'W2': p(ks[8], (HEADS * HID, HEADS * OUT)), 'as2': p(ks[9], (HEADS, OUT)), 'ad2': p(ks[10], (HEADS, OUT)), 'b2': jnp.zeros((HEADS * OUT,), jnp.float32)}
    _L3_gnn_all = _L3_gnn_setup()
    _L3_gnn_in = {k: v for k, v in _L3_gnn_all.items() if k in ('W0', 'as0', 'ad0', 'b0', 'W1', 'as1', 'ad1', 'b1', 'W2', 'as2', 'ad2', 'b2')}
    del _L3_gnn_all
    return {'x': x, 'src': src, 'dst': dst, 'edge_attr_64': edge_attr_64, 'edge_weight': edge_weight, 'L0_gnn_Wq': _L0_gnn_in['Wq'], 'L0_gnn_bq': _L0_gnn_in['bq'], 'L0_gnn_Wk': _L0_gnn_in['Wk'], 'L0_gnn_bk': _L0_gnn_in['bk'], 'L0_gnn_Wv': _L0_gnn_in['Wv'], 'L0_gnn_bv': _L0_gnn_in['bv'], 'L0_gnn_We': _L0_gnn_in['We'], 'L0_gnn_be': _L0_gnn_in['be'], 'L0_gnn_Wo': _L0_gnn_in['Wo'], 'L0_gnn_bo': _L0_gnn_in['bo'], 'L0_gnn_ln1_g': _L0_gnn_in['ln1_g'], 'L0_gnn_ln1_b': _L0_gnn_in['ln1_b'], 'L0_gnn_ln2_g': _L0_gnn_in['ln2_g'], 'L0_gnn_ln2_b': _L0_gnn_in['ln2_b'], 'L0_gnn_W1': _L0_gnn_in['W1'], 'L0_gnn_b1': _L0_gnn_in['b1'], 'L0_gnn_W2': _L0_gnn_in['W2'], 'L0_gnn_b2': _L0_gnn_in['b2'], 'L0_gnn_alpha': _L0_gnn_in['alpha'], 'L0_gnn_beta': _L0_gnn_in['beta'], 'L1_gnn_W': _L1_gnn_in['W'], 'L1_gnn_b_lin': _L1_gnn_in['b_lin'], 'L1_gnn_att': _L1_gnn_in['att'], 'L1_gnn_b_conv': _L1_gnn_in['b_conv'], 'L3_gnn_W0': _L3_gnn_in['W0'], 'L3_gnn_as0': _L3_gnn_in['as0'], 'L3_gnn_ad0': _L3_gnn_in['ad0'], 'L3_gnn_b0': _L3_gnn_in['b0'], 'L3_gnn_W1': _L3_gnn_in['W1'], 'L3_gnn_as1': _L3_gnn_in['as1'], 'L3_gnn_ad1': _L3_gnn_in['ad1'], 'L3_gnn_b1': _L3_gnn_in['b1'], 'L3_gnn_W2': _L3_gnn_in['W2'], 'L3_gnn_as2': _L3_gnn_in['as2'], 'L3_gnn_ad2': _L3_gnn_in['ad2'], 'L3_gnn_b2': _L3_gnn_in['b2']}

def reference(x, src, dst, edge_attr_64, edge_weight, L0_gnn_Wq, L0_gnn_bq, L0_gnn_Wk, L0_gnn_bk, L0_gnn_Wv, L0_gnn_bv, L0_gnn_We, L0_gnn_be, L0_gnn_Wo, L0_gnn_bo, L0_gnn_ln1_g, L0_gnn_ln1_b, L0_gnn_ln2_g, L0_gnn_ln2_b, L0_gnn_W1, L0_gnn_b1, L0_gnn_W2, L0_gnn_b2, L0_gnn_alpha, L0_gnn_beta, L1_gnn_W, L1_gnn_b_lin, L1_gnn_att, L1_gnn_b_conv, L3_gnn_W0, L3_gnn_as0, L3_gnn_ad0, L3_gnn_b0, L3_gnn_W1, L3_gnn_as1, L3_gnn_ad1, L3_gnn_b1, L3_gnn_W2, L3_gnn_as2, L3_gnn_ad2, L3_gnn_b2):
    import jax
    import jax.numpy as jnp

    def _L0_gnn_ref(x, edge_features, edge_weights, edge_index, Wq, bq, Wk, bk, Wv, bv, We, be, Wo, bo, ln1_g, ln1_b, ln2_g, ln2_b, W1, b1, W2, b2, alpha, beta):
        import jax, jax.numpy as jnp
        import numpy as np
        N = 625
        E = 10000
        D = 256
        H = 8
        DH = D // H
        ED = 64
        FF = 4 * D
        EPS = 1e-05

        def _layernorm(x, g, b):
            m = jnp.mean(x, axis=-1, keepdims=True)
            v = jnp.var(x, axis=-1, keepdims=True)
            return (x - m) * jax.lax.rsqrt(v + EPS) * g + b

        def _edge_attention(xn, edge_index, ef, ew, Wq, bq, Wk, bk, Wv, bv, We, be, Wo, bo):
            n = xn.shape[0]
            scale = DH ** (-0.5)
            q = (xn @ Wq + bq).reshape(n, H, DH)
            k = (xn @ Wk + bk).reshape(n, H, DH)
            v = (xn @ Wv + bv).reshape(n, H, DH)
            src, dst = (edge_index[0], edge_index[1])
            ep = ef @ We + be
            scores = jnp.einsum('ehd,ehd->eh', q[dst], k[src] + ep[:, None, :]) * scale
            scores = scores * ew[:, None]
            m = jax.ops.segment_max(scores, dst, num_segments=n)
            m = jnp.where(jnp.isfinite(m), m, 0.0)
            ex = jnp.exp(scores - m[dst])
            s = jax.ops.segment_sum(ex, dst, num_segments=n)
            attn = ex / s[dst]
            out = jax.ops.segment_sum(attn[:, :, None] * v[src], dst, num_segments=n)
            out = out.reshape(n, D) @ Wo + bo
            return out
        xn = _layernorm(x, ln1_g, ln1_b)
        attn_out = _edge_attention(xn, edge_index, edge_features, edge_weights, Wq, bq, Wk, bk, Wv, bv, We, be, Wo, bo)
        x = x + alpha * attn_out
        xn = _layernorm(x, ln2_g, ln2_b)
        ff = jax.nn.gelu(xn @ W1 + b1, approximate=False) @ W2 + b2
        x = x + beta * ff
        return x

    def _L1_gnn_ref(x, edge_index, W, b_lin, att, b_conv):
        import jax, jax.numpy as jnp
        import numpy as np
        C = 1.0
        SQC = 1.0
        MIN_NORM = 1e-15
        PROJ_EPS = 0.004

        def _norm(x):
            return jnp.clip(jnp.linalg.norm(x, axis=-1, keepdims=True), MIN_NORM)

        def logmap0(x):
            n = _norm(x)
            return jnp.arctanh(jnp.minimum(SQC * n, 1.0 - 1e-07)) * x / (SQC * n)

        def expmap0(u):
            n = _norm(u)
            return jnp.tanh(SQC * n) * u / (SQC * n)

        def proj(x):
            n = _norm(x)
            maxn = (1.0 - PROJ_EPS) / SQC
            return jnp.where(n > maxn, x / n * maxn, x)

        def mobius_add(x, y):
            x2 = jnp.sum(x * x, -1, keepdims=True)
            y2 = jnp.sum(y * y, -1, keepdims=True)
            xy = jnp.sum(x * y, -1, keepdims=True)
            num = (1.0 + 2.0 * C * xy + C * y2) * x + (1.0 - C * x2) * y
            den = 1.0 + 2.0 * C * xy + C * C * x2 * y2
            return num / jnp.clip(den, MIN_NORM)
        N, E, DIN, H, DH = (50000, 25000, 256, 4, 64)
        n = x.shape[0]
        xh = proj(expmap0(logmap0(x) @ W.T))
        hb = proj(expmap0(b_lin[None, :]))
        xh = proj(mobius_add(xh, hb))
        loop = jnp.arange(n)
        src = jnp.concatenate([edge_index[0], loop])
        dst = jnp.concatenate([edge_index[1], loop])
        logx = logmap0(xh).reshape(H, n, DH)
        s_i = jnp.einsum('hnd,hd->nh', logx, att[:, :DH])
        s_j = jnp.einsum('hnd,hd->nh', logx, att[:, DH:])
        alpha = jax.nn.leaky_relu(s_i[dst] + s_j[src], 0.2)
        m = jax.ops.segment_max(alpha, dst, num_segments=n)
        a = jnp.exp(alpha - m[dst])
        ssum = jax.ops.segment_sum(a, dst, num_segments=n)
        a = a / jnp.clip(ssum[dst], MIN_NORM)
        xj = jnp.take(logx, src, axis=1).transpose(1, 0, 2)
        out = jax.ops.segment_sum(xj * a[:, :, None], dst, num_segments=n)
        out = out.transpose(1, 0, 2).reshape(n, H * DH) + b_conv
        out = jax.nn.relu(out)
        return proj(expmap0(out))

    def _L2_gnn_ref(X, w_est, rows, cols):
        import jax, jax.numpy as jnp
        import numpy as np
        BLOCK_DIMS = [8] * 32

        def _mask_indices():
            d = sum(BLOCK_DIMS)
            mask = np.ones((d, d), dtype=np.int8)
            off = 0
            for b in BLOCK_DIMS:
                mask[off:off + b, off:off + b] = 0
                off += b
            rows, cols = np.nonzero(mask)
            return (d, rows.astype(np.int32), cols.astype(np.int32))
        d = X.shape[1]
        W = jnp.zeros((d, d), dtype=X.dtype).at[rows, cols].set(w_est)
        return X @ W

    def _L3_gnn_ref(x, edge_index, W0, as0, ad0, b0, W1, as1, ad1, b1, W2, as2, ad2, b2):
        import jax, jax.numpy as jnp
        import numpy as np
        N_NODES = 50000
        N_EDGES = 25000
        IN_FEATS = 256
        HID = 64
        HEADS = 4
        OUT = 64

        def _gat_layer(x, src, dst, W, a_s, a_d, b, num_nodes):
            H, F = a_s.shape
            h = (x @ W).reshape(num_nodes, H, F)
            al_s = jnp.einsum('nhf,hf->nh', h, a_s)
            al_d = jnp.einsum('nhf,hf->nh', h, a_d)
            e = jax.nn.leaky_relu(al_s[src] + al_d[dst], 0.2)
            emax = jax.ops.segment_max(e, dst, num_segments=num_nodes)
            emax = jnp.where(jnp.isfinite(emax), emax, 0.0)
            ee = jnp.exp(e - emax[dst])
            denom = jax.ops.segment_sum(ee, dst, num_segments=num_nodes)
            alpha = ee / (denom[dst] + 1e-16)
            out = jax.ops.segment_sum(alpha[:, :, None] * h[src], dst, num_segments=num_nodes)
            return out.reshape(num_nodes, H * F) + b
        n = x.shape[0]
        loop = jnp.arange(n, dtype=edge_index.dtype)
        src = jnp.concatenate([edge_index[0], loop])
        dst = jnp.concatenate([edge_index[1], loop])
        h = _gat_layer(x, src, dst, W0, as0, ad0, b0, n)
        h = _gat_layer(h, src, dst, W1, as1, ad1, b1, n)
        h = _gat_layer(h, src, dst, W2, as2, ad2, b2, n)
        return h
    edge_index = jnp.stack([src, dst])
    h = jnp.maximum(_layernorm(x, axis=-1), 0.0)
    x = x + _L0_gnn_ref(h, edge_attr_64, edge_weight, edge_index, L0_gnn_Wq, L0_gnn_bq, L0_gnn_Wk, L0_gnn_bk, L0_gnn_Wv, L0_gnn_bv, L0_gnn_We, L0_gnn_be, L0_gnn_Wo, L0_gnn_bo, L0_gnn_ln1_g, L0_gnn_ln1_b, L0_gnn_ln2_g, L0_gnn_ln2_b, L0_gnn_W1, L0_gnn_b1, L0_gnn_W2, L0_gnn_b2, L0_gnn_alpha, L0_gnn_beta)
    h = jnp.maximum(_layernorm(x, axis=-1), 0.0)
    x = x + _L1_gnn_ref(h, edge_index, L1_gnn_W, L1_gnn_b_lin, L1_gnn_att, L1_gnn_b_conv)
    h = jnp.maximum(_layernorm(x, axis=-1), 0.0)
    x = x + _L2_gnn_ref(h, edge_weight, src, dst)
    h = jnp.maximum(_layernorm(x, axis=-1), 0.0)
    x = x + _L3_gnn_ref(h, edge_index, L3_gnn_W0, L3_gnn_as0, L3_gnn_ad0, L3_gnn_b0, L3_gnn_W1, L3_gnn_as1, L3_gnn_ad1, L3_gnn_b1, L3_gnn_W2, L3_gnn_as2, L3_gnn_ad2, L3_gnn_b2)
    return x

_drawn_inputs = setup_inputs


def setup_inputs(seed=0):
    import zlib

    import numpy as np

    out = dict(_drawn_inputs(seed))
    spreads = {'L0_gnn_bq': (0.0, 0.376),
     'L0_gnn_bk': (0.0, 0.8),
     'L0_gnn_bv': (0.0, 0.1),
     'L0_gnn_be': (0.0, 0.8),
     'L0_gnn_bo': (0.0, 0.1),
     'L0_gnn_ln1_g': (1.0, 0.2),
     'L0_gnn_ln1_b': (0.0, 0.1),
     'L0_gnn_ln2_g': (1.0, 0.2),
     'L0_gnn_ln2_b': (0.0, 0.1),
     'L0_gnn_b1': (0.0, 0.1),
     'L0_gnn_b2': (0.0, 0.1),
     'L1_gnn_b_conv': (0.0, 0.369),
     'L3_gnn_b0': (0.0, 0.1),
     'L3_gnn_b1': (0.0, 0.1),
     'L3_gnn_b2': (0.0, 0.1)}
    factors = {'L1_gnn_W': 97.2,
     'L1_gnn_b_lin': 200.0,
     'L1_gnn_att': 200.0,
     'L3_gnn_as0': 21.372,
     'L3_gnn_ad0': 64.0,
     'L3_gnn_as1': 64.0,
     'L3_gnn_ad1': 183.982,
     'L3_gnn_as2': 64.0,
     'L3_gnn_ad2': 191.34}
    for name, (base, spread) in spreads.items():
        noise = np.random.default_rng([zlib.crc32(name.encode()), seed]).standard_normal(out[name].shape)
        drawn = base * np.exp(spread * noise) if base else spread * noise
        out[name] = jnp.asarray(drawn.astype(out[name].dtype))
    for name, factor in factors.items():
        out[name] = (out[name] * factor).astype(out[name].dtype)
    return out
```

```python
from contextlib import ExitStack

import numpy as np

import concourse.bass as bass
from concourse import mybir

ALU = mybir.AluOpType
ACT = mybir.ActivationFunctionType
AX = mybir.AxisListType
F32 = mybir.dt.float32
BF16 = mybir.dt.bfloat16
I32 = mybir.dt.int32
ENGINE = mybir.EngineType

P = 128
N, D = 3125, 256
NP, NL = 125, 25
E = 53125
EL = E + N
T = -(-EL // P)
K = 8
J = 5
IT = T // (K * J)
G = IT * J
TP = T + K
EP = T * P
SL = 512
NS = EP // SL
FB = SL // P
ED = 64
DH0 = 32
H0, H1 = 8, 4
ROW = 4 + DH0
NB = N + 1
HI = NB // NL + 1 if NB % NL else NB // NL
ACOLS = N + P
FF = 4 * D
BIG = 1.0e30
LN_EPS = 1e-5
DONE0 = J
assert IT * J * K == T and NS * SL == EP and NL * NP == N


def node_rows(table, width):
    return table[0:N, 0:width].rearrange("(p l) d -> p l d", l=NL)


class Chain:

    def __init__(self, eng, sem):
        self.eng, self.sem, self.n, self.turn, self.per = eng, sem, 0, None, 0

    def __call__(self, ins):
        self.mark(ins)
        self.wait()

    def mark(self, ins):
        ins.then_inc(self.sem, 1)
        self.n += 1

    def wait(self, back=0):
        value = self.n - back
        if self.turn is not None:
            value = self.turn * self.per + value
        self.eng.wait_ge(self.sem, value)

    def loop(self, turns, per):
        outer = self

        class Loop:
            def __enter__(self):
                self.fori = outer.eng.Fori(0, turns)
                self.first = outer.n
                outer.turn, outer.per = self.fori.__enter__(), per
                return outer.turn

            def __exit__(self, *e):
                assert e[0] is not None or outer.n - self.first == per, (outer.n - self.first, per)
                self.fori.__exit__(*e)
                outer.turn, outer.n = None, self.first + turns * per if isinstance(turns, int) else None

        return Loop()


class Signal:

    def __init__(self, sem):
        self.sem, self.total, self.base = sem, 0, {}

    def plan(self, stage, n):
        self.base[stage] = self.total
        self.total += n


class Turns:

    def __init__(self, sem):
        self.sem, self.sent, self.seen = sem, 0, {}

    def send(self, ins, n=1):
        self.sent += n
        ins.then_inc(self.sem, n)

    def receive(self, eng, n=1):
        self.seen[eng.engine] = self.seen.get(eng.engine, 0) + n
        eng.wait_ge(self.sem, self.seen[eng.engine])


class Memory:
    pass


def place_memory(nc, ctx, stop=None):
    m = Memory()
    m.nc = nc

    def sb(name, shape, dt=F32):
        return ctx.enter_context(nc.sbuf_tensor("sb_" + name, shape, dt))

    def sem(name):
        return ctx.enter_context(nc.semaphore(name))

    def dram(name, shape, dt=F32):
        return nc.dram_tensor(name, shape, dt, kind="Internal").ap()

    m.sb, m.sem, m.dram = sb, sem, dram
    m.x = sb("x", [P, NL, D])
    m.h = sb("h", [P, NL, D])
    m.sums = sb("sums", [P, 4 * ACOLS])
    m.acc = m.sums[:, :].rearrange("p (a f c) -> p a f c", a=2, f=2)
    m.rows = sb("rows", [P, J * K, D])
    m.sel = sb("sel", [P, J * K, P])
    m.w1 = sb("w1", [P, 2, FF])
    m.w2 = sb("w2", [P, FF // P, D])
    m.consts = sb("consts", [P, 7, P])
    (m.iota, m.before, m.after, m.ident, m.first_row, m.shift_on,
     m.shift_back) = (m.consts[:, i, :] for i in range(7))
    m.edge = sb("edge", [P, T * 2 * 4])
    m.fields = m.edge[:, 0:T * 4].rearrange("p (t f) -> p t f", f=4)
    m.src_i = sb("src_i", [P, TP], I32)
    m.src_now = sb("src_now", [P, J, K], I32)
    m.start_i = sb("start_i", [P, NL], I32)
    m.banks = [ctx.enter_context(nc.psum_tensor(f"bank{i}", [P, 512], F32)) for i in range(8)]
    m.sorted = dram("sorted_edges", [EP, ROW])
    m.loc = sb("loc", [P, TP], BF16)
    m.base_i = sb("base_i", [P, T], I32)
    m.flags = sb("flags", [P, 3, SL])
    m.goes_on, m.has_next, m.at_start = (m.flags[0:NS, i, :] for i in range(3))
    m.small = sb("small", [P, 192])
    m.fields_sorted = m.w1[:, :, :].rearrange("p a c -> p (a c)")[:, 0:4 * T].rearrange("p (t f) -> p t f", f=4)
    m.digit_rows = dram("digit_rows", [2, EP], BF16)
    m.q_table = dram("q_table", [ACOLS, D])
    m.k_table = dram("k_table", [N, D])
    m.row_table = dram("row_table", [N, D])
    m.dst_table = dram("dst_table", [N, H1])
    m.flat = dram("flat_rows", [N * D])
    m.at_starts = dram("at_starts", [EP, H1])
    m.landed = [sem(f"landed{j}") for j in range(J)]
    m.rows_free = Signal(sem("rows_free"))
    m.taken = Signal(sem("sources_taken"))
    m.vector_step = sem("vector_step")
    m.scalar_step = sem("scalar_step")
    m.pool_step = sem("pool_step")
    return m



def place_sort(m):
    s = m.s = Memory()
    a = m.sums
    at = 0

    def cut(n):
        nonlocal at
        at += n
        return a[:, at - n:at]

    s.src0 = cut(T).bitcast(I32)
    s.dst0 = cut(T).bitcast(I32)
    s.hi = cut(T)
    s.lo = cut(T)
    s.t1 = cut(T)
    s.t2 = cut(T)
    s.one_hi = cut(J * K * HI // 2).bitcast(BF16).rearrange("p (j k h) -> p j k h", j=J, k=K)
    s.one_lo = cut(J * K * NL // 2).bitcast(BF16).rearrange("p (j k l) -> p j k l", j=J, k=K)
    s.payload = cut(J * K * ROW).rearrange("p (j k r) -> p j k r", j=J, k=K)
    s.place = cut(J * NL * K).rearrange("p (j l k) -> p j l k", j=J, l=NL)
    s.incl = cut(NL * K)
    s.excl = cut(NL * K)
    s.keep = cut(NL * K)
    s.now = cut(NL)
    s.count = cut(NL)
    s.zeros = cut(K).bitcast(I32)
    s.pos_now = cut(J * K).bitcast(I32).rearrange("p (j k) -> p j k", j=J)
    s.rowsum = cut(1)
    s.rank = cut(J * K).rearrange("p (j k) -> p j k", j=J)
    s.found = cut(J * K).rearrange("p (j k) -> p j k", j=J)
    s.junk = cut(K * P)
    s.dst_now = cut(J * K).rearrange("p (j k) -> p j k", j=J)
    s.picked = cut(K * NL)
    s.weights = cut(DH0)
    assert at <= 4 * ACOLS
    s.hi_t = m.sel[:, :, :].rearrange("p (j k) c -> p j (k c)", j=J)
    r = m.rows[:, :, :].rearrange("p t d -> p (t d)")
    s.ef = r[:, 0:J * K * P].rearrange("p (j c) -> p j c", j=J)
    s.dst_row = r[:, J * K * P:2 * J * K * P].bitcast(I32).rearrange("p (j c) -> p j c", j=J)
    s.ident_bf = cut(P // 2).bitcast(BF16)
    s.zero_bf = cut(P // 2).bitcast(BF16)
    s.place_i = cut(J * K).bitcast(I32).rearrange("p (j k) -> p j k", j=J)
    assert at <= 4 * ACOLS
    s.inputs = m.sem("sort_inputs")
    s.ready = m.sem("sort_ready")
    s.digits = m.sem("sort_digits")
    s.digits_free = m.sem("sort_digits_free")
    s.counted = m.sem("sort_counted")
    s.summed = m.sem("sort_summed")
    s.sum_done = m.sem("sort_sum_done")
    s.tile_counted = m.sem("sort_tile_counted")
    s.turned = m.sem("sort_turned")
    s.turned_read = m.sem("sort_turned_read")
    s.placed = m.sem("sort_placed")
    s.look_read = m.sem("sort_look_read")
    s.projected_read = m.sem("sort_projected_read")
    s.row_free = m.sem("sort_row_free")
    s.ef_free = m.sem("sort_ef_free")
    s.pos_ready = m.sem("sort_pos_ready")
    s.taken = m.sem("sort_taken")
    s.fields_in = m.sem("sort_fields_in")
    s.sent_all = m.sem("sort_sent_all")
    s.row_in = [m.sem(f"sort_row_in{j}") for j in range(J)]
    s.ef_in = [m.sem(f"sort_ef_in{j}") for j in range(J)]
    s.sent = [m.sem(f"sort_sent{j}") for j in range(J)]


def sort_sync(m, io, sp):
    s = m.s
    sp.dma_start(s.src0[:, 0:T], io["src_tiles"]).then_inc(s.inputs, 16)
    sp.dma_start(s.dst0[:, 0:T], io["dst_tiles"]).then_inc(s.inputs, 16)
    sp.dma_start(s.t1[:, 0:T], io["weight_tiles"]).then_inc(s.inputs, 16)
    sp.dma_start(s.t2[:, 0:T], io["given_tiles"]).then_inc(s.inputs, 16)
    sp.dma_start(s.weights[0:ED + 1, :], io["We"]).then_inc(s.inputs, 16)
    with sp.Fori(0, IT) as it:
        for j in range(J):
            g = it * J + j
            sp.wait_ge(s.row_free, g + 1)
            sp.dma_start(s.dst_row[:, j, :], io["dst_row"][0:1, bass.ds(g * K * P, K * P)].to_broadcast([P, K * P])
                         ).then_inc(s.row_in[j], 16)
            sp.wait_ge(s.ef_free, g + 1)
            sp.dma_start(s.ef[0:ED + 1, j, :], io["efT"][:, bass.ds(g * K * P, K * P)]).then_inc(s.ef_in[j], 16)


def digits_of_group(m, dve, g, j, signal):
    s = m.s
    for one, digit, width in ((s.one_hi, s.hi, HI), (s.one_lo, s.lo, NL)):
        dve.tensor_tensor(one[:, j], m.iota[:, 0:width].unsqueeze(1).to_broadcast([P, K, width]),
                          digit[:, bass.ds(g * K, K)].unsqueeze(2).to_broadcast([P, K, width]),
                          ALU.is_equal).then_inc(signal, 1)


def sort_vector(m, dve, step):
    s = m.s
    dve.sem_inc(s.row_free, J)
    dve.wait_ge(s.inputs, 80)
    step.mark(dve.tensor_copy(m.fields[:, :, 0], s.src0[:, :]))
    step.mark(dve.tensor_copy(m.fields[:, :, 1], s.dst0[:, :]))
    step.mark(dve.tensor_copy(m.fields[:, :, 2], s.t1[:, :]))
    step.mark(dve.tensor_copy(m.fields[:, :, 3], s.t2[:, :]))
    step(dve.memset(s.zero_bf[:, :], 0.0))
    dve.tensor_copy(s.ident_bf[:, :], m.ident).then_inc(s.ready, 1)
    dst = m.fields[:, :, 1]
    step(dve.tensor_scalar(s.t1[:, :], dst, 1.0 / NL, -(0.5 - 0.5 / NL), ALU.mult, ALU.add))
    step(dve.tensor_scalar(s.t2[:, :], s.t1[:, :], 12582912.0, None, ALU.add))
    step(dve.tensor_scalar(s.hi[:, :], s.t2[:, :], -12582912.0, None, ALU.add))
    step(dve.scalar_tensor_tensor(s.lo[:, :], s.hi[:, :], -float(NL), dst, ALU.mult, ALU.add))
    with dve.Fori(0, IT) as it:
        for j in range(J):
            g = it * J + j
            dve.wait_ge(s.digits_free, g + 1)
            digits_of_group(m, dve, g, j, s.digits)
    dve.wait_ge(s.counted, 1)
    step(dve.tensor_copy(s.count[0:HI, :], m.banks[0][0:HI, 0:NL]))
    dve.tensor_reduce(s.rowsum[0:HI, :], s.count[0:HI, :], AX.X, ALU.add).then_inc(s.summed, 1)
    step(dve.memset(s.excl[0:HI, 0:NL], 1.0))
    dve.wait_ge(s.sum_done, 1)
    step(dve.tensor_copy(s.rowsum[0:HI, :], m.banks[0][0:HI, 64:65]))
    step(dve.tensor_tensor_scan(s.incl[0:HI, 0:NL], s.excl[0:HI, 0:NL], s.count[0:HI, :],
                                s.rowsum[0:HI, :], ALU.mult, ALU.add))
    step(dve.tensor_tensor(s.now[0:HI, :], s.incl[0:HI, 0:NL], s.count[0:HI, :], ALU.subtract))
    step(dve.tensor_copy(m.start_i[0:NP, :], s.now[0:NP, :]))
    step(dve.memset(s.keep[:, :], 1.0))
    step(dve.memset(s.keep[:, :].rearrange("p (l k) -> p l k", k=K)[:, :, 0:1], 0.0))
    with step.loop(IT, J * 5) as it:
        for j in range(J):
            g = it * J + j
            dve.wait_ge(s.digits_free, G + g + 1)
            digits_of_group(m, dve, g, j, s.digits)
            step.mark(dve.tensor_copy(s.dst_now[:, j, :], m.fields[:, bass.ds(g * K, K), 1]))
            dve.wait_ge(s.tile_counted, g + 1)
            count = m.banks[1][0:HI, 0:NL * K]
            now = s.now[0:HI, :]
            incl = s.incl[0:HI, :].rearrange("p (l k) -> p l k", k=K)
            excl = s.excl[0:HI, :].rearrange("p (l k) -> p l k", k=K)
            step(dve.tensor_tensor_scan(s.incl[0:HI, :], s.keep[0:HI, :], count, 0.0, ALU.mult, ALU.add))
            step(dve.tensor_tensor(s.excl[0:HI, :], s.incl[0:HI, :], count, ALU.subtract))
            dve.tensor_tensor(s.place[0:HI, j], excl, now.unsqueeze(2).to_broadcast([HI, NL, K]),
                              ALU.add).then_inc(s.placed, 1)
            dve.wait_ge(s.placed, g + 1)
            step(dve.tensor_tensor(now, now, incl[:, :, K - 1], ALU.add))
            dve.wait_ge(s.row_in[j], 16 * it + 16)
            for k in range(K):
                last = dve.scalar_tensor_tensor(
                    s.junk[:, k * P:(k + 1) * P], s.dst_row[:, j, k * P:(k + 1) * P], s.dst_now[:, j, k:k + 1],
                    m.before, ALU.is_equal, ALU.mult, accum_out=s.rank[:, j, k:k + 1])
            last.then_inc(s.row_free, 1)
            dve.wait_ge(s.digits_free, J + G + g + 1)
            dve.tensor_tensor(s.picked[:, :], m.banks[3][:, 0:K * NL],
                              s.one_lo[:, j].rearrange("p k l -> p (k l)"), ALU.mult).then_inc(s.look_read, 1)
            dve.wait_ge(s.look_read, g + 1)
            step(dve.tensor_reduce(s.found[:, j, :], s.picked[:, :].rearrange("p (k l) -> p k l", l=NL),
                                   AX.X, ALU.add))
            dve.wait_ge(s.row_free, J + g + 1)
            dve.wait_ge(s.taken, g + 1)
            dve.tensor_tensor(s.place_i[:, j, :], s.found[:, j, :], s.rank[:, j, :], ALU.add).then_inc(s.pos_ready, 1)
    dve.wait_ge(s.pos_ready, G)
    dve.sem_inc(s.pos_ready, 1)


def sort_tensor(m, pe):
    s = m.s
    pe.sem_inc(s.digits_free, J)
    pe.sem_inc(s.ef_free, J)
    pe.wait_ge(s.inputs, 80)
    pe.wait_ge(s.ready, 1)
    total = m.banks[0][0:HI, 0:NL]
    pe.matmul(total, s.zero_bf[:, 0:HI], s.zero_bf[:, 0:NL], start=True, stop=False, skip_group_check=True)
    with pe.Fori(0, IT) as it:
        for j in range(J):
            g = it * J + j
            pe.wait_ge(s.digits, 2 * g + 2)
            for k in range(K):
                last = pe.matmul(total, s.one_hi[:, j, k], s.one_lo[:, j, k], start=False, stop=False,
                                 skip_group_check=True)
            last.then_inc(s.digits_free, 1)
    pe.matmul(total, s.zero_bf[:, 0:HI], s.zero_bf[:, 0:NL], start=False, stop=True,
              skip_group_check=True).then_inc(s.counted, 1)
    pe.wait_ge(s.summed, 1)
    pe.matmul(m.banks[0][0:HI, 64:65], m.after[0:HI, 0:HI], s.rowsum[0:HI, :], start=True, stop=True
              ).then_inc(s.sum_done, 1)
    turned = m.banks[2][:, :].bitcast(BF16)
    with pe.Fori(0, IT) as it:
        for j in range(J):
            g = it * J + j
            pe.wait_ge(s.digits, 2 * G + 2 * g + 2)
            pe.wait_ge(s.placed, g)
            for k in range(K):
                count = m.banks[1][0:HI, 0:NL * K].rearrange("p (l k) -> p l k", k=K)[:, :, k]
                last = pe.matmul(count, s.one_hi[:, j, k], s.one_lo[:, j, k], start=True, stop=True)
            last.then_inc(s.tile_counted, 1)
            pe.wait_ge(s.turned_read, g)
            for k in range(K):
                last = pe.transpose(turned[0:HI, k * P:(k + 1) * P], s.one_hi[:, j, k], s.ident_bf[:, :])
            last.then_inc(s.turned, 1)
            pe.wait_ge(s.ef_in[j], 16 * it + 16)
            pe.wait_ge(s.projected_read, g)
            for k in range(K):
                last = pe.matmul(m.banks[4][:, k * DH0:(k + 1) * DH0], s.ef[0:ED + 1, j, k * P:(k + 1) * P],
                                 s.weights[0:ED + 1, :], start=True, stop=True)
            last.then_inc(s.ef_free, 1)
            pe.wait_ge(s.turned_read, g + 1)
            pe.wait_ge(s.placed, g + 1)
            pe.wait_ge(s.look_read, g)
            for k in range(K):
                last = pe.matmul(m.banks[3][:, k * NL:(k + 1) * NL], s.hi_t[0:HI, j, k * P:(k + 1) * P],
                                 s.place[0:HI, j, :, k], start=True, stop=True)
            last.then_inc(s.digits_free, 1)


def sort_scalar(m, act):
    s = m.s
    turned = m.banks[2][:, :].bitcast(BF16)
    with act.Fori(0, IT) as it:
        for j in range(J):
            g = it * J + j
            act.wait_ge(s.turned, g + 1)
            act.activation(s.hi_t[0:HI, j, :], turned[0:HI, :], ACT.Copy).then_inc(s.turned_read, 1)
            act.wait_ge(s.sent[j], 16 * K * it)
            act.activation(s.payload[:, j, :, 0:4], m.fields[:, bass.ds(g * K, K), :],
                           ACT.Copy).then_inc(s.fields_in, 1)
            act.wait_ge(s.ef_free, J + g + 1)
            act.activation(s.payload[:, j, :, 4:ROW], m.banks[4][:, 0:K * DH0].rearrange("p (k d) -> p k d", k=K),
                           ACT.Copy).then_inc(s.projected_read, 1)


def sort_pool(m, pool):
    s = m.s

    def take(g, j):
        pool.tensor_tensor(s.pos_now[:, j, :], s.place_i[:, j, :], s.zeros[:, :], ALU.add).then_inc(s.taken, 1)

    pool.sem_inc(s.taken, J)
    pool.memset(s.zeros[:, :], 0).then_inc(m.pool_step, 1)
    pool.wait_ge(m.pool_step, 1)
    pool.wait_ge(s.pos_ready, 1)
    take(0, 0)
    with pool.Fori(0, IT) as it:
        for j in range(J):
            g = it * J + j
            pool.wait_ge(s.fields_in, g + 1)
            pool.wait_ge(s.projected_read, g + 1)
            pool.wait_ge(s.taken, J + g + 1)
            nxt = (j + 1) % J
            pool.wait_ge(s.sent[nxt], 16 * K * (it + (nxt == 0)))
            pool.wait_ge(s.pos_ready, g + 2)
            take(g + 1, nxt)
            for k in range(K):
                pool.indirect_dma_start(out=m.sorted[:, :],
                                        out_offset=bass.IndirectOffsetOnAxis(ap=s.pos_now[:, j, k:k + 1], axis=0),
                                        in_=s.payload[:, j, k, :], in_offset=None).then_inc(s.sent[j], 16)
    for j in range(J):
        pool.wait_ge(s.sent[j], 16 * K * IT)
    pool.wait_ge(s.taken, J + G + 1)
    pool.sem_inc(s.sent_all, 1)



GATHERS = ["keys", "values"] + [f"rows{i}" for i in range(4)]


def plan_gathers(m):
    m.rows_free.total = J
    for n, stage in enumerate(GATHERS):
        m.rows_free.plan(stage, G)
        m.taken.plan(stage, G + 1)


def landed(m, eng, stage, it, j):
    eng.wait_ge(m.landed[j], 16 * K * (IT * GATHERS.index(stage) + it + 1))


def gather(m, pool, stage, table, width):
    b, t = m.rows_free.base[stage], m.taken.base[stage]

    def take(g, j):
        pool.tensor_copy(m.src_now[:, j, :], m.src_i[:, bass.ds(g * K, K)]).then_inc(m.taken.sem, 1)

    if t:
        pool.wait_ge(m.taken.sem, t)
        for j in range(J):
            pool.wait_ge(m.landed[j], 16 * K * IT * GATHERS.index(stage))
    take(0, 0)
    with pool.Fori(0, IT) as it:
        for j in range(J):
            g = it * J + j
            pool.wait_ge(m.taken.sem, t + g + 1)
            pool.wait_ge(m.rows_free.sem, b - J + g + 1)
            nxt = (j + 1) % J
            pool.wait_ge(m.landed[nxt], 16 * K * (IT * GATHERS.index(stage) + it + (nxt == 0)))
            take(g + 1, nxt)
            for k in range(K):
                out = m.rows[:, j * K + k, 0:width]
                pool.indirect_dma_start(out=out, out_offset=None, in_=table[:, :],
                                        in_offset=bass.IndirectOffsetOnAxis(ap=m.src_now[:, j, k:k + 1], axis=0)
                                        ).then_inc(m.landed[j], 16)



def place_scores(m):
    s = m.sc = Memory()
    s.q_win = m.sums[:, 0:J * K * D].rearrange("p (t d) -> p t d", d=D)
    s.edges = m.sums[:, J * K * D:J * K * (D + ROW)].rearrange("p (j k r) -> p j k r", j=J, k=K)
    at = J * K * (D + ROW)
    s.weight = m.sums[:, at:at + K]
    s.dots = m.sums[:, at + K:at + K + K * H0]
    sel = m.sel[:, :, :].rearrange("p a c -> p (a c)")
    at = 12 * P
    s.digits = sel[:, at:at + 3 * T].rearrange("p (a t) -> p a t", a=3)
    s.digit_strips = sel[0:NS, at + 3 * T:at + 3 * T + SL].bitcast(BF16).rearrange("p (a c) -> p a c", a=2)
    s.turned = m.w2[:, 0:4, :].rearrange("p (a b) (c e) -> p a (b c) e", a=2, e=P)
    s.fields_in = m.sem("scores_fields_in")
    s.numbers_in = m.sem("scores_numbers_in")
    s.base_out = m.sem("scores_base_out")
    s.digits_there = m.sem("scores_digits_there")
    s.digits_turned = m.sem("scores_digits_turned")
    s.digits_in_strips = m.sem("scores_digits_in_strips")
    s.digits_stored = m.sem("scores_digits_stored")
    s.edges_free = m.sem("scores_edges_free")
    s.chosen = m.sem("scores_chosen")
    s.sel_turned = m.sem("scores_sel_turned")
    s.sel_copied = m.sem("scores_sel_copied")
    s.q_done = m.sem("scores_q_done")
    s.q_read = m.sem("scores_q_read")
    s.win_free = m.sem("scores_win_free")
    s.edges_in = [m.sem(f"scores_edges_in{j}") for j in range(J)]
    s.win_in = [m.sem(f"scores_win_in{j}") for j in range(J)]


def fields_sync(m, sp):
    s = m.sc
    sp.wait_ge(m.s.sent_all, 1)
    part = T // IT
    for i in range(IT):
        sp.dma_start(m.fields_sorted[:, i * part:(i + 1) * part, :],
                     m.sorted.rearrange("(t p) r -> p t r", p=P)[:, i * part:(i + 1) * part, 0:4]
                     ).then_inc(s.fields_in, 16)
    sp.wait_ge(s.digits_in_strips, 1)
    sp.dma_start(m.digit_rows.rearrange("a (s c) -> s a c", s=NS), s.digit_strips).then_inc(s.digits_stored, 16)


def fields_scalar(m, act):
    s = m.sc
    act.wait_ge(s.fields_in, 16 * IT)
    act.activation(m.src_i[:, 0:T], m.fields_sorted[:, :, 0], ACT.Copy).then_inc(s.numbers_in, 1)
    act.activation(m.base_i[0:1, :], m.fields_sorted[0:1, :, 1], ACT.Copy).then_inc(s.numbers_in, 1)


def fields_tensor(m, pe):
    s = m.sc
    pe.wait_ge(s.fields_in, 16 * IT)
    pe.matmul(m.banks[4][:, 0:T], m.first_row, m.fields_sorted[:, :, 1], start=True, stop=True
              ).then_inc(s.base_out, 1)
    pe.wait_ge(s.digits_there, 1)
    for a in range(2):
        for b in range(FB):
            last = pe.transpose(m.banks[5 + a][0:NS, b * P:(b + 1) * P], s.digits[:, a, b::FB], m.ident)
        last.then_inc(s.digits_turned, 1)


def fields_vector(m, dve, step):
    s = m.sc
    dve.wait_ge(s.fields_in, 16 * IT)
    source = m.fields_sorted[:, :, 0]
    high, low, t = s.digits[:, 0, :], s.digits[:, 1, :], s.digits[:, 2, :]
    step(dve.tensor_scalar(t, source, 1.0 / NL, -(0.5 - 0.5 / NL), ALU.mult, ALU.add))
    step(dve.tensor_scalar(t, t, 12582912.0, None, ALU.add))
    step(dve.tensor_scalar(high, t, -12582912.0, None, ALU.add))
    dve.scalar_tensor_tensor(low, high, -float(NL), source, ALU.mult, ALU.add).then_inc(s.digits_there, 1)
    dve.wait_ge(s.base_out, 1)
    step.mark(dve.memset(m.loc[:, T:TP], 0.0))
    step(dve.tensor_tensor(m.loc[:, 0:T], m.fields_sorted[:, :, 1], m.banks[4][:, 0:T], ALU.subtract))
    dve.wait_ge(s.digits_turned, 2)
    step.mark(dve.tensor_copy(s.digit_strips[:, 0, :], m.banks[5][0:NS, :]))
    dve.tensor_copy(s.digit_strips[:, 1, :], m.banks[6][0:NS, :]).then_inc(s.digits_in_strips, 1)


def scores_sync(m, sp):
    s = m.sc
    sp.wait_ge(s.numbers_in, 2)
    with sp.Fori(0, IT) as it:
        for j in range(J):
            g = it * J + j
            sp.wait_ge(s.edges_free, g + 1)
            sp.dma_start(s.edges[:, j], m.sorted.rearrange("(g k p) r -> p g k r", k=K, p=P)[:, bass.ds(g, 1), :, :]
                         .rearrange("p g k r -> p (g k) r")).then_inc(s.edges_in[j], 16)
            sp.wait_ge(s.win_free, g + 1)
            first = windows(m, ENGINE.SP, g)
            for k in range(K):
                sp.dma_start(s.q_win[:, j * K + k, :], m.q_table[bass.ds(first[k], P), :]).then_inc(s.win_in[j], 16)


def windows(m, engine, g):
    _, first = m.nc.values_load_multi_w_load_instructions(
        m.base_i[0:1, bass.ds(g * K, K)], engines=[engine], min_val=0, max_val=N,
        skip_runtime_bounds_check_because="they are node numbers, 0 to N with the padding's")
    return first


def scores_scalar(m, act):
    s = m.sc
    with act.Fori(0, IT) as it:
        for j in range(J):
            g = it * J + j
            for half in range(2):
                act.wait_ge(s.sel_turned, 2 * g + half + 1)
                act.wait_ge(s.q_done, 4 * g)
                act.activation(s.turned[:, half], m.banks[1 + half][:, :].rearrange("p (k e) -> p k e", e=P),
                               ACT.Copy).then_inc(s.sel_copied, 1)


def scores_tensor(m, pe):
    s = m.sc
    with pe.Fori(0, IT) as it:
        for j in range(J):
            g = it * J + j
            pe.wait_ge(s.chosen, g + 1)
            for half in range(2):
                pe.wait_ge(s.sel_copied, 2 * g)
                for k in range(4):
                    last = pe.transpose(m.banks[1 + half][:, k * P:(k + 1) * P], m.sel[:, j * K + half * 4 + k, :],
                                        m.ident)
                last.then_inc(s.sel_turned, 1)
            pe.wait_ge(s.win_in[j], 16 * K * (it + 1))
            for k in range(K):
                if k % 4 == 0:
                    pe.wait_ge(s.sel_copied, 2 * g + k // 4 + 1)
                if k % 2 == 0:
                    pe.wait_ge(s.q_read, 4 * g + k // 2 + 1)
                last = pe.matmul(m.banks[3 + k // 2][:, (k % 2) * D:(k % 2 + 1) * D], s.turned[:, k // 4, k % 4, :],
                                 s.q_win[:, j * K + k, :], start=True, stop=True)
                if k % 2:
                    last.then_inc(s.q_done, 1)


def scores_vector(m, dve, step):
    s = m.sc
    dve.sem_inc(s.win_free, J)
    dve.sem_inc(s.edges_free, J)
    dve.sem_inc(s.q_read, 4)
    dve.sem_inc(m.rows_free.sem, J)
    dve.wait_ge(s.digits_stored, 16)
    choose(m, dve, 0, 0).then_inc(s.chosen, 1)
    with step.loop(IT, J * 3) as it:
        for j in range(J):
            g = it * J + j
            choose(m, dve, g + 1, (j + 1) % J).then_inc(s.chosen, 1)
            dve.wait_ge(s.edges_in[j], 16 * it + 16)
            landed(m, dve, "keys", it, j)
            rows = m.rows[:, j * K:(j + 1) * K, :]
            heads = rows.rearrange("p k (h d) -> p k h d", h=H0)
            step(dve.tensor_tensor(heads, heads, s.edges[:, j, :, 4:ROW].unsqueeze(2).to_broadcast([P, K, H0, DH0]),
                                   ALU.add))
            step.mark(dve.tensor_scalar(s.weight, s.edges[:, j, :, 2], float(DH0) ** -0.5, None, ALU.mult))
            for b in range(4):
                dve.wait_ge(s.q_done, 4 * g + b + 1)
                pair = m.rows[:, j * K + 2 * b:j * K + 2 * b + 2, :]
                dve.tensor_tensor(pair, pair, m.banks[3 + b][:, :].rearrange("p (k d) -> p k d", k=2), ALU.mult
                                  ).then_inc(s.q_read, 1)
            dve.wait_ge(s.q_read, 4 * g + 8)
            dve.sem_inc(s.win_free, 1)
            step(dve.tensor_reduce(s.dots, rows.rearrange("p k (h d) -> p (k h) d", d=DH0), AX.X, ALU.add))
            dve.tensor_tensor(m.edge[:, bass.ds(g * K * H0, K * H0)].rearrange("p (k h) -> p k h", h=H0),
                              s.dots.rearrange("p (k h) -> p k h", h=H0),
                              s.weight.unsqueeze(2).to_broadcast([P, K, H0]), ALU.mult).then_inc(m.rows_free.sem, 1)
            dve.sem_inc(s.edges_free, 1)
    dve.wait_ge(m.rows_free.sem, J + G)
    dve.wait_ge(s.chosen, G + 1)
    dve.sem_inc(m.st.scores_there.sem, 1)
    m.st.scores_there.sent += 1


def choose(m, dve, g, j):
    return dve.tensor_tensor(m.sel[:, j * K:(j + 1) * K, :], m.iota.unsqueeze(1).to_broadcast([P, K, P]),
                             m.loc[:, bass.ds(g * K, K)].unsqueeze(2).to_broadcast([P, K, P]), ALU.is_equal)



def place_strips(m):
    s = m.st = Memory()
    z = m.sums

    def heads(n, count):
        return z[0:NS, n * SL:(n + count) * SL].rearrange("p (h c) -> p h c", c=SL)

    s.arrays = {H0: [heads(n * H0, H0) for n in range(3)], H1: [heads(n * H1, H1) for n in range(4)]}
    s.given = m.w2[0:NS, 4:6, :].rearrange("p a c -> p (a c)")
    s.absent = m.w2[0:NS, 6:8, :].rearrange("p a c -> p (a c)")
    s.dst = m.sel[0:NS, 8:12, :].rearrange("p a c -> p (a c)")
    sm = m.small
    s.ends = sm[0:NS, 0:8]
    s.start = sm[0:NS, 8:16]
    s.whole = sm[0:NS, 16:18]
    s.first_f = sm[0:NS, 18:20]
    s.first_i = sm[0:NS, 20:21].bitcast(I32)
    s.fill0 = sm[0:NS, 24:28]
    s.around = sm[0:NS, 28:30]
    s.wide = sm[0:NS, 144:160].rearrange("p (w h) -> p w h", h=H0)
    s.row = m.sb("strip_row", [H0, 5, 112])
    s.ended, s.scanned = s.row[:, 0, :], s.row[:, 1, :]
    s.through = s.row[:, 2:5, :]
    s.dst_turned = Turns(m.sem("strip_dst_turned"))
    s.around_in = Turns(m.sem("strip_around_in"))
    s.around_out = Turns(m.sem("strip_around_out"))
    s.whole_out = Turns(m.sem("strip_whole_out"))
    s.whole_in = Turns(m.sem("strip_whole_in"))
    s.scores_there = Turns(m.sem("strip_scores_there"))
    s.turned = Turns(m.sem("strip_turned"))
    s.taken = Turns(m.sem("strip_taken"))
    s.ends_out = Turns(m.sem("strip_ends_out"))
    s.ends_in = Turns(m.sem("strip_ends_in"))
    s.scans_out = Turns(m.sem("strip_scans_out"))
    s.scans_in = Turns(m.sem("strip_scans_in"))
    s.shifted = Turns(m.sem("strip_shifted"))
    s.grown = Turns(m.sem("strip_grown"))
    s.attention = Turns(m.sem("strip_attention"))
    s.back = Turns(m.sem("strip_back"))
    s.back_in = Turns(m.sem("strip_back_in"))
    s.fill_in = Turns(m.sem("strip_fill_in"))
    s.first_filled = Turns(m.sem("strip_first_filled"))
    s.scattered = Turns(m.sem("strip_scattered"))


def flags_tensor(m, pe):
    s = m.st
    for bank, field in ((0, 1), (1, 3)):
        for b in range(FB):
            last = pe.transpose(m.banks[bank][0:NS, b * P:(b + 1) * P], m.fields_sorted[:, b::FB, field], m.ident)
        s.dst_turned.send(last)
    s.around_out.receive(pe)
    pe.matmul(m.banks[2][0:NS, 0:1], m.shift_on[0:NS, 0:NS], s.dst[:, SL - 1:SL], start=True, stop=True)
    s.around_in.send(pe.matmul(m.banks[2][0:NS, 1:2], m.shift_back[0:NS, 0:NS], s.dst[:, 0:1], start=True, stop=True))
    s.whole_out.receive(pe)
    pe.transpose(m.banks[3][0:H0, 0:NS], s.wide[:, 0, :], m.ident[0:NS, 0:NS])
    s.whole_in.send(pe.transpose(m.banks[3][0:H0, 128:128 + NS], s.wide[:, 1, :], m.ident[0:NS, 0:NS]))


def flags_vector(m, dve, step):
    s = m.st
    s.dst_turned.receive(dve, 2)
    step(dve.tensor_scalar(s.dst, m.banks[0][0:NS, :], 1.0, None, ALU.add))
    step.mark(dve.tensor_copy(s.given, m.banks[1][0:NS, :]))
    step.mark(dve.tensor_scalar(s.absent, m.banks[1][0:NS, :], -1.0, BIG, ALU.add, ALU.mult))
    step.mark(dve.tensor_scalar(s.first_i, s.dst[:, 0:1], -1.0, None, ALU.add))
    s.around_out.send(dve.tensor_tensor(m.goes_on[:, 1:SL], s.dst[:, 1:SL], s.dst[:, 0:SL - 1], ALU.is_equal))
    s.around_in.receive(dve)
    step.mark(dve.tensor_tensor(m.has_next[:, 0:SL - 1], s.dst[:, 1:SL], s.dst[:, 0:SL - 1], ALU.is_equal))
    step.mark(dve.tensor_tensor(m.goes_on[:, 0:1], s.dst[:, 0:1], m.banks[2][0:NS, 0:1], ALU.is_equal))
    step(dve.tensor_tensor(m.has_next[:, SL - 1:SL], s.dst[:, SL - 1:SL], m.banks[2][0:NS, 1:2], ALU.is_equal))
    step.mark(dve.tensor_scalar(m.at_start, m.goes_on, -1.0, BIG, ALU.add, ALU.mult))
    step.mark(dve.tensor_reduce(s.whole[:, 0:1], m.goes_on, AX.X, ALU.min))
    step(dve.tensor_reduce(s.whole[:, 1:2], m.has_next, AX.X, ALU.min))
    s.whole_out.send(dve.tensor_copy(s.wide, s.whole.unsqueeze(2).to_broadcast([NS, 2, H0])))
    s.whole_in.receive(dve)
    step.mark(dve.tensor_scalar(s.through[:, 0, 0:NS], m.banks[3][0:H0, 0:NS], -1.0, BIG, ALU.add, ALU.mult))
    step.mark(dve.tensor_copy(s.through[:, 1, 0:NS], m.banks[3][0:H0, 0:NS]))
    step(dve.tensor_copy(s.through[:, 2, 0:NS], m.banks[3][0:H0, 128:128 + NS]))


def strips_tensor(m, pe, heads):
    s = m.st
    s.scores_there.receive(pe)
    scores = m.edge[:, 0:T * heads].rearrange("p (t h) -> p t h", h=heads)
    for h in range(heads):
        for b in range(FB):
            last = pe.transpose(m.banks[h][0:NS, b * P:(b + 1) * P], scores[:, b::FB, h], m.ident)
        s.turned.send(last)
    for n in range(4):
        s.ends_out.receive(pe)
        s.ends_in.send(pe.transpose(m.banks[0][0:heads, 0:NS], s.ends[:, 0:heads], m.ident[0:NS, 0:NS]))
        s.scans_out.receive(pe)
        moved = s.scanned[0:heads, 0:NS] if n % 2 == 0 else s.scanned[0:heads, 1:NS + 1]
        s.scans_in.send(pe.transpose(m.banks[1][0:NS, 0:heads], moved, m.ident[0:heads, 0:heads]))
    s.attention.receive(pe)
    x = s.arrays[heads][0]
    for h in range(heads):
        for b in range(FB):
            last = pe.transpose(m.banks[h][:, b * NS:(b + 1) * NS], x[:, h, b * P:(b + 1) * P], m.ident[0:NS, 0:NS])
        s.back.send(last)


def strips_scalar(m, act, heads):
    s = m.st
    x = s.arrays[heads][0]
    for h in range(heads):
        s.turned.receive(act)
        s.taken.send(act.activation(x[:, h, :], m.banks[h][0:NS, :], ACT.Copy))
    s.shifted.receive(act)
    s.grown.send(act.activation(x, x, ACT.Exp))
    edges = m.edge[:, 0:T * heads].rearrange("p (s b h) -> p h b s", b=FB, h=heads)
    for h in range(heads):
        s.back.receive(act)
        s.back_in.send(act.activation(edges[:, h], m.banks[h][:, 0:FB * NS].rearrange("p (b s) -> p b s", b=FB),
                                      ACT.Copy))


def strips_vector(m, dve, step, heads, slope=None, least=None, more=None):
    s = m.st
    x, on, back = s.arrays[heads][0:3]
    wide = [NS, heads, SL]

    def each(flag):
        return flag.unsqueeze(1).to_broadcast(wide)

    def run(out, x, flag, ops, start, rev=False):
        way = slice(None, None, -1) if rev else slice(None)
        for h in range(heads):
            first = start if isinstance(start, float) else start[:, h:h + 1]
            step.mark(dve.tensor_tensor_scan(out[:, h, way], flag[:, way], x[:, h, way], first, *ops))
        step.wait()

    def starts(values, through, ops, zero, rev=False):
        s.ends_out.send(dve.tensor_copy(s.ends[:, 0:heads], values))
        s.ends_in.receive(dve)
        step(dve.tensor_copy(s.ended[0:heads, 0:NS], m.banks[0][0:heads, 0:NS]))
        through = through[0:heads, 0:NS]
        if rev:
            step(dve.memset(s.scanned[0:heads, NS:NS + 1], zero))
            s.scans_out.send(dve.tensor_tensor_scan(s.scanned[0:heads, 0:NS][:, ::-1], through[:, ::-1],
                                                    s.ended[0:heads, 0:NS][:, ::-1], zero, *ops))
        else:
            step(dve.memset(s.scanned[0:heads, 0:1], zero))
            s.scans_out.send(dve.tensor_tensor_scan(s.scanned[0:heads, 1:NS + 1], through,
                                                    s.ended[0:heads, 0:NS], zero, *ops))
        s.scans_in.receive(dve)
        step(dve.tensor_copy(s.start[:, 0:heads], m.banks[1][0:NS, 0:heads]))
        return s.start

    def over_runs(x, flag, ops, through, zero):
        run(on, x, flag, ops, zero)
        run(on, x, flag, ops, starts(on[:, :, SL - 1], through, ops, zero))
        step(dve.scalar_tensor_tensor(on, each(m.has_next), 0.0, on, ALU.is_equal, ALU.mult))
        ops = (ALU.mult, ALU.add)
        run(back, on, m.has_next, ops, 0.0, rev=True)
        run(back, on, m.has_next, ops, starts(back[:, :, 0], s.through[:, 2], ops, 0.0, rev=True), rev=True)

    s.taken.receive(dve, heads)
    if heads == H0:
        step(dve.tensor_tensor(x, x, each(s.given), ALU.mult))
        step(dve.tensor_tensor(x, x, each(s.absent), ALU.add))
    else:
        s.fill_in.receive(dve, 16)
        s.first_filled.receive(dve, 16)
        filled = s.arrays[heads][3].rearrange("p h c -> p (h c)").rearrange("p (c h) -> p h c", h=heads)
        run(on, filled, m.goes_on, (ALU.mult, ALU.add), s.fill0)
        step(dve.tensor_tensor(x, x, on, ALU.add))
        step(dve.scalar_tensor_tensor(x, x, slope, x, ALU.mult, ALU.max))
    over_runs(x, m.at_start, (ALU.add, ALU.max), s.through[:, 0], -BIG)
    s.shifted.send(dve.tensor_tensor(x, x, back, ALU.subtract))
    s.grown.receive(dve)
    if heads == H0:
        step(dve.tensor_tensor(x, x, each(s.given), ALU.mult))
    over_runs(x, m.goes_on, (ALU.mult, ALU.add), s.through[:, 1], 0.0)
    if least is not None:
        step(dve.tensor_scalar(back, back, least, None, ALU.max))
    if more is not None:
        step(dve.tensor_scalar(back, back, more, None, ALU.add))
    step(dve.reciprocal(back, back))
    s.attention.send(dve.tensor_tensor(x, x, back, ALU.mult))



AGGREGATES = ["values"] + [f"rows{i}" for i in range(4)]


def plan_aggregates(m):
    m.ag = Memory()
    a = m.ag
    a.weighted = Signal(m.sem("aggregate_weighted"))
    a.banks_free = Signal(m.sem("aggregate_banks_free"))
    a.products = Signal(m.sem("aggregate_products"))
    for stage in AGGREGATES:
        a.weighted.plan(stage, 2 * G)
        a.banks_free.plan(stage, 4 * G)
        a.products.plan(stage, 4 * G)


def aggregate_vector(m, dve, step, stage, heads):
    a = m.ag
    bw, bp, bf = a.weighted.base[stage], a.products.base[stage], a.banks_free.base[stage]
    br = m.rows_free.base[stage]
    m.st.back_in.receive(dve, heads)
    edges = m.edge[:, 0:T * heads].rearrange("p (t h) -> p t h", h=heads)
    if not bf:
        dve.sem_inc(a.banks_free.sem, 4)
    step(dve.memset(m.sums[:, :], 0.0))

    def add(g, j):
        first = windows(m, ENGINE.DVE, g)
        for k in range(K):
            if k % 2 == 0:
                dve.wait_ge(a.products.sem, bp + 4 * g + k // 2 + 1)
            w = m.acc[:, k % 2, :, bass.ds(first[k], P)]
            ins = dve.tensor_tensor(w, w, m.banks[k // 2][:, (k % 2) * D:(k % 2 + 1) * D]
                                    .rearrange("p (f c) -> p f c", f=2), ALU.add)
            if k % 2:
                ins.then_inc(a.banks_free.sem, 1)
                dve.wait_ge(a.banks_free.sem, 4 + bf + 4 * g + k // 2 + 1)

    with dve.Fori(0, IT) as it:
        for j in range(J):
            g = it * J + j
            dve.wait_ge(m.rows_free.sem, br - J + g + 1)
            choose(m, dve, g, j).then_inc(a.weighted.sem, 1)
            landed(m, dve, stage, it, j)
            rows = m.rows[:, j * K:(j + 1) * K, :].rearrange("p k (h d) -> p k h d", h=heads)
            dve.tensor_tensor(rows, rows, edges[:, bass.ds(g * K, K), :].unsqueeze(3)
                              .to_broadcast([P, K, heads, D // heads]), ALU.mult).then_inc(a.weighted.sem, 1)
            add(g, j)


def aggregate_tensor(m, pe, stage):
    a = m.ag
    bw, bp, bf = a.weighted.base[stage], a.products.base[stage], a.banks_free.base[stage]
    with pe.Fori(0, IT) as it:
        for j in range(J):
            g = it * J + j
            pe.wait_ge(a.weighted.sem, bw + 2 * g + 2)
            for k in range(K):
                if k % 2 == 0:
                    pe.wait_ge(a.banks_free.sem, bf + 4 * g + k // 2 + 1)
                for f in range(2):
                    at = (k % 2) * D + f * P
                    last = pe.matmul(m.banks[k // 2][:, at:at + P], m.rows[:, j * K + k, f * P:(f + 1) * P],
                                     m.sel[:, j * K + k, :], start=True, stop=True)
                if k % 2:
                    last.then_inc(a.products.sem, 1)
            pe.wait_ge(a.products.sem, bp + 4 * g + 4)
            pe.sem_inc(m.rows_free.sem, 1)



class Marks:

    def __init__(self, sem, plan):
        self.sem, self.plan, self.at, self.n = sem, plan, {}, 0
        total = 0
        for label, count in plan:
            total += count
            self.at[label] = total

    def reach(self, label, ins):
        assert self.plan[self.n][0] == label, (self.plan[self.n], label)
        self.n += 1
        return ins.then_inc(self.sem, 1)

    def wait(self, eng, label):
        eng.wait_ge(self.sem, self.at[label])


def norm_labels(stage):
    return [(stage + " variance", 1), (stage + " norm", 1)]


LAYERS = range(3)
VECTOR_MARKS = ([("zeros", 1)] + norm_labels("A") + norm_labels("A2") + [("B sum", 1), ("B rows", NL)]
                + norm_labels("C") + [("C rows", NL)]
                + norm_labels("D") + [("D ratio", 1), ("D factor", 1), ("D product", NL), ("D2 square", 1),
                                      ("D sum", 1), ("D3 ratio", 1), ("D rows", 1), ("D terms", 1)]
                + [("F sum", 1), ("F product", NL), ("F relu", 1), ("F rows", NL)]
                + [("G turns", 1)] + norm_labels("G") + [("G weights", 1), ("G rows", NL)] + norm_labels("H")
                + [(f"H{i} {what}", n) for i in LAYERS
                   for what, n in (("weights", 1),) + ((("sum", 1),) if i else ()) + (("rows", NL),)]
                + [("J sum", 1), ("J rows", NL)])
SCALAR_MARKS = ([("A deviation", 1), ("A rows", NL), ("A2 deviation", 1), ("C deviation", 1)]
                + [("D deviation", 1), ("D rows", NL), ("D squares", NL), ("D root", 1), ("D log", 1),
                   ("D2 squares", NL), ("D2 root", 1), ("D2 tanh", 1), ("D3 squares", NL), ("D3 root", 1),
                   ("D3 log", 1)]
                + [("F squares", NL), ("F root", 1), ("F tanh", 1)]
                + [("G deviation", 1), ("H deviation", 1), ("H1 sum", 1), ("H2 sum", 1), ("J sum", 1)])
SYNC_MARKS = ([("inputs", 16 * 5), ("zeros", 32), ("B weights", 48), ("C weights", 32), ("D weights", 64),
               ("D flat", 16), ("D rows", 64), ("D tables", 32),
               ("F flat", 64), ("F rows", 16)]
              + [(f"H{i} {what}", n) for i in LAYERS for what, n in (("weights", 32), ("tables", 32))]
              + [("output", 16)])
TURNING = ["A", "C", "D", "G", "H0"]
PASSES = ["A", "B", "C", "D", "F", "G", "H0", "H1", "H2", "J"]


def place_nodes(m):
    n = m.n = Memory()
    r = m.rows[:, :, :].rearrange("p t d -> p (t d)")
    n.z = r[0:NP, 0:J * D].rearrange("p (j d) -> p j d", j=J)
    n.lhs = r[:, 1280:1280 + J * 2 * NP].rearrange("p (j f n) -> p j f n", j=J, f=2)
    n.lhs_c = r[:, 1280:1280 + 2 * J * NP].rearrange("p (f c) -> p f c", f=2)
    n.out = r[0:NP, 2560:2560 + J * 3 * D].rearrange("p (j d) -> p j d", j=J)
    n.spare = r[:, 6400:10240]
    n.hidden = m.sel[:, :, :].rearrange("p a b -> p (a b)")[:, 0:FF // P * J * NP].rearrange(
        "p (c n) -> p c n", c=FF // P)
    n.squares = m.sums[0:NP, 0:NL * D].rearrange("p (l d) -> p l d", l=NL)
    e = m.edge
    n.stats = e[0:NP, 0:6 * NL].rearrange("p (l s) -> p l s", s=6)
    n.wide = [e[0:NP, 150 + (NL + 1) * i:150 + (NL + 1) * (i + 1)] for i in range(16)]
    n.v = [v[:, 0:NL] for v in n.wide]
    n.mean, n.rs, n.nb, n.sq = n.v[0:4]
    n.cols = m.sb("cols", [P, 30])
    n.g1, n.b1, n.g2, n.b2 = (n.cols[:, 2 * i:2 * i + 2] for i in range(4))
    n.hidden_bias = n.cols[:, 8:16]
    n.b3 = [n.cols[:, 18 + 2 * i:20 + 2 * i] for i in LAYERS]
    n.alpha, n.beta = n.cols[0:NP, 24:25], n.cols[0:NP, 25:26]
    n.qkv = m.w1[:, :, 0:3 * D]
    n.qkv_bias = m.w2[0:NP, 0:3, :].rearrange("p a d -> p (a d)")
    n.wo = n.spare[:, 0:2 * D].rearrange("p (f d) -> p f d", f=2)
    n.bo = n.spare[0:NP, 2 * D:3 * D]
    n.b_ff = n.spare[0:NP, 3 * D:4 * D]
    w = m.w2[:, :, :].rearrange("p a d -> p (a d)")
    n.w = w[:, 0:2 * (D + 2 * H1)].rearrange("p (f d) -> p f d", f=2)
    n.att = w[:, 528:528 + 2 * D].rearrange("p (a d) -> p a d", a=2)
    n.b_lin = w[0:NP, 1040:1040 + D]
    n.b_conv = w[0:NP, 1296:1296 + D]
    n.scratch = w[:, 1296:1296 + 2 * D].rearrange("p (f d) -> p f d", f=2)
    m.terms = m.w1[0:NP, 0, 0:NL * 2 * H1].rearrange("p (a l h) -> p a l h", a=2, l=NL)
    n.vector = Marks(m.sem("vector_reached"), VECTOR_MARKS)
    n.scalar = Marks(m.sem("scalar_reached"), SCALAR_MARKS)
    n.sync = Marks(m.sem("loaded"), SYNC_MARKS)
    n.z_in = Signal(m.sem("node_z_in"))
    n.turned = Signal(m.sem("node_turned"))
    n.lhs_in = Signal(m.sem("node_lhs_in"))
    n.out_ready = Signal(m.sem("node_out_ready"))
    n.out_read = Signal(m.sem("node_out_read"))
    n.turned.total = n.out_ready.total = n.out_read.total = J
    for p in TURNING:
        if p != "C":
            n.z_in.plan(p, NL)
            n.turned.plan(p, NL)
    for p in PASSES:
        if p != "C":
            for signal in (n.lhs_in, n.out_ready, n.out_read):
                signal.plan(p, NL)
    n.stored = [m.sem(f"tables_stored{j}") for j in range(J)]
    n.ff_z_in = m.sem("ff_z_in")
    n.ff_turned = m.sem("ff_turned")
    n.ff_lhs_in = m.sem("ff_lhs_in")
    n.ff_hidden_out = m.sem("ff_hidden_out")
    n.ff_hidden_read = m.sem("ff_hidden_read")
    n.ff_out_ready = m.sem("ff_out_ready")
    n.ff_out_read = m.sem("ff_out_read")


def done(eng, signal, p, l):
    eng.wait_ge(signal.sem, signal.base[p] + l + 1)


def free(eng, signal, p, l):
    eng.wait_ge(signal.sem, signal.base[p] - J + l + 1)


def pass_scalar(m, act, p, z, lhs):
    n = m.n
    with act.Fori(0, NL // J) as it:
        def first(k):
            l = it * J + k
            free(act, n.turned, p, l)
            z(l, k).then_inc(n.z_in.sem, 1)

        def second(k):
            l = it * J + k
            done(act, n.turned, p, l)
            free(act, n.out_ready, p, l)
            lhs(l, k).then_inc(n.lhs_in.sem, 1)

        for k in range(J):
            first(k)
            if k:
                second(k - 1)
        second(J - 1)


def turn_back(m, act, k, scale=None, bias=None):
    n = m.n
    for f in range(2):
        bank = m.banks[k][:, f * P:f * P + NP]
        if scale is None:
            last = act.activation(n.lhs[:, k, f, :], bank, ACT.Copy)
        else:
            last = act.activation(n.lhs[:, k, f, :], bank, ACT.Identity, bias=bias[:, f:f + 1],
                                  scale=scale[:, f:f + 1])
    return last


def sums_scalar(m, act, p):
    n = m.n
    columns = m.acc[:, 0, :, 0:N].rearrange("p f (n l) -> p l f n", l=NL)
    with act.Fori(0, NL // J) as it:
        for k in range(J):
            l = it * J + k
            free(act, n.out_ready, p, l)
            act.activation(n.lhs[:, k, :, :], columns[:, bass.ds(l, 1)].rearrange("p o f n -> p (o f) n"),
                           ACT.Copy).then_inc(n.lhs_in.sem, 1)


def pass_tensor(m, pe, p, product):
    n = m.n
    turning = p in TURNING
    with pe.Fori(0, NL // J) as it:
        def turn(k):
            l = it * J + k
            done(pe, n.z_in, p, l)
            free(pe, n.out_read, p, l)
            for f in range(2):
                last = pe.transpose(m.banks[k][:, f * P:f * P + NP], n.z[:, k, f * P:(f + 1) * P], m.ident[0:NP, 0:NP])
            last.then_inc(n.turned.sem, 1)

        def multiply(k):
            l = it * J + k
            done(pe, n.lhs_in, p, l)
            free(pe, n.out_read, p, l + J - 2)
            product(k).then_inc(n.out_ready.sem, 1)

        for k in range(J):
            if turning:
                turn(k)
                if k:
                    multiply(k - 1)
            else:
                multiply(k)
        if turning:
            multiply(J - 1)


def product_of(m, pe, weights, width):
    def product(k):
        for first in range(0, width, 512):
            bank = m.banks[k] if not first else m.banks[J + k % 3]
            end = min(first + 512, width)
            for f in range(2):
                last = pe.matmul(bank[0:NP, 0:end - first], m.n.lhs[:, k, f, :], weights[:, f, first:end],
                                 start=f == 0, stop=f == 1)
        return last
    return product


def rows_of(m, pe):
    def product(k):
        for f in range(2):
            last = pe.transpose(m.banks[k][0:NP, f * P:(f + 1) * P], m.n.lhs[:, k, f, :], m.ident)
        return last
    return product


def norm_vector(m, dve, step, stage, rows):
    n = m.n
    with step.loop(NL // J, J) as it:
        for k in range(J):
            l = it * J + k
            step.mark(dve.bn_stats(n.stats[:, bass.ds(l, 1), :].rearrange("p l s -> p (l s)"),
                                   rows[0:NP, bass.ds(l, 1), :].rearrange("p l d -> p (l d)")))
    step.wait()
    st = n.stats
    step.mark(dve.tensor_tensor(n.v[4], st[:, :, 1], st[:, :, 4], ALU.add))
    step.mark(dve.tensor_tensor(n.v[5], st[:, :, 1], st[:, :, 4], ALU.subtract))
    step(dve.tensor_tensor(n.v[6], st[:, :, 2], st[:, :, 5], ALU.add))
    step.mark(dve.tensor_scalar(n.mean, n.v[4], 0.5, None, ALU.mult))
    step.mark(dve.tensor_tensor(n.v[7], n.v[5], n.v[5], ALU.mult))
    step(dve.tensor_scalar(n.v[8], n.v[6], 1.0 / D, LN_EPS, ALU.mult, ALU.add))
    n.vector.reach(stage + " variance", dve.scalar_tensor_tensor(n.v[9], n.v[7], 0.25, n.v[8], ALU.mult, ALU.add))
    n.scalar.wait(dve, stage + " deviation")
    step(dve.reciprocal(n.rs, n.v[10]))
    n.vector.reach(stage + " norm", dve.scalar_tensor_tensor(n.nb, n.mean, -1.0, n.rs, ALU.mult, ALU.mult))


def norm_scalar(m, act, stage):
    n = m.n
    n.vector.wait(act, stage + " variance")
    n.scalar.reach(stage + " deviation", act.activation(n.v[10], n.v[9], ACT.Sqrt))
    n.vector.wait(act, stage + " norm")


def row(rows, l):
    return rows[0:NP, bass.ds(l, 1), :].rearrange("p l d -> p (l d)")


def normed(m, act, rows, func, k_slot=True):
    n = m.n
    return lambda l, k: act.activation(n.z[:, k, :], row(rows, l), func, bias=n.nb[:, bass.ds(l, 1)],
                                       scale=n.rs[:, bass.ds(l, 1)])


def each_node(eng, signal, body):
    with eng.Fori(0, NL // J) as it:
        for k in range(J):
            body(it * J + k, k).then_inc(signal.sem, 1)
    signal.n += 1



def a_sync(m, io, sp):
    n = m.n
    sp.dma_start(m.x[0:NP, :, :], io["x"].rearrange("(p l) d -> p l d", l=NL)).then_inc(n.sync.sem, 16)
    sp.dma_start(n.cols[:, :], io["cols"]).then_inc(n.sync.sem, 16)
    sp.dma_start(n.qkv, io["qkv"]).then_inc(n.sync.sem, 16)
    sp.dma_start(n.qkv_bias, io["qkv_bias"][0:1, :].to_broadcast([NP, 3 * D])).then_inc(n.sync.sem, 16)
    sp.dma_start(m.consts[:, :, :], io["consts"]).then_inc(n.sync.sem, 16)
    n.vector.wait(sp, "zeros")
    n.sync.wait(sp, "inputs")
    zeros = m.sums[:, 0:SL * H1]
    sp.dma_start(m.q_table[N:N + P, :], zeros[:, 0:D]).then_inc(n.sync.sem, 16)
    sp.dma_start(m.at_starts.rearrange("(s c) h -> s (c h)", s=NS), zeros[0:NS, :]).then_inc(n.sync.sem, 16)
    with sp.Fori(0, NL // J) as it:
        for k in range(J):
            l = it * J + k
            done(sp, n.out_read, "A", l)
            for i, table in enumerate((m.q_table, m.k_table, m.row_table)):
                sp.dma_start(node_rows(table, D)[:, bass.ds(l, 1), :].rearrange("p l d -> p (l d)"),
                             n.out[:, k, i * D:(i + 1) * D]).then_inc(n.stored[k], 16)
    for k in range(J):
        sp.wait_ge(n.stored[k], 48 * NL // J)
    n.sync.wait(sp, "zeros")
    n.sync.n = 2


def a_vector(m, dve, step):
    n = m.n
    dve.sem_inc(n.out_read.sem, J)
    n.vector.reach("zeros", dve.memset(m.sums[:, 0:SL * H1], 0.0))
    n.sync.wait(dve, "inputs")
    norm_vector(m, dve, step, "A", m.x)
    n.scalar.wait(dve, "A rows")
    norm_vector(m, dve, step, "A2", m.h)
    with dve.Fori(0, NL // J) as it:
        for k in range(J):
            l = it * J + k
            done(dve, n.out_ready, "A", l)
            dve.wait_ge(n.stored[k], 48 * it)
            dve.tensor_tensor(n.out[:, k, 0:2 * D], m.banks[k][0:NP, :], n.qkv_bias[:, 0:2 * D], ALU.add)
            dve.tensor_tensor(n.out[:, k, 2 * D:3 * D], m.banks[J + k % 3][0:NP, 0:D], n.qkv_bias[:, 2 * D:3 * D],
                              ALU.add).then_inc(n.out_read.sem, 1)


def a_scalar(m, act):
    n = m.n
    norm_scalar(m, act, "A")
    each_node(act, n.scalar, lambda l, k: act.activation(row(m.h, l), row(m.x, l), ACT.Relu,
                                                         bias=n.nb[:, bass.ds(l, 1)], scale=n.rs[:, bass.ds(l, 1)]))
    norm_scalar(m, act, "A2")
    pass_scalar(m, act, "A", normed(m, act, m.h, ACT.Identity), lambda l, k: turn_back(m, act, k, n.g1, n.b1))


def a_tensor(m, pe):
    n = m.n
    pe.sem_inc(n.turned.sem, J)
    pe.sem_inc(n.out_ready.sem, J)
    n.sync.wait(pe, "inputs")
    pass_tensor(m, pe, "A", product_of(m, pe, n.qkv, 3 * D))



def load(m, sp, parts):
    m.n.sync.wait(sp, m.n.sync.plan[m.n.sync.n - 1][0])
    for out, in_ in parts:
        sp.dma_start(out, in_).then_inc(m.n.sync.sem, 16)
    m.n.sync.n += 1


def spread(source, rows, width):
    return source[0:1, :].to_broadcast([rows, width])


def b_sync(m, io, sp):
    n = m.n
    n.vector.wait(sp, "B sum")
    load(m, sp, [(n.wo, io["wo"]), (n.bo, spread(io["bo"], NP, D)), (n.b_ff, spread(io["b_ff"], NP, D))])
    load(m, sp, [(m.w1[:, :, :], io["w1"]), (m.w2[:, :, :], io["w2"])])


def add_parities(m, dve, label):
    a = m.acc
    m.n.vector.reach(label, dve.tensor_tensor(a[:, 0, :, 0:N], a[:, 0, :, 0:N], a[:, 1, :, 0:N], ALU.add))


def b_vector(m, dve, step):
    n = m.n
    add_parities(m, dve, "B sum")
    n.sync.wait(dve, "B weights")
    with step.loop(NL // J, J) as it:
        for k in range(J):
            l = it * J + k
            done(dve, n.out_ready, "B", l)
            step(dve.tensor_tensor(n.out[:, k, 0:D], m.banks[k][0:NP, 0:D], n.bo, ALU.add))
            dve.sem_inc(n.out_read.sem, 1)
            dve.scalar_tensor_tensor(row(m.h, l), n.out[:, k, 0:D], n.alpha, row(m.h, l), ALU.mult, ALU.add
                                     ).then_inc(n.vector.sem, 1)
    n.vector.n += 1
    n.vector.wait(dve, "B rows")


def b_scalar(m, act):
    m.n.vector.wait(act, "B sum")
    sums_scalar(m, act, "B")


def b_tensor(m, pe):
    m.n.sync.wait(pe, "B weights")
    pass_tensor(m, pe, "B", product_of(m, pe, m.n.wo, D))



def c_vector(m, dve, step):
    n = m.n
    norm_vector(m, dve, step, "C", m.h)
    with step.loop(NL // J, 2 * J) as it:
        for k in range(J):
            l = it * J + k
            dve.wait_ge(n.ff_out_ready, l + 1)
            step(dve.tensor_tensor(n.out[:, k, 0:D], m.banks[k][0:NP, 0:D], n.b_ff, ALU.add))
            dve.sem_inc(n.ff_out_read, 1)
            step(dve.scalar_tensor_tensor(n.out[:, k, D:2 * D], n.out[:, k, 0:D], n.beta, row(m.h, l),
                                          ALU.mult, ALU.add))
            dve.tensor_tensor(row(m.x, l), n.out[:, k, D:2 * D], row(m.x, l), ALU.add).then_inc(n.vector.sem, 1)
    n.vector.n += 1
    n.vector.wait(dve, "C rows")


HIDDEN = FF // P
CUTS = [(0, 313), (313, J * NP)]


def c_scalar(m, act):
    n = m.n
    norm_scalar(m, act, "C")
    z = normed(m, act, m.h, ACT.Identity)
    with act.Fori(0, NL // J) as it:
        for k in range(J):
            l = it * J + k
            act.wait_ge(n.ff_turned, 5 * it)
            z(l, k).then_inc(n.ff_z_in, 1)
        for k in range(J):
            act.wait_ge(n.ff_turned, J * it + k + 1)
            act.wait_ge(n.ff_hidden_out, 2 * HIDDEN * it)
            for f in range(2):
                last = act.activation(n.lhs_c[:, f, k * NP:(k + 1) * NP], m.banks[k][:, f * P:f * P + NP],
                                      ACT.Identity, bias=n.b2[:, f:f + 1], scale=n.g2[:, f:f + 1])
            last.then_inc(n.ff_lhs_in, 1)
        for i in range(2 * HIDDEN):
            c, (a, b) = i // 2, CUTS[i % 2]
            act.wait_ge(n.ff_hidden_out, 2 * HIDDEN * it + i + 1)
            act.wait_ge(n.ff_out_ready, J * it)
            act.activation(n.hidden[:, c, a:b], m.banks[5 + i % 3][:, 0:b - a], ACT.Gelu,
                           bias=n.hidden_bias[:, c:c + 1]).then_inc(n.ff_hidden_read, 1)


def c_tensor(m, pe):
    n = m.n
    n.sync.wait(pe, "C weights")
    with pe.Fori(0, NL // J) as it:
        for k in range(J):
            pe.wait_ge(n.ff_z_in, J * it + k + 1)
            pe.wait_ge(n.ff_out_read, J * it)
            for f in range(2):
                last = pe.transpose(m.banks[k][:, f * P:f * P + NP], n.z[:, k, f * P:(f + 1) * P],
                                    m.ident[0:NP, 0:NP])
            last.then_inc(n.ff_turned, 1)
        for i in range(2 * HIDDEN):
            c, (a, b) = i // 2, CUTS[i % 2]
            if i == 0:
                pe.wait_ge(n.ff_lhs_in, J * it + J)
                pe.wait_ge(n.ff_hidden_read, 2 * HIDDEN * it)
            elif i >= 3:
                pe.wait_ge(n.ff_hidden_read, 2 * HIDDEN * it + i - 2)
            for f in range(2):
                last = pe.matmul(m.banks[5 + i % 3][:, 0:b - a], m.w1[:, f, c * P:(c + 1) * P], n.lhs_c[:, f, a:b],
                                 start=f == 0, stop=f == 1)
            last.then_inc(n.ff_hidden_out, 1)
        pe.wait_ge(n.ff_hidden_read, 2 * HIDDEN * it + 2 * HIDDEN)
        for k in range(J):
            for c in range(HIDDEN):
                last = pe.matmul(m.banks[k][0:NP, 0:D], n.hidden[:, c, k * NP:(k + 1) * NP], m.w2[:, c, :],
                                 start=c == 0, stop=c == HIDDEN - 1)
            last.then_inc(n.ff_out_ready, 1)



MIN_NORM = 1e-15
EDGE_OF_BALL = 1.0 - 0.004
SMALL = 0.1


def squares_scalar(m, act, stage, width=NL):
    n = m.n
    each_node(act, n.scalar, lambda l, k: act.activation(row(n.squares, l), row(m.h, l), ACT.Square,
                                                         accum_out=n.sq[:, bass.ds(l, 1)]))
    n.scalar.wait(act, stage + " squares")
    if width > NL:
        n.vector.wait(act, stage + " square")
    n.scalar.reach(stage + " root", act.activation(n.wide[4][:, 0:width], n.wide[3][:, 0:width], ACT.Sqrt))


def atanh_ratio_vector(m, dve, step, stage, cap, label):
    n, v = m.n, m.n.v
    n.scalar.wait(dve, stage + " root")
    step(dve.tensor_scalar(v[6], v[4], MIN_NORM, None, ALU.max))
    step(dve.tensor_scalar(v[7], v[6], cap, None, ALU.min))
    step.mark(dve.tensor_scalar(v[8], v[7], 1.0, None, ALU.add))
    step(dve.tensor_scalar(v[9], v[7], -1.0, 1.0, ALU.mult, ALU.add))
    step(dve.reciprocal(v[9], v[9]))
    n.vector.reach(stage + " ratio", dve.tensor_tensor(v[10], v[8], v[9], ALU.mult))
    step(dve.tensor_tensor(v[11], v[7], v[7], ALU.mult))
    step(dve.tensor_scalar(v[12], v[11], 1.0 / 7, 1.0 / 5, ALU.mult, ALU.add))
    step(dve.tensor_tensor(v[12], v[12], v[11], ALU.mult))
    step(dve.tensor_scalar(v[12], v[12], 1.0 / 3, None, ALU.add))
    step(dve.tensor_tensor(v[12], v[12], v[11], ALU.mult))
    step(dve.tensor_scalar(v[12], v[12], 1.0, None, ALU.add))
    step(dve.tensor_tensor(v[12], v[12], v[7], ALU.mult))
    n.scalar.wait(dve, stage + " log")
    step(dve.scalar_tensor_tensor(v[13], v[5], 0.5, v[12], ALU.mult, ALU.subtract))
    step(dve.tensor_scalar(v[8], v[7], SMALL, None, ALU.is_ge))
    step(dve.tensor_tensor(v[13], v[13], v[8], ALU.mult))
    step(dve.tensor_tensor(v[13], v[13], v[12], ALU.add))
    step(dve.reciprocal(v[6], v[6]))
    last = dve.tensor_tensor(v[14], v[13], v[6], ALU.mult)
    if label:
        n.vector.reach(label, last)
    else:
        step(last)


def atanh_scalar(m, act, stage, width=NL):
    n = m.n
    squares_scalar(m, act, stage)
    n.vector.wait(act, stage + " ratio")
    n.scalar.reach(stage + " log", act.activation(n.v[5], n.v[10], ACT.Ln))


def tanh_scalar(m, act, stage, width=NL):
    n = m.n
    squares_scalar(m, act, stage, width)
    n.scalar.wait(act, stage + " root")
    n.scalar.reach(stage + " tanh", act.activation(n.wide[5][:, 0:width], n.wide[4][:, 0:width], ACT.Tanh))


def tanh_ratio_vector(m, dve, step, stage, width=NL):
    n, v = m.n, [w[:, 0:width] for w in m.n.wide]
    n.scalar.wait(dve, stage + " tanh")
    step.mark(dve.tensor_scalar(v[6], v[4], MIN_NORM, None, ALU.max))
    step(dve.tensor_scalar(v[7], v[5], MIN_NORM, EDGE_OF_BALL, ALU.max, ALU.min))
    step(dve.reciprocal(v[8], v[6]))
    step(dve.tensor_tensor(v[14], v[7], v[8], ALU.mult))


def by_heads(m):
    heads = m.flat.rearrange("(h p l d) -> h p l d", h=H1, p=NP, l=NL)
    return [(m.h[0:NP, :, i * D // H1:(i + 1) * D // H1], heads[i]) for i in range(H1)]


def d_sync(m, io, sp):
    n = m.n
    n.vector.wait(sp, "C rows")
    load(m, sp, [(n.w[:, :, 0:D], io["w_hyp"]), (n.b_lin, spread(io["b_lin"], NP, D)), (n.b_conv, spread(io["b_conv"], NP, D)),
                 (n.att, spread(io["att_hyp"], P, 2 * D).rearrange("p (a d) -> p a d", a=2))])
    n.vector.wait(sp, "D rows")
    rows = m.h[0:NP, :, :].rearrange("p l d -> p (l d)")
    load(m, sp, [(m.flat.rearrange("(p c) -> p c", p=NP), rows)])
    load(m, sp, by_heads(m))
    tables_sync(m, sp, "D terms")


def tables_sync(m, sp, label):
    m.n.vector.wait(sp, label)
    flat = "p l d -> p (l d)"
    load(m, sp, [(node_rows(m.row_table, D).rearrange(flat), m.h[0:NP, :, :].rearrange(flat)),
                 (node_rows(m.dst_table, H1).rearrange(flat), m.terms[:, 1].rearrange(flat))])


def d_vector(m, dve, step):
    n = m.n
    norm_vector(m, dve, step, "D", m.x)
    atanh_ratio_vector(m, dve, step, "D", 1.0 - 1e-7, "D factor")
    n.sync.wait(dve, "D weights")

    read_products(m, dve, "D", lambda l, k: dve.tensor_copy(row(m.h, l), m.banks[k][0:NP, 0:D]))
    n.vector.wait(dve, "D product")
    b2, hb = n.out[:, 0, 0:D], n.out[:, 0, D:2 * D]
    step(dve.tensor_tensor(b2, n.b_lin, n.b_lin, ALU.mult))
    n.vector.reach("D2 square", dve.tensor_reduce(n.wide[3][:, NL:NL + 1], b2, AX.X, ALU.add))
    tanh_ratio_vector(m, dve, step, "D2", NL + 1)
    v, one = n.v, lambda i: n.wide[i][:, NL:NL + 1]
    step(dve.tensor_scalar(hb, n.b_lin, one(14), None, ALU.mult))
    big = [NP, NL, D]
    t = m.sums[0:NP, NL * D:2 * NL * D].rearrange("p (l d) -> p l d", l=NL)
    h = m.h[0:NP, :, :]

    def along(value):
        return value.unsqueeze(2).to_broadcast(big)

    step(dve.tensor_tensor(t, h, hb.unsqueeze(1).to_broadcast(big), ALU.mult))
    step(dve.tensor_reduce(v[9], t, AX.X, ALU.add))
    step(dve.tensor_tensor(v[9], v[9], v[14], ALU.mult))
    step.mark(dve.tensor_tensor(v[10], v[7], v[7], ALU.mult))
    step.mark(dve.tensor_tensor(one(10), one(7), one(7), ALU.mult))
    step(dve.tensor_scalar(v[11], v[9], 2.0, 1.0, ALU.mult, ALU.add))
    step(dve.tensor_scalar(v[12], v[10], one(10), None, ALU.mult))
    step(dve.tensor_tensor(v[12], v[12], v[11], ALU.add))
    step(dve.tensor_scalar(v[12], v[12], MIN_NORM, None, ALU.max))
    step(dve.reciprocal(v[12], v[12]))
    step(dve.tensor_scalar(v[11], v[11], one(10), None, ALU.add))
    step(dve.tensor_tensor(v[11], v[11], v[14], ALU.mult))
    step(dve.tensor_tensor(v[11], v[11], v[12], ALU.mult))
    step(dve.tensor_scalar(v[10], v[10], -1.0, 1.0, ALU.mult, ALU.add))
    step(dve.tensor_tensor(v[10], v[10], v[12], ALU.mult))
    step(dve.tensor_tensor(t, h, along(v[11]), ALU.mult))
    step(dve.tensor_tensor(h, hb.unsqueeze(1).to_broadcast(big), along(v[10]), ALU.mult))
    n.vector.reach("D sum", dve.tensor_tensor(h, t, h, ALU.add))
    atanh_ratio_vector(m, dve, step, "D3", EDGE_OF_BALL, None)
    n.vector.reach("D rows", dve.tensor_tensor(h, h, along(v[14]), ALU.mult))
    n.sync.wait(dve, "D rows")
    for a in range(2):
        step(dve.tensor_tensor(t, h, n.att[0:NP, a, :].unsqueeze(1).to_broadcast(big), ALU.mult))
        last = dve.tensor_reduce(m.terms[:, a].rearrange("p l h -> p (l h)"),
                                 t.rearrange("p l (h d) -> p (l h) d", h=H1), AX.X, ALU.add)
        if a == 0:
            step(last)
    n.vector.reach("D terms", last)


def read_products(m, dve, p, read):
    n = m.n
    with dve.Fori(0, NL // J) as it:
        for k in range(J):
            l = it * J + k
            done(dve, n.out_ready, p, l)
            read(l, k).then_inc(n.out_read.sem, 1)
    done(dve, n.out_read, p, NL - 1)
    dve.sem_inc(n.vector.sem, NL)
    n.vector.n += 1


def d_scalar(m, act):
    n = m.n
    norm_scalar(m, act, "D")
    each_node(act, n.scalar, lambda l, k: act.activation(row(m.h, l), row(m.x, l), ACT.Relu,
                                                         bias=n.nb[:, bass.ds(l, 1)], scale=n.rs[:, bass.ds(l, 1)]))
    n.scalar.wait(act, "D rows")
    atanh_scalar(m, act, "D")
    n.vector.wait(act, "D factor")
    pass_scalar(m, act, "D", lambda l, k: act.activation(n.z[:, k, :], row(m.h, l), ACT.Copy,
                                                         scale=n.v[14][:, bass.ds(l, 1)]),
                lambda l, k: turn_back(m, act, k))
    n.vector.wait(act, "D product")
    tanh_scalar(m, act, "D2", NL + 1)
    n.vector.wait(act, "D sum")
    atanh_scalar(m, act, "D3")


def d_tensor(m, pe):
    m.n.sync.wait(pe, "D weights")
    pass_tensor(m, pe, "D", product_of(m, pe, m.n.w, D))


def keys_pool(m, pool):
    for j in range(J):
        pool.wait_ge(m.n.stored[j], 48 * NL // J)
    pool.memset(m.src_i[:, T:TP], 0).then_inc(m.pool_step, 1)
    pool.wait_ge(m.pool_step, 2)
    pool.wait_ge(m.sc.numbers_in, 2)
    gather(m, pool, "keys", m.k_table, D)



def terms_pool(m, pool, i, tables):
    n, s = m.n, m.st
    n.sync.wait(pool, tables)
    for l in range(NL):
        pool.indirect_dma_start(out=m.at_starts[:, :],
                                out_offset=bass.IndirectOffsetOnAxis(ap=m.start_i[0:NP, l:l + 1], axis=0),
                                in_=m.terms[:, 1, l, :], in_offset=None).then_inc(s.scattered.sem, 16)
    s.scattered.sent += 16 * NL
    s.first_filled.send(pool.indirect_dma_start(out=s.fill0, out_offset=None, in_=m.dst_table[:, :],
                                                in_offset=bass.IndirectOffsetOnAxis(ap=s.first_i, axis=0)), 16)
    gather(m, pool, f"rows{i}", m.row_table, D)



def place_lookup(m):
    s = m.lk = Memory()
    wide = K * P
    z = m.sums
    s.digits = z[:, 0:J * wide].bitcast(BF16).rearrange("p (j a c) -> p j a c", j=J, a=2)
    around = [J * wide] + [4 * H1 * SL + j * wide for j in range(J - 1)]
    assert around[0] + wide <= 3 * H1 * SL and around[-1] + wide <= 4 * ACOLS
    s.masked = [z[0:NL * H1, at:at + wide] for at in around]
    sel = m.sel[:, :, :].rearrange("p (j k) c -> p j (k c)", j=J)
    s.one_hot = sel[0:NP]
    s.digits_in = [m.sem(f"lookup_digits_in{j}") for j in range(J)]
    s.chosen = m.sem("lookup_chosen")
    s.found = m.sem("lookup_found")
    s.masks = m.sem("lookup_masked")
    s.picked = m.sem("lookup_picked")
    s.copied = m.sem("lookup_copied")
    s.high, s.low = m.n.cols[0:NP, 16:17], m.n.cols[0:NL * H1, 17:18]
    s.heads = m.n.cols[0:NL * H1, 26:26 + H1]


def terms_sync(m, sp, i):
    s, st = m.lk, m.st
    m.n.sync.wait(sp, m.n.sync.plan[m.n.sync.n - 1][0])
    with sp.Fori(0, IT) as it:
        for j in range(J):
            g = it * J + j + G * i
            sp.wait_ge(s.masks, 2 * g + 2)
            for a in range(2):
                sp.dma_start(s.digits[:, j, a, :], m.digit_rows[a:a + 1, bass.ds((it * J + j) * K * P, K * P)]
                             .to_broadcast([P, K * P])).then_inc(s.digits_in[j], 16)
    st.scattered.receive(sp, 16 * NL)
    st.fill_in.send(sp.dma_start(st.arrays[H1][3].rearrange("p h c -> p (h c)"),
                                 m.at_starts.rearrange("(s c) h -> s (c h)", s=NS)), 16)


def terms_vector(m, dve, i):
    s = m.lk
    if not i:
        dve.sem_inc(s.masks, 2 * J)
    half = K * P // 2
    with dve.Fori(0, IT) as it:
        def choose_high(j):
            dve.wait_ge(s.digits_in[j], 32 * (it + IT * i + 1))
            dve.tensor_scalar(s.one_hot[:, j, :], s.digits[0:NP, j, 0, :], s.high, None, ALU.is_equal
                              ).then_inc(s.chosen, 1)

        def mask_low(j):
            g = it * J + j + G * i
            dve.wait_ge(s.found, g + 1)
            dve.wait_ge(s.picked, g + 1)
            for b in range(2):
                dve.scalar_tensor_tensor(s.masked[j][:, b * half:(b + 1) * half],
                                         s.digits[0:NL * H1, j, 1, b * half:(b + 1) * half], s.low,
                                         m.banks[2 * (j % 3) + b][0:NL * H1, :], ALU.is_equal, ALU.mult
                                         ).then_inc(s.masks, 1)

        for j in range(J):
            choose_high(j)
            if j:
                mask_low(j - 1)
        mask_low(J - 1)


def terms_tensor(m, pe, i):
    s = m.lk
    if not i:
        pe.sem_inc(s.picked, J)
    half = K * P // 2
    terms = m.terms[:, 0].rearrange("p l h -> p (l h)")
    with pe.Fori(0, IT) as it:
        def find(j):
            g = it * J + j + G * i
            pe.wait_ge(s.chosen, g + 1)
            pe.wait_ge(s.masks, 2 * g + 2 * J - 2)
            for b in range(2):
                last = pe.matmul(m.banks[2 * (j % 3) + b][0:NL * H1, :], terms,
                                 s.one_hot[:, j, b * half:(b + 1) * half], start=True, stop=True)
            last.then_inc(s.found, 1)

        def pick(j):
            g = it * J + j + G * i
            pe.wait_ge(s.masks, 2 * J + 2 * g + 2)
            pe.wait_ge(s.copied, g + 1)
            for k in range(K):
                last = pe.matmul(m.banks[6 + j % 2][:, k * H1:(k + 1) * H1], s.masked[j][:, k * P:(k + 1) * P],
                                 s.heads, start=True, stop=True)
            last.then_inc(s.picked, 1)

        for j in range(J):
            find(j)
            if j:
                pick(j - 1)
        pick(J - 1)


def terms_scalar(m, act, i):
    s = m.lk
    if not i:
        act.sem_inc(s.copied, 1)
    with act.Fori(0, IT) as it:
        for j in range(J):
            g = it * J + j + G * i
            act.wait_ge(s.picked, J + g + 1)
            act.activation(m.edge[:, bass.ds((it * J + j) * K * H1, K * H1)], m.banks[6 + j % 2][:, 0:K * H1],
                           ACT.Copy).then_inc(s.copied, 1)
    act.wait_ge(s.copied, 1 + G * (i + 1))
    act.sem_inc(m.st.scores_there.sem, 1)
    m.st.scores_there.sent += 1



def bias_scalar(m, act, label, bias, func=ACT.Identity):
    n = m.n
    n.vector.wait(act, label)
    for f in range(2):
        last = act.activation(m.acc[:, 0, f, 0:N], m.acc[:, 0, f, 0:N], func, bias=bias[:, f:f + 1])
    n.scalar.reach(label, last)
    n.scalar.wait(act, label)


def f_scalar(m, act):
    m.n.vector.wait(act, "F sum")
    sums_scalar(m, act, "F")
    m.n.vector.wait(act, "F relu")
    tanh_scalar(m, act, "F")


def f_sync(m, sp):
    m.n.vector.wait(sp, "F product")
    load(m, sp, [(flat, rows) for rows, flat in by_heads(m)])
    load(m, sp, [(m.h[0:NP, :, :].rearrange("p l d -> p (l d)"), m.flat.rearrange("(p c) -> p c", p=NP))])


def f_tensor(m, pe):
    pass_tensor(m, pe, "F", rows_of(m, pe))


def f_vector(m, dve, step):
    n = m.n
    add_parities(m, dve, "F sum")
    read_products(m, dve, "F", lambda l, k: dve.tensor_copy(row(m.h, l), m.banks[k][0:NP, 0:D]))
    n.sync.wait(dve, "F rows")
    h = m.h[0:NP, :, :]
    step(dve.tensor_tensor(h, h, n.b_conv.unsqueeze(1).to_broadcast([NP, NL, D]), ALU.add))
    n.vector.reach("F relu", dve.tensor_scalar(h, h, 0.0, None, ALU.max))
    tanh_ratio_vector(m, dve, step, "F")
    each_node(dve, n.vector, lambda l, k: dve.scalar_tensor_tensor(
        row(m.x, l), row(m.h, l), n.v[14][:, bass.ds(l, 1)], row(m.x, l), ALU.mult, ALU.add))
    n.vector.wait(dve, "F rows")



def place_masked(m):
    s = m.mk = Memory()
    s.sources = m.rows
    s.weighted = m.sums[:, 2 * ACOLS:2 * ACOLS + J * K * P].rearrange("p (t c) -> p t c", c=P)
    w = m.w2[:, :, :].rearrange("p a d -> p (a d)")
    s.fields = w[:, 0:J * K * 4].rearrange("p (j k f) -> p j k f", j=J, k=K)
    s.key = w[:, 160:168]
    s.later = w[:, 168:176]
    s.source = w[:, 176:192].rearrange("p (f k) -> p f k", f=2)
    s.shift = w[:, 192:200]
    s.junk = w[:, 256:256 + K * P]
    s.turns = w[:, 200:201]
    s.turns_i = w[:, 201:202].bitcast(I32)
    s.step = m.sem("masked_step")
    s.fields_free = m.sem("masked_fields_free")
    s.keys = m.sem("masked_keys")
    s.keys_out = m.sem("masked_keys_out")
    s.chosen = m.sem("masked_chosen")
    s.products = m.sem("masked_products")
    s.merged = m.sem("masked_merged")
    s.fields_in = [m.sem(f"masked_fields_in{j}") for j in range(J)]


MASKED_TURN = J * K * P


def masked_turns(m, engine):
    at = D // NL
    _, turns = m.nc.values_load_multi_w_load_instructions(
        m.mk.turns_i[at:at + 1, 0:1], engines=[engine], min_val=1, max_val=IT,
        skip_runtime_bounds_check_because="it is at least 1, and no more than all edges take")
    return turns[0]


def g_sync(m, sp):
    s = m.mk
    m.n.vector.wait(sp, "G turns")
    with sp.Fori(0, masked_turns(m, ENGINE.SP)) as it:
        for j in range(J):
            g = it * J + j
            sp.wait_ge(s.fields_free, g + 1)
            sp.dma_start(s.fields[:, j], m.sorted.rearrange("(g k p) r -> p g k r", k=K, p=P)
                         [:, bass.ds(g, 1), :, 0:4].rearrange("p g k r -> p (g k) r")).then_inc(s.fields_in[j], 16)


def g_vector(m, dve, step):
    n, s = m.n, m.mk
    place = m.start_i[0:NP, D % NL:D % NL + 1]
    step(dve.tensor_copy(s.turns[0:NP, :], place))
    step(dve.tensor_scalar(s.turns[0:NP, :], s.turns[0:NP, :], 1.0 / MASKED_TURN, 0.5 - 0.5 / MASKED_TURN,
                           ALU.mult, ALU.add))
    step(dve.tensor_scalar(s.turns[0:NP, :], s.turns[0:NP, :], 12582912.0, None, ALU.add))
    step(dve.tensor_scalar(s.turns[0:NP, :], s.turns[0:NP, :], -12582912.0, 1.0, ALU.add, ALU.max))
    n.vector.reach("G turns", dve.tensor_copy(s.turns_i[0:NP, :], s.turns[0:NP, :]))
    norm_vector(m, dve, step, "G", m.x)
    dve.sem_inc(s.fields_free, J)
    step(dve.memset(m.acc[:, 0], 0.0))
    step = Chain(dve, s.step)
    tile = [P, K, P]
    with step.loop(masked_turns(m, ENGINE.DVE), J * 26) as it:
        for j in range(J):
            g = it * J + j
            dve.wait_ge(s.fields_in[j], 16 * it + 16)
            source, weight, given = (s.fields[:, j, :, f] for f in (0, 2, 3))
            step(dve.tensor_scalar(s.shift, m.loc[:, bass.ds(g * K, K)], 1.0, None, ALU.add))
            step(dve.scalar_tensor_tensor(s.key, source, float(P), s.shift, ALU.mult, ALU.add))
            dve.tensor_tensor(s.key, s.key, given, ALU.mult).then_inc(s.keys, 1)
            slots = slice(j * K, (j + 1) * K)
            step(dve.tensor_tensor(m.sel[:, slots, :], m.iota.unsqueeze(1).to_broadcast(tile),
                                   m.loc[:, bass.ds(g * K, K)].unsqueeze(2).to_broadcast(tile), ALU.is_equal))
            step.mark(dve.tensor_tensor(s.weighted[:, slots, :], m.sel[:, slots, :],
                                        weight.unsqueeze(2).to_broadcast(tile), ALU.mult))
            dve.wait_ge(s.keys_out, g + 1)
            for k in range(K):
                ins = dve.scalar_tensor_tensor(s.junk[:, k * P:(k + 1) * P],
                                               m.banks[4 + k // 4][:, (k % 4) * P:(k % 4 + 1) * P],
                                               s.key[:, k:k + 1], m.after, ALU.is_equal, ALU.mult,
                                               accum_out=s.later[:, k:k + 1])
            step(ins)
            step(dve.scalar_tensor_tensor(s.later, s.later, 0.0, given, ALU.is_equal, ALU.mult))
            step(dve.tensor_scalar(s.source[:, 0], source, 1.0, None, ALU.add))
            step(dve.tensor_tensor(s.source[:, 0], s.source[:, 0], s.later, ALU.mult))
            step(dve.tensor_scalar(s.source[:, 1], s.source[:, 0], -1.0 - P, None, ALU.add))
            step(dve.tensor_scalar(s.source[:, 0], s.source[:, 0], -1.0, None, ALU.add))
            for f in range(2):
                dve.tensor_tensor(s.sources[:, slots, f * P:(f + 1) * P], m.iota.unsqueeze(1).to_broadcast(tile),
                                  s.source[:, f].unsqueeze(2).to_broadcast(tile), ALU.is_equal).then_inc(s.chosen, 1)
            dve.wait_ge(s.chosen, 2 * g + 2)
            dve.sem_inc(s.fields_free, 1)
            first = windows(m, ENGINE.DVE, g)
            for k in range(K):
                dve.wait_ge(s.products, K * g + k + 1)
                bank = m.banks[k % 4][:, :].rearrange("p (f c) -> p f c", f=2)
                old = s.junk[:, 0:2 * P].rearrange("p (f c) -> p f c", f=2)
                w = m.acc[:, 0, :, bass.ds(first[k], P)]
                step(dve.tensor_tensor(old, w, bank[:, :, 0:P], ALU.mult))
                step(dve.tensor_tensor(w, w, old, ALU.subtract))
                dve.tensor_tensor(w, w, bank[:, :, P:2 * P], ALU.add).then_inc(s.merged, 1)
                dve.wait_ge(s.merged, 4 + K * g + k + 1)
    n.vector.reach("G weights", dve.memset(s.later, 0.0))
    read_products(m, dve, "G", lambda l, k: dve.tensor_tensor(row(m.x, l), m.banks[k][0:NP, 0:D], row(m.x, l),
                                                              ALU.add))
    n.vector.wait(dve, "G rows")


def g_tensor(m, pe):
    s = m.mk
    pe.sem_inc(s.merged, 4)
    m.n.vector.wait(pe, "G turns")
    with pe.Fori(0, masked_turns(m, ENGINE.PE)) as it:
        for j in range(J):
            g = it * J + j
            pe.wait_ge(s.keys, g + 1)
            pe.wait_ge(s.chosen, 2 * g)
            for k in range(K):
                last = pe.matmul(m.banks[4 + k // 4][:, (k % 4) * P:(k % 4 + 1) * P],
                                 s.key[:, k:k + 1].to_broadcast([P, P]), m.ident, start=True, stop=True)
            last.then_inc(s.keys_out, 1)
            pe.wait_ge(s.chosen, 2 * g + 2)
            for k in range(K):
                pe.wait_ge(s.merged, K * g + k + 1)
                for f in range(2):
                    for i, side in enumerate((m.sel, s.weighted)):
                        last = pe.matmul(m.banks[k % 4][:, (2 * f + i) * P:(2 * f + i + 1) * P],
                                         s.sources[:, j * K + k, f * P:(f + 1) * P], side[:, j * K + k, :],
                                         start=True, stop=True)
                last.then_inc(s.products, 1)
    m.n.vector.wait(pe, "G weights")
    pass_tensor(m, pe, "G", product_of(m, pe, m.acc[:, 0], D))


def g_scalar(m, act):
    norm_scalar(m, act, "G")
    m.n.vector.wait(act, "G weights")
    pass_scalar(m, act, "G", normed(m, act, m.x, ACT.Relu), lambda l, k: turn_back(m, act, k))



def h_sync(m, io, sp, i):
    n = m.n
    n.vector.wait(sp, f"H{i - 1} rows" if i else "G rows")
    load(m, sp, [(n.w[:, :, 0:D], io[f"w3_{i}"]),
                 (n.att, spread(io[f"att3_{i}"], P, 2 * D).rearrange("p (a d) -> p a d", a=2))])
    tables_sync(m, sp, f"H{i} rows")


def h_vector(m, dve, step, i):
    n = m.n
    if i == 0:
        norm_vector(m, dve, step, "H", m.x)
    n.sync.wait(dve, f"H{i} weights")
    for a in range(2):
        step(dve.tensor_tensor(n.scratch, n.w[:, :, 0:D], n.att[:, a].unsqueeze(1).to_broadcast([P, 2, D]), ALU.mult))
        at = D + a * H1
        last = dve.tensor_reduce(n.w[:, :, at:at + H1], n.scratch.rearrange("p f (h d) -> p f h d", h=H1),
                                 AX.X, ALU.add)
        if a == 0:
            step(last)
    n.vector.reach(f"H{i} weights", last)
    if i:
        add_parities(m, dve, f"H{i} sum")
    with dve.Fori(0, NL // J) as it:
        for k in range(J):
            l = it * J + k
            done(dve, n.out_ready, f"H{i}", l)
            dve.tensor_copy(row(m.h, l), m.banks[k][0:NP, 0:D])
            dve.tensor_copy(m.terms[:, :, bass.ds(l, 1), :].rearrange("p a l h -> p a (l h)"),
                            m.banks[k][0:NP, D:D + 2 * H1].rearrange("p (a h) -> p a h", a=2)
                            ).then_inc(n.out_read.sem, 1)
    done(dve, n.out_read, f"H{i}", NL - 1)
    dve.sem_inc(n.vector.sem, NL)
    n.vector.n += 1


def h_scalar(m, act, i):
    n = m.n
    if i == 0:
        norm_scalar(m, act, "H")
        pass_scalar(m, act, "H0", normed(m, act, m.x, ACT.Relu), lambda l, k: turn_back(m, act, k))
    else:
        bias_scalar(m, act, f"H{i} sum", n.b3[i - 1])
        sums_scalar(m, act, f"H{i}")


def h_tensor(m, pe, i):
    m.n.vector.wait(pe, f"H{i} weights")
    pass_tensor(m, pe, f"H{i}", product_of(m, pe, m.n.w, D + 2 * H1))


def j_vector(m, dve):
    add_parities(m, dve, "J sum")
    read_products(m, dve, "J", lambda l, k: dve.tensor_tensor(row(m.x, l), m.banks[k][0:NP, 0:D], row(m.x, l),
                                                              ALU.add))


def j_scalar(m, act):
    bias_scalar(m, act, "J sum", m.n.b3[2])
    sums_scalar(m, act, "J")


def j_tensor(m, pe):
    pass_tensor(m, pe, "J", rows_of(m, pe))


def j_sync(m, out, sp):
    m.n.vector.wait(sp, "J rows")
    load(m, sp, [(out.rearrange("(p l) d -> p l d", l=NL), m.x[0:NP, :, :])])
    m.n.sync.wait(sp, "output")


def build(nc, io, out):
    with ExitStack() as ctx:
        m = place_memory(nc, ctx)
        place_nodes(m)
        place_sort(m)
        place_scores(m)
        place_strips(m)
        place_masked(m)
        place_lookup(m)
        plan_gathers(m)
        plan_aggregates(m)
        block = ctx.enter_context(nc.Block())

        @block.sync
        def _(sp):
            a_sync(m, io, sp)
            sort_sync(m, io, sp)
            fields_sync(m, sp)
            scores_sync(m, sp)
            b_sync(m, io, sp)
            d_sync(m, io, sp)
            terms_sync(m, sp, 0)
            f_sync(m, sp)
            g_sync(m, sp)
            for i in LAYERS:
                h_sync(m, io, sp, i)
                terms_sync(m, sp, i + 1)
            j_sync(m, out, sp)

        @block.vector
        def _(dve):
            step = Chain(dve, m.vector_step)
            a_vector(m, dve, step)
            sort_vector(m, dve, step)
            fields_vector(m, dve, step)
            flags_vector(m, dve, step)
            scores_vector(m, dve, step)
            strips_vector(m, dve, step, H0, least=MIN_NORM)
            aggregate_vector(m, dve, step, "values", H0)
            b_vector(m, dve, step)
            c_vector(m, dve, step)
            d_vector(m, dve, step)
            terms_vector(m, dve, 0)
            strips_vector(m, dve, step, H1, slope=0.2, least=MIN_NORM)
            aggregate_vector(m, dve, step, "rows0", H1)
            f_vector(m, dve, step)
            g_vector(m, dve, step)
            for i in LAYERS:
                h_vector(m, dve, step, i)
                terms_vector(m, dve, i + 1)
                strips_vector(m, dve, step, H1, slope=0.2, more=1e-16)
                aggregate_vector(m, dve, step, f"rows{i + 1}", H1)
            j_vector(m, dve)

        @block.tensor
        def _(pe):
            a_tensor(m, pe)
            sort_tensor(m, pe)
            fields_tensor(m, pe)
            flags_tensor(m, pe)
            scores_tensor(m, pe)
            strips_tensor(m, pe, H0)
            aggregate_tensor(m, pe, "values")
            b_tensor(m, pe)
            c_tensor(m, pe)
            d_tensor(m, pe)
            terms_tensor(m, pe, 0)
            strips_tensor(m, pe, H1)
            aggregate_tensor(m, pe, "rows0")
            f_tensor(m, pe)
            g_tensor(m, pe)
            for i in LAYERS:
                h_tensor(m, pe, i)
                terms_tensor(m, pe, i + 1)
                strips_tensor(m, pe, H1)
                aggregate_tensor(m, pe, f"rows{i + 1}")
            j_tensor(m, pe)

        @block.scalar
        def _(act):
            a_scalar(m, act)
            sort_scalar(m, act)
            fields_scalar(m, act)
            scores_scalar(m, act)
            strips_scalar(m, act, H0)
            b_scalar(m, act)
            c_scalar(m, act)
            d_scalar(m, act)
            terms_scalar(m, act, 0)
            strips_scalar(m, act, H1)
            f_scalar(m, act)
            g_scalar(m, act)
            for i in LAYERS:
                h_scalar(m, act, i)
                terms_scalar(m, act, i + 1)
                strips_scalar(m, act, H1)
            j_scalar(m, act)

        @block.gpsimd
        def _(pool):
            sort_pool(m, pool)
            keys_pool(m, pool)
            gather(m, pool, "values", m.row_table, D)
            terms_pool(m, pool, 0, "D tables")
            for i in LAYERS:
                terms_pool(m, pool, i + 1, f"H{i} tables")


def layout(a):
    f = np.float32
    loop = np.arange(N, dtype=np.int32)
    src = np.concatenate([a["src"], loop, np.zeros(EP - EL, np.int32)]).astype(np.int32)
    dst = np.concatenate([a["dst"], loop, np.full(EP - EL, N, np.int32)]).astype(np.int32)
    weight = np.concatenate([a["edge_weight"], np.zeros(EP - E, f)])
    given = np.concatenate([np.ones(E, f), np.zeros(EP - E, f)])

    def tiles(v):
        return np.ascontiguousarray(v.reshape(T, P).T)

    ef = np.zeros((ED + 1, EP), f)
    ef[0:ED, 0:E] = a["edge_attr_64"].T
    ef[ED, :] = 1.0
    row, col = np.indices((P, P))
    consts = np.stack([col, col < row, col > row, col == row, row == 0, row == col - 1, row == col + 1], 1).astype(f)
    out = dict(x=a["x"], src_tiles=tiles(src), dst_tiles=tiles(dst), weight_tiles=tiles(weight),
               given_tiles=tiles(given), dst_row=dst[None, :], efT=ef, consts=consts,
               We=np.concatenate([a["L0_gnn_We"], a["L0_gnn_be"][None, :]]))
    return {k: np.ascontiguousarray(v) for k, v in out.items()}
def node_inputs(a):
    f = np.float32

    def halves(w):
        return np.ascontiguousarray(w.reshape(2, P, -1).transpose(1, 0, 2))

    def col(v):
        return v.reshape(-1, P).T

    cols = [col(a["L0_gnn_" + k]) for k in ("ln1_g", "ln1_b", "ln2_g", "ln2_b", "b1")]
    place = np.arange(P)
    cols += [np.stack([place, place // H1], 1)] + [col(a[f"L3_gnn_b{i}"]) for i in range(3)]
    cols += [np.broadcast_to(a["L0_gnn_alpha"], (P, 1)), np.broadcast_to(a["L0_gnn_beta"], (P, 1)),
             place[:, None] % H1 == np.arange(H1)]
    out = dict(cols=np.concatenate(cols, 1),
               qkv=halves(np.concatenate([a["L0_gnn_Wq"], a["L0_gnn_Wk"], a["L0_gnn_Wv"]], 1)),
               qkv_bias=np.concatenate([a["L0_gnn_bq"], a["L0_gnn_bk"], a["L0_gnn_bv"]])[None],
               wo=halves(a["L0_gnn_Wo"]), bo=a["L0_gnn_bo"][None], b_ff=a["L0_gnn_b2"][None],
               w1=halves(a["L0_gnn_W1"]), w2=a["L0_gnn_W2"].reshape(FF // P, P, D).transpose(1, 0, 2),
               w_hyp=halves(a["L1_gnn_W"].T), b_lin=a["L1_gnn_b_lin"][None], b_conv=a["L1_gnn_b_conv"][None],
               att_hyp=np.concatenate([a["L1_gnn_att"][:, 64:].reshape(-1), a["L1_gnn_att"][:, :64].reshape(-1)])[None])
    for i in range(3):
        out[f"w3_{i}"] = halves(a[f"L3_gnn_W{i}"])
        out[f"att3_{i}"] = np.concatenate([a[f"L3_gnn_as{i}"].reshape(-1), a[f"L3_gnn_ad{i}"].reshape(-1)])[None]
    return {k: np.ascontiguousarray(v, dtype=f) for k, v in out.items()}


def kernel(**a):
    from concourse import bacc
    from concourse.bass_utils import run_bass_kernel_spmd

    nc = bacc.Bacc("TRN2", target_bir_lowering=False, num_devices=1)
    a = {k: np.asarray(v) for k, v in a.items()}
    arrays = {"in_" + k: v for k, v in {**layout(a), **node_inputs(a)}.items()}
    io = {k[3:]: nc.dram_tensor(k, v.shape, mybir.dt.from_np(v.dtype), kind="ExternalInput").ap()
          for k, v in arrays.items()}
    out = nc.dram_tensor("out", (N, D), F32, kind="ExternalOutput").ap()
    build(nc, io, out)
    result = run_bass_kernel_spmd(nc, [arrays], core_ids=[0])
    return result.results[0]["out"]
```

```python
from contextlib import ExitStack

import numpy as np

import concourse.bass as bass
from concourse import mybir

ALU = mybir.AluOpType
ACT = mybir.ActivationFunctionType
AX = mybir.AxisListType
F32 = mybir.dt.float32
BF16 = mybir.dt.bfloat16
I32 = mybir.dt.int32
ENGINE = mybir.EngineType

P = 128
N, D = 3125, 256
NP, NL = 125, 25
E = 53125
EL = E + N
T = -(-EL // P)
K = 8
J = 5
IT = T // (K * J)
G = IT * J
TP = T + K
EP = T * P
SL = 512
NS = EP // SL
FB = SL // P
ED = 64
DH0 = 32
H0, H1 = 8, 4
ROW = 4 + DH0
NB = N + 1
HI = NB // NL + 1 if NB % NL else NB // NL
W2 = 2 * P
ACOLS = N + W2
SUMS = 4 * (N + P)
FF = 4 * D
BIG = 1.0e30
LN_EPS = 1e-5
assert IT * J * K == T and NS * SL == EP and NL * NP == N


def node_rows(table, width):
    return table[0:N, 0:width].rearrange("(p l) d -> p l d", l=NL)


class Chain:

    def __init__(self, eng, sem):
        self.eng, self.sem, self.n, self.turn, self.per = eng, sem, 0, None, 0

    def __call__(self, ins):
        self.mark(ins)
        self.wait()

    def mark(self, ins):
        ins.then_inc(self.sem, 1)
        self.n += 1

    def wait(self, back=0):
        value = self.n - back
        if self.turn is not None:
            value = self.turn * self.per + value
        self.eng.wait_ge(self.sem, value)

    def loop(self, turns, per):
        outer = self

        class Loop:
            def __enter__(self):
                self.fori = outer.eng.Fori(0, turns)
                self.first = outer.n
                outer.turn, outer.per = self.fori.__enter__(), per
                return outer.turn

            def __exit__(self, *e):
                assert e[0] is not None or outer.n - self.first == per, (outer.n - self.first, per)
                self.fori.__exit__(*e)
                outer.turn, outer.n = None, self.first + turns * per if isinstance(turns, int) else None

        return Loop()


class Signal:

    def __init__(self, sem):
        self.sem, self.total, self.base = sem, 0, {}

    def plan(self, stage, n):
        self.base[stage] = self.total
        self.total += n


class Turns:

    def __init__(self, sem):
        self.sem, self.sent, self.seen = sem, 0, {}

    def send(self, ins, n=1):
        self.sent += n
        ins.then_inc(self.sem, n)

    def receive(self, eng, n=1):
        self.seen[eng.engine] = self.seen.get(eng.engine, 0) + n
        eng.wait_ge(self.sem, self.seen[eng.engine])


class Memory:
    pass


def place_memory(nc, ctx):
    m = Memory()
    m.nc = nc

    def sb(name, shape, dt=F32):
        return ctx.enter_context(nc.sbuf_tensor("sb_" + name, shape, dt))

    def sem(name):
        return ctx.enter_context(nc.semaphore(name))

    def dram(name, shape, dt=F32):
        return nc.dram_tensor(name, shape, dt, kind="Internal").ap()

    m.sb, m.sem, m.dram = sb, sem, dram
    m.x = sb("x", [P, NL, D])
    m.h = sb("h", [P, NL, D])
    m.sums = sb("sums", [P, SUMS])
    m.zeros = m.sums[:, SUMS - SL * H1:SUMS]
    m.acc = m.sums[:, 0:2 * ACOLS].rearrange("p (f c) -> p f c", f=2)
    m.rows = sb("rows", [P, J * K, D])
    m.sel = sb("sel", [P, J * K, P])
    m.w1 = sb("w1", [P, 2, FF])
    m.w2 = sb("w2", [P, FF // P, D])
    m.consts = sb("consts", [P, 7, P])
    (m.iota, m.before, m.after, m.ident, m.first_row, m.shift_on,
     m.shift_back) = (m.consts[:, i, :] for i in range(7))
    m.edge = sb("edge", [P, T * 2 * 4])
    m.fields = m.edge[:, 0:T * 4].rearrange("p (t f) -> p t f", f=4)
    m.src_i = sb("src_i", [P, TP], I32)
    m.src_now = sb("src_now", [P, J, K], I32)
    m.start_i = sb("start_i", [P, NL], I32)
    m.banks = [ctx.enter_context(nc.psum_tensor(f"bank{i}", [P, 512], F32)) for i in range(8)]
    m.sorted = dram("sorted_edges", [EP, ROW])
    m.loc = sb("loc", [P, TP], BF16)
    m.base_i = sb("base_i", [P, T], I32)
    m.flags = sb("flags", [P, 3, SL])
    m.goes_on, m.has_next, m.at_start = (m.flags[0:NS, i, :] for i in range(3))
    m.small = sb("small", [P, 192])
    m.fields_sorted = m.w1[:, :, :].rearrange("p a c -> p (a c)")[:, 0:4 * T].rearrange("p (t f) -> p t f", f=4)
    m.digit_rows = dram("digit_rows", [2, EP], BF16)
    m.q_table = dram("q_table", [ACOLS, D])
    m.k_table = dram("k_table", [N, D])
    m.row_table = dram("row_table", [N, D])
    m.dst_table = dram("dst_table", [N, H1])
    m.flat = dram("flat_rows", [N * D])
    m.at_starts = dram("at_starts", [EP, H1])
    m.landed = [sem(f"landed{j}") for j in range(J)]
    m.rows_free = Signal(sem("rows_free"))
    m.taken = Signal(sem("sources_taken"))
    m.vector_step = sem("vector_step")
    m.scalar_step = sem("scalar_step")
    m.pool_step = sem("pool_step")
    return m



def place_sort(m):
    s = m.s = Memory()
    a = m.sums
    at = 0

    def cut(n):
        nonlocal at
        at += n
        return a[:, at - n:at]

    s.src0 = cut(T).bitcast(I32)
    s.dst0 = cut(T).bitcast(I32)
    s.hi = cut(T)
    s.lo = cut(T)
    s.t1 = cut(T)
    s.t2 = cut(T)
    s.one_hi = cut(J * K * HI // 2).bitcast(BF16).rearrange("p (j k h) -> p j k h", j=J, k=K)
    s.one_lo = cut(J * K * NL // 2).bitcast(BF16).rearrange("p (j k l) -> p j k l", j=J, k=K)
    s.payload = cut(J * K * ROW).rearrange("p (j k r) -> p j k r", j=J, k=K)
    s.place = cut(J * NL * K).rearrange("p (j l k) -> p j l k", j=J, l=NL)
    s.incl = cut(NL * K)
    s.excl = cut(NL * K)
    s.keep = cut(NL * K)
    s.now = cut(NL)
    s.count = cut(NL)
    s.zeros = cut(K).bitcast(I32)
    s.pos_now = cut(J * K).bitcast(I32).rearrange("p (j k) -> p j k", j=J)
    s.rowsum = cut(1)
    s.rank = cut(J * K).rearrange("p (j k) -> p j k", j=J)
    s.found = cut(J * K).rearrange("p (j k) -> p j k", j=J)
    s.junk = cut(K * P)
    s.dst_now = cut(J * K).rearrange("p (j k) -> p j k", j=J)
    s.picked = cut(K * NL)
    s.weights = cut(DH0)
    assert at <= SUMS
    s.hi_t = m.sel[:, :, :].rearrange("p (j k) c -> p j (k c)", j=J)
    r = m.rows[:, :, :].rearrange("p t d -> p (t d)")
    s.ef = r[:, 0:J * K * P].rearrange("p (j c) -> p j c", j=J)
    s.dst_row = r[:, J * K * P:2 * J * K * P].bitcast(I32).rearrange("p (j c) -> p j c", j=J)
    s.ident_bf = cut(P // 2).bitcast(BF16)
    s.zero_bf = cut(P // 2).bitcast(BF16)
    s.place_i = cut(J * K).bitcast(I32).rearrange("p (j k) -> p j k", j=J)
    assert at <= SUMS
    s.inputs = m.sem("sort_inputs")
    s.ready = m.sem("sort_ready")
    s.digits = m.sem("sort_digits")
    s.digits_free = m.sem("sort_digits_free")
    s.counted = m.sem("sort_counted")
    s.summed = m.sem("sort_summed")
    s.sum_done = m.sem("sort_sum_done")
    s.tile_counted = m.sem("sort_tile_counted")
    s.turned = m.sem("sort_turned")
    s.turned_read = m.sem("sort_turned_read")
    s.placed = m.sem("sort_placed")
    s.look_read = m.sem("sort_look_read")
    s.projected_read = m.sem("sort_projected_read")
    s.row_free = m.sem("sort_row_free")
    s.ef_free = m.sem("sort_ef_free")
    s.pos_ready = m.sem("sort_pos_ready")
    s.taken = m.sem("sort_taken")
    s.fields_in = m.sem("sort_fields_in")
    s.sent_all = m.sem("sort_sent_all")
    s.row_in = [m.sem(f"sort_row_in{j}") for j in range(J)]
    s.ef_in = [m.sem(f"sort_ef_in{j}") for j in range(J)]
    s.sent = [m.sem(f"sort_sent{j}") for j in range(J)]


def sort_inputs(m, io, sp):
    s = m.s
    sp.dma_start(s.src0[:, 0:T], io["src_tiles"]).then_inc(s.inputs, 16)
    sp.dma_start(s.dst0[:, 0:T], io["dst_tiles"]).then_inc(s.inputs, 16)
    sp.dma_start(s.t1[:, 0:T], io["weight_tiles"]).then_inc(s.inputs, 16)
    sp.dma_start(s.t2[:, 0:T], io["given_tiles"]).then_inc(s.inputs, 16)
    sp.dma_start(s.weights[0:ED + 1, :], io["We"]).then_inc(s.inputs, 16)


def sort_sync(m, io, sp):
    s = m.s
    with sp.Fori(0, IT) as it:
        for j in range(J):
            g = it * J + j
            sp.wait_ge(s.row_free, g + 1)
            sp.dma_start(s.dst_row[:, j, :], io["dst_row"][0:1, bass.ds(g * K * P, K * P)].to_broadcast([P, K * P])
                         ).then_inc(s.row_in[j], 16)
            sp.wait_ge(s.ef_free, g + 1)
            sp.dma_start(s.ef[0:ED + 1, j, :], io["efT"][:, bass.ds(g * K * P, K * P)]).then_inc(s.ef_in[j], 16)


def digits_of_group(m, dve, g, j, signal):
    s = m.s
    for one, digit, width in ((s.one_hi, s.hi, HI), (s.one_lo, s.lo, NL)):
        dve.tensor_tensor(one[:, j], m.iota[:, 0:width].unsqueeze(1).to_broadcast([P, K, width]),
                          digit[:, bass.ds(g * K, K)].unsqueeze(2).to_broadcast([P, K, width]),
                          ALU.is_equal).then_inc(signal, 1)


def sort_vector(m, dve, step):
    s = m.s
    dve.sem_inc(s.row_free, J)
    dve.wait_ge(s.inputs, 80)
    step.mark(dve.tensor_copy(m.fields[:, :, 0], s.src0[:, :]))
    step.mark(dve.tensor_copy(m.fields[:, :, 1], s.dst0[:, :]))
    step.mark(dve.tensor_copy(m.fields[:, :, 2], s.t1[:, :]))
    step.mark(dve.tensor_copy(m.fields[:, :, 3], s.t2[:, :]))
    step(dve.memset(s.zero_bf[:, :], 0.0))
    dve.tensor_copy(s.ident_bf[:, :], m.ident).then_inc(s.ready, 1)
    dst = m.fields[:, :, 1]
    step(dve.tensor_scalar(s.t1[:, :], dst, 1.0 / NL, -(0.5 - 0.5 / NL), ALU.mult, ALU.add))
    step(dve.tensor_scalar(s.t2[:, :], s.t1[:, :], 12582912.0, None, ALU.add))
    step(dve.tensor_scalar(s.hi[:, :], s.t2[:, :], -12582912.0, None, ALU.add))
    step(dve.scalar_tensor_tensor(s.lo[:, :], s.hi[:, :], -float(NL), dst, ALU.mult, ALU.add))
    with dve.Fori(0, IT) as it:
        for j in range(J):
            g = it * J + j
            dve.wait_ge(s.digits_free, g + 1)
            digits_of_group(m, dve, g, j, s.digits)
    dve.wait_ge(s.counted, 1)
    step(dve.tensor_copy(s.count[0:HI, :], m.banks[0][0:HI, 0:NL]))
    dve.tensor_reduce(s.rowsum[0:HI, :], s.count[0:HI, :], AX.X, ALU.add).then_inc(s.summed, 1)
    step(dve.memset(s.excl[0:HI, 0:NL], 1.0))
    dve.wait_ge(s.sum_done, 1)
    step(dve.tensor_copy(s.rowsum[0:HI, :], m.banks[0][0:HI, 64:65]))
    step(dve.tensor_tensor_scan(s.incl[0:HI, 0:NL], s.excl[0:HI, 0:NL], s.count[0:HI, :],
                                s.rowsum[0:HI, :], ALU.mult, ALU.add))
    step(dve.tensor_tensor(s.now[0:HI, :], s.incl[0:HI, 0:NL], s.count[0:HI, :], ALU.subtract))
    step(dve.tensor_copy(m.start_i[0:NP, :], s.now[0:NP, :]))
    step(dve.memset(s.keep[:, :], 1.0))
    step(dve.memset(s.keep[:, :].rearrange("p (l k) -> p l k", k=K)[:, :, 0:1], 0.0))

    def places(it, j):
        g = it * J + j
        dve.wait_ge(s.digits_free, G + g + 1)
        digits_of_group(m, dve, g, j, s.digits)
        step.mark(dve.tensor_copy(s.dst_now[:, j, :], m.fields[:, bass.ds(g * K, K), 1]))
        dve.wait_ge(s.tile_counted, g + 1)
        count = m.banks[1][0:HI, 0:NL * K]
        now = s.now[0:HI, :]
        incl = s.incl[0:HI, :].rearrange("p (l k) -> p l k", k=K)
        excl = s.excl[0:HI, :].rearrange("p (l k) -> p l k", k=K)
        step(dve.tensor_tensor_scan(s.incl[0:HI, :], s.keep[0:HI, :], count, 0.0, ALU.mult, ALU.add))
        step(dve.tensor_tensor(s.excl[0:HI, :], s.incl[0:HI, :], count, ALU.subtract))
        dve.tensor_tensor(s.place[0:HI, j], excl, now.unsqueeze(2).to_broadcast([HI, NL, K]),
                          ALU.add).then_inc(s.placed, 1)
        dve.wait_ge(s.placed, g + 1)
        step(dve.tensor_tensor(now, now, incl[:, :, K - 1], ALU.add))
        dve.wait_ge(s.row_in[j], 16 * it + 16)
        for k in range(K):
            last = dve.scalar_tensor_tensor(
                s.junk[:, k * P:(k + 1) * P], s.dst_row[:, j, k * P:(k + 1) * P], s.dst_now[:, j, k:k + 1],
                m.before, ALU.is_equal, ALU.mult, accum_out=s.rank[:, j, k:k + 1])
        last.then_inc(s.row_free, 1)

    def place_edges(it, j):
        g = it * J + j
        dve.wait_ge(s.digits_free, J + G + g + 1)
        dve.tensor_tensor(s.picked[:, :], m.banks[3][:, 0:K * NL],
                          s.one_lo[:, j].rearrange("p k l -> p (k l)"), ALU.mult).then_inc(s.look_read, 1)
        dve.wait_ge(s.look_read, g + 1)
        step(dve.tensor_reduce(s.found[:, j, :], s.picked[:, :].rearrange("p (k l) -> p k l", l=NL),
                               AX.X, ALU.add))
        dve.wait_ge(s.row_free, J + g + 1)
        dve.wait_ge(s.taken, g + 1)
        dve.tensor_tensor(s.place_i[:, j, :], s.found[:, j, :], s.rank[:, j, :], ALU.add).then_inc(s.pos_ready, 1)

    places(0, 0)
    with step.loop(IT - 1, J * 5) as it:
        for j in range(J):
            places(it + (j + 1) // J, (j + 1) % J)
            place_edges(it, j)
    for j in range(J):
        if j + 1 < J:
            places(IT - 1, j + 1)
        place_edges(IT - 1, j)
    dve.wait_ge(s.pos_ready, G)
    dve.sem_inc(s.pos_ready, 1)


def sort_tensor(m, pe):
    s = m.s
    pe.sem_inc(s.digits_free, J)
    pe.sem_inc(s.ef_free, J)
    pe.wait_ge(s.inputs, 80)
    pe.wait_ge(s.ready, 1)
    total = m.banks[0][0:HI, 0:NL]
    pe.matmul(total, s.zero_bf[:, 0:HI], s.zero_bf[:, 0:NL], start=True, stop=False, skip_group_check=True)
    with pe.Fori(0, IT) as it:
        for j in range(J):
            g = it * J + j
            pe.wait_ge(s.digits, 2 * g + 2)
            for k in range(K):
                last = pe.matmul(total, s.one_hi[:, j, k], s.one_lo[:, j, k], start=False, stop=False,
                                 skip_group_check=True)
            last.then_inc(s.digits_free, 1)
    pe.matmul(total, s.zero_bf[:, 0:HI], s.zero_bf[:, 0:NL], start=False, stop=True,
              skip_group_check=True).then_inc(s.counted, 1)
    pe.wait_ge(s.summed, 1)
    pe.matmul(m.banks[0][0:HI, 64:65], m.after[0:HI, 0:HI], s.rowsum[0:HI, :], start=True, stop=True
              ).then_inc(s.sum_done, 1)
    turned = m.banks[2][:, :].bitcast(BF16)
    with pe.Fori(0, IT) as it:
        for j in range(J):
            g = it * J + j
            pe.wait_ge(s.digits, 2 * G + 2 * g + 2)
            pe.wait_ge(s.placed, g)
            for k in range(K):
                count = m.banks[1][0:HI, 0:NL * K].rearrange("p (l k) -> p l k", k=K)[:, :, k]
                last = pe.matmul(count, s.one_hi[:, j, k], s.one_lo[:, j, k], start=True, stop=True)
            last.then_inc(s.tile_counted, 1)
            pe.wait_ge(s.turned_read, g)
            for k in range(K):
                last = pe.transpose(turned[0:HI, k * P:(k + 1) * P], s.one_hi[:, j, k], s.ident_bf[:, :])
            last.then_inc(s.turned, 1)
            pe.wait_ge(s.ef_in[j], 16 * it + 16)
            pe.wait_ge(s.projected_read, g)
            for k in range(K):
                last = pe.matmul(m.banks[4][:, k * DH0:(k + 1) * DH0], s.ef[0:ED + 1, j, k * P:(k + 1) * P],
                                 s.weights[0:ED + 1, :], start=True, stop=True)
            last.then_inc(s.ef_free, 1)
            pe.wait_ge(s.turned_read, g + 1)
            pe.wait_ge(s.placed, g + 1)
            pe.wait_ge(s.look_read, g)
            for k in range(K):
                last = pe.matmul(m.banks[3][:, k * NL:(k + 1) * NL], s.hi_t[0:HI, j, k * P:(k + 1) * P],
                                 s.place[0:HI, j, :, k], start=True, stop=True)
            last.then_inc(s.digits_free, 1)


def sort_scalar(m, act):
    s = m.s
    turned = m.banks[2][:, :].bitcast(BF16)
    with act.Fori(0, IT) as it:
        for j in range(J):
            g = it * J + j
            act.wait_ge(s.turned, g + 1)
            act.activation(s.hi_t[0:HI, j, :], turned[0:HI, :], ACT.Copy).then_inc(s.turned_read, 1)
            act.wait_ge(s.sent[j], 16 * K * it)
            act.activation(s.payload[:, j, :, 0:4], m.fields[:, bass.ds(g * K, K), :],
                           ACT.Copy).then_inc(s.fields_in, 1)
            act.wait_ge(s.ef_free, J + g + 1)
            act.activation(s.payload[:, j, :, 4:ROW], m.banks[4][:, 0:K * DH0].rearrange("p (k d) -> p k d", k=K),
                           ACT.Copy).then_inc(s.projected_read, 1)


def sort_pool(m, pool):
    s = m.s

    def take(g, j):
        pool.tensor_tensor(s.pos_now[:, j, :], s.place_i[:, j, :], s.zeros[:, :], ALU.add).then_inc(s.taken, 1)

    pool.sem_inc(s.taken, J)
    pool.memset(s.zeros[:, :], 0).then_inc(m.pool_step, 1)
    pool.wait_ge(m.pool_step, 1)
    pool.wait_ge(s.pos_ready, 1)
    take(0, 0)
    with pool.Fori(0, IT) as it:
        for j in range(J):
            g = it * J + j
            pool.wait_ge(s.fields_in, g + 1)
            pool.wait_ge(s.projected_read, g + 1)
            pool.wait_ge(s.taken, J + g + 1)
            nxt = (j + 1) % J
            pool.wait_ge(s.sent[nxt], 16 * K * (it + (nxt == 0)))
            pool.wait_ge(s.pos_ready, g + 2)
            take(g + 1, nxt)
            for k in range(K):
                pool.indirect_dma_start(out=m.sorted[:, :],
                                        out_offset=bass.IndirectOffsetOnAxis(ap=s.pos_now[:, j, k:k + 1], axis=0),
                                        in_=s.payload[:, j, k, :], in_offset=None).then_inc(s.sent[j], 16)
    for j in range(J):
        pool.wait_ge(s.sent[j], 16 * K * IT)
    pool.wait_ge(s.taken, J + G + 1)
    pool.sem_inc(s.sent_all, 1)



GATHERS = ["keys", "values"] + [f"rows{i}" for i in range(4)]


def plan_gathers(m):
    m.rows_free.total = J
    for n, stage in enumerate(GATHERS):
        m.rows_free.plan(stage, G)
        m.taken.plan(stage, G + 1)


def landed(m, eng, stage, it, j):
    eng.wait_ge(m.landed[j], 16 * K * (IT * GATHERS.index(stage) + it + 1))


def gather(m, pool, stage, table, width, numbers=None):
    b, t = m.rows_free.base[stage], m.taken.base[stage]

    def take(g, j):
        pool.tensor_copy(m.src_now[:, j, :], m.src_i[:, bass.ds(g * K, K)]).then_inc(m.taken.sem, 1)

    if t:
        pool.wait_ge(m.taken.sem, t)
        for j in range(J):
            pool.wait_ge(m.landed[j], 16 * K * IT * GATHERS.index(stage))
    if numbers:
        numbers(0, 0)
    take(0, 0)
    with pool.Fori(0, IT) as it:
        for j in range(J):
            g = it * J + j
            if numbers:
                numbers(it + (j + 1) // J, (j + 1) % J)
            pool.wait_ge(m.taken.sem, t + g + 1)
            pool.wait_ge(m.rows_free.sem, b - J + g + 1)
            nxt = (j + 1) % J
            pool.wait_ge(m.landed[nxt], 16 * K * (IT * GATHERS.index(stage) + it + (nxt == 0)))
            take(g + 1, nxt)
            for k in range(K):
                out = m.rows[:, j * K + k, 0:width]
                pool.indirect_dma_start(out=out, out_offset=None, in_=table[:, :],
                                        in_offset=bass.IndirectOffsetOnAxis(ap=m.src_now[:, j, k:k + 1], axis=0)
                                        ).then_inc(m.landed[j], 16)



def place_scores(m):
    s = m.sc = Memory()
    s.q_win = m.sums[:, 0:J * K * D].rearrange("p (t d) -> p t d", d=D)
    s.edges = m.sums[:, J * K * D:J * K * (D + ROW)].rearrange("p (j k r) -> p j k r", j=J, k=K)
    at = J * K * (D + ROW)
    s.weight = m.sums[:, at:at + K]
    s.dots = m.sums[:, at + K:at + K + K * H0]
    s.loc = m.sums[:, at + K + K * H0:at + K + K * H0 + TP]
    sel = m.sel[:, :, :].rearrange("p a c -> p (a c)")
    at = 12 * P
    s.digits = sel[:, at:at + 3 * T].rearrange("p (a t) -> p a t", a=3)
    s.digit_strips = sel[0:NS, at + 3 * T:at + 3 * T + SL].bitcast(BF16).rearrange("p (a c) -> p a c", a=2)
    s.turned = m.w2[:, 0:4, :].rearrange("p (a b) (c e) -> p a (b c) e", a=2, e=P)
    s.fields_in = [m.sem(f"scores_fields_in{i}") for i in range(IT)]
    s.sources_in = m.sem("scores_sources_in")
    s.begun = m.sem("scores_begun")
    s.numbers_in = m.sem("scores_numbers_in")
    s.base_out = m.sem("scores_base_out")
    s.digits_there = m.sem("scores_digits_there")
    s.digits_turned = m.sem("scores_digits_turned")
    s.digits_in_strips = m.sem("scores_digits_in_strips")
    s.digits_stored = m.sem("scores_digits_stored")
    s.edges_free = m.sem("scores_edges_free")
    s.chosen = m.sem("scores_chosen")
    s.sel_turned = m.sem("scores_sel_turned")
    s.sel_copied = m.sem("scores_sel_copied")
    s.q_done = m.sem("scores_q_done")
    s.q_read = m.sem("scores_q_read")
    s.win_free = m.sem("scores_win_free")
    s.edges_in = [m.sem(f"scores_edges_in{j}") for j in range(J)]
    s.win_in = [m.sem(f"scores_win_in{j}") for j in range(J)]


def fields_sync(m, sp):
    s = m.sc
    sp.wait_ge(m.s.sent_all, 1)
    part = T // IT
    for i in range(IT):
        sp.dma_start(m.fields_sorted[:, i * part:(i + 1) * part, :],
                     m.sorted.rearrange("(t p) r -> p t r", p=P)[:, i * part:(i + 1) * part, 0:4]
                     ).then_inc(s.fields_in[i], 16)
    sp.wait_ge(s.digits_in_strips, 1)
    sp.dma_start(m.digit_rows.rearrange("a (s c) -> s a c", s=NS), s.digit_strips).then_inc(s.digits_stored, 16)


def fields_there(m, eng):
    for i in range(IT):
        eng.wait_ge(m.sc.fields_in[i], 16)


def fields_scalar(m, act):
    s = m.sc
    part = T // IT
    for i in range(IT):
        act.wait_ge(s.fields_in[i], 16)
        act.activation(m.src_i[:, i * part:(i + 1) * part], m.fields_sorted[:, i * part:(i + 1) * part, 0], ACT.Copy
                       ).then_inc(s.sources_in, 1)
    act.activation(m.base_i[0:1, :], m.fields_sorted[0:1, :, 1], ACT.Copy).then_inc(s.numbers_in, 1)
    act.wait_ge(s.sources_in, IT)
    act.sem_inc(s.sources_in, 1)


def fields_tensor(m, pe):
    s = m.sc
    fields_there(m, pe)
    pe.matmul(m.banks[4][:, 0:T], m.first_row, m.fields_sorted[:, :, 1], start=True, stop=True
              ).then_inc(s.base_out, 1)
    pe.wait_ge(s.digits_there, 1)
    for a in range(2):
        for b in range(FB):
            last = pe.transpose(m.banks[5 + a][0:NS, b * P:(b + 1) * P], s.digits[:, a, b::FB], m.ident)
        last.then_inc(s.digits_turned, 1)


def fields_vector(m, dve, step):
    s = m.sc
    fields_there(m, dve)
    source = m.fields_sorted[:, :, 0]
    high, low, t = s.digits[:, 0, :], s.digits[:, 1, :], s.digits[:, 2, :]
    step(dve.tensor_scalar(t, source, 1.0 / NL, -(0.5 - 0.5 / NL), ALU.mult, ALU.add))
    step(dve.tensor_scalar(t, t, 12582912.0, None, ALU.add))
    step(dve.tensor_scalar(high, t, -12582912.0, None, ALU.add))
    dve.scalar_tensor_tensor(low, high, -float(NL), source, ALU.mult, ALU.add).then_inc(s.digits_there, 1)
    dve.wait_ge(s.base_out, 1)
    step.mark(dve.memset(m.loc[:, T:TP], 0.0))
    step.mark(dve.memset(s.loc[:, T:TP], 0.0))
    first = m.banks[4][:, 0:T]
    step.mark(dve.tensor_tensor(s.loc[:, 0:T], m.fields_sorted[:, :, 1], first, ALU.subtract))
    pairs = "p (t b) -> p t b"
    step(dve.tensor_tensor(m.loc[:, 0:T].rearrange(pairs, b=2),
                           m.fields_sorted.rearrange("p (t b) f -> p t b f", b=2)[:, :, :, 1],
                           first.rearrange(pairs, b=2)[:, :, 0:1].to_broadcast([P, T // 2, 2]), ALU.subtract))
    dve.wait_ge(s.digits_turned, 2)
    step.mark(dve.tensor_copy(s.digit_strips[:, 0, :], m.banks[5][0:NS, :]))
    dve.tensor_copy(s.digit_strips[:, 1, :], m.banks[6][0:NS, :]).then_inc(s.digits_in_strips, 1)


def scores_sync(m, sp):
    s = m.sc
    sp.wait_ge(s.numbers_in, 1)
    with sp.Fori(0, IT) as it:
        for j in range(J):
            g = it * J + j
            sp.wait_ge(s.edges_free, g + 1)
            sp.dma_start(s.edges[:, j], m.sorted.rearrange("(g k p) r -> p g k r", k=K, p=P)[:, bass.ds(g, 1), :, :]
                         .rearrange("p g k r -> p (g k) r")).then_inc(s.edges_in[j], 16)
            sp.wait_ge(s.win_free, g + 1)
            first = windows(m, ENGINE.SP, g)
            for k in range(K):
                sp.dma_start(s.q_win[:, j * K + k, :], m.q_table[bass.ds(first[k], P), :]).then_inc(s.win_in[j], 16)


def windows(m, engine, g):
    _, first = m.nc.values_load_multi_w_load_instructions(
        m.base_i[0:1, bass.ds(g * K, K)], engines=[engine], min_val=0, max_val=N,
        skip_runtime_bounds_check_because="they are node numbers, 0 to N with the padding's")
    return first


def scores_scalar(m, act, step):
    s = m.sc

    def choose(g, j):
        for k in range(K):
            last = act.activation(m.sel[:, j * K + k, :], m.iota, ACT.Abs, scale=-1.0,
                                  bias=s.loc[:, bass.ds(g * K + k, 1)])
        step(last)
        group = m.sel[:, j * K:(j + 1) * K, :]
        act.activation(group, group, ACT.Relu, scale=-1.0, bias=1.0).then_inc(s.chosen, 1)

    act.wait_ge(s.begun, 1)
    choose(0, 0)
    with step.loop(IT, J) as it:
        for j in range(J):
            g = it * J + j
            choose(g + 1, (j + 1) % J)
            for half in range(2):
                act.wait_ge(s.sel_turned, 2 * g + half + 1)
                act.wait_ge(s.q_done, 4 * g)
                act.activation(s.turned[:, half], m.banks[1 + half][:, :].rearrange("p (k e) -> p k e", e=P),
                               ACT.Copy).then_inc(s.sel_copied, 1)
    act.wait_ge(s.chosen, G + 1)


def scores_tensor(m, pe):
    s = m.sc
    with pe.Fori(0, IT) as it:
        for j in range(J):
            g = it * J + j
            pe.wait_ge(s.chosen, g + 1)
            for half in range(2):
                pe.wait_ge(s.sel_copied, 2 * g)
                for k in range(4):
                    last = pe.transpose(m.banks[1 + half][:, k * P:(k + 1) * P], m.sel[:, j * K + half * 4 + k, :],
                                        m.ident)
                last.then_inc(s.sel_turned, 1)
            pe.wait_ge(s.win_in[j], 16 * K * (it + 1))
            for k in range(K):
                if k % 4 == 0:
                    pe.wait_ge(s.sel_copied, 2 * g + k // 4 + 1)
                if k % 2 == 0:
                    pe.wait_ge(s.q_read, 4 * g + k // 2 + 1)
                last = pe.matmul(m.banks[3 + k // 2][:, (k % 2) * D:(k % 2 + 1) * D], s.turned[:, k // 4, k % 4, :],
                                 s.q_win[:, j * K + k, :], start=True, stop=True)
                if k % 2:
                    last.then_inc(s.q_done, 1)


def scores_vector(m, dve, step):
    s = m.sc
    dve.sem_inc(s.win_free, J)
    dve.sem_inc(s.edges_free, J)
    dve.sem_inc(s.q_read, 4)
    dve.sem_inc(m.rows_free.sem, J)
    dve.wait_ge(s.digits_stored, 16)
    dve.sem_inc(s.begun, 1)
    with step.loop(IT, J * 3) as it:
        for j in range(J):
            g = it * J + j
            dve.wait_ge(s.edges_in[j], 16 * it + 16)
            landed(m, dve, "keys", it, j)
            rows = m.rows[:, j * K:(j + 1) * K, :]
            heads = rows.rearrange("p k (h d) -> p k h d", h=H0)
            step(dve.tensor_tensor(heads, heads, s.edges[:, j, :, 4:ROW].unsqueeze(2).to_broadcast([P, K, H0, DH0]),
                                   ALU.add))
            step.mark(dve.tensor_scalar(s.weight, s.edges[:, j, :, 2], float(DH0) ** -0.5, None, ALU.mult))
            for b in range(4):
                dve.wait_ge(s.q_done, 4 * g + b + 1)
                pair = m.rows[:, j * K + 2 * b:j * K + 2 * b + 2, :]
                dve.tensor_tensor(pair, pair, m.banks[3 + b][:, :].rearrange("p (k d) -> p k d", k=2), ALU.mult
                                  ).then_inc(s.q_read, 1)
            dve.wait_ge(s.q_read, 4 * g + 8)
            dve.sem_inc(s.win_free, 1)
            step(dve.tensor_reduce(s.dots, rows.rearrange("p k (h d) -> p (k h) d", d=DH0), AX.X, ALU.add))
            dve.tensor_tensor(m.edge[:, bass.ds(g * K * H0, K * H0)].rearrange("p (k h) -> p k h", h=H0),
                              s.dots.rearrange("p (k h) -> p k h", h=H0),
                              s.weight.unsqueeze(2).to_broadcast([P, K, H0]), ALU.mult).then_inc(m.rows_free.sem, 1)
            dve.sem_inc(s.edges_free, 1)
    dve.wait_ge(m.rows_free.sem, J + G)
    dve.wait_ge(s.chosen, G + 1)
    dve.sem_inc(m.st.scores_there.sem, 1)
    m.st.scores_there.sent += 1



def place_strips(m):
    s = m.st = Memory()
    z = m.sums

    def heads(n, count):
        return z[0:NS, n * SL:(n + count) * SL].rearrange("p (h c) -> p h c", c=SL)

    s.arrays = {H0: [heads(n * H0, H0) for n in range(3)], H1: [heads(n * H1, H1) for n in range(4)]}
    s.given = m.w2[0:NS, 4:6, :].rearrange("p a c -> p (a c)")
    s.absent = m.w2[0:NS, 6:8, :].rearrange("p a c -> p (a c)")
    s.dst = m.sel[0:NS, 8:12, :].rearrange("p a c -> p (a c)")
    sm = m.small
    s.ends = sm[0:NS, 0:8]
    s.start = sm[0:NS, 8:16]
    s.whole = sm[0:NS, 16:18]
    s.first_f = sm[0:NS, 18:20]
    s.first_i = sm[0:NS, 20:21].bitcast(I32)
    s.fill0 = sm[0:NS, 24:28]
    s.wide = sm[0:NS, 144:160].rearrange("p (w h) -> p w h", h=H0)
    s.row = m.sb("strip_row", [H0, 5, 112])
    s.ended, s.scanned = s.row[:, 0, :], s.row[:, 1, :]
    s.through = s.row[:, 2:5, :]
    s.dst_turned = Turns(m.sem("strip_dst_turned"))
    s.around_in = Turns(m.sem("strip_around_in"))
    s.around_out = Turns(m.sem("strip_around_out"))
    s.whole_out = Turns(m.sem("strip_whole_out"))
    s.whole_in = Turns(m.sem("strip_whole_in"))
    s.scores_there = Turns(m.sem("strip_scores_there"))
    s.turned = Turns(m.sem("strip_turned"))
    s.taken = Turns(m.sem("strip_taken"))
    s.ends_out = Turns(m.sem("strip_ends_out"))
    s.ends_in = Turns(m.sem("strip_ends_in"))
    s.scans_out = Turns(m.sem("strip_scans_out"))
    s.scans_in = Turns(m.sem("strip_scans_in"))
    s.shifted = Turns(m.sem("strip_shifted"))
    s.grown = Turns(m.sem("strip_grown"))
    s.attention = Turns(m.sem("strip_attention"))
    s.back = Turns(m.sem("strip_back"))
    s.back_in = Turns(m.sem("strip_back_in"))
    s.fill_in = Turns(m.sem("strip_fill_in"))
    s.first_filled = Turns(m.sem("strip_first_filled"))
    s.scattered = Turns(m.sem("strip_scattered"))


def flags_tensor(m, pe):
    s = m.st
    for bank, field in ((0, 1), (1, 3)):
        for b in range(FB):
            last = pe.transpose(m.banks[bank][0:NS, b * P:(b + 1) * P], m.fields_sorted[:, b::FB, field], m.ident)
        s.dst_turned.send(last)
    s.around_out.receive(pe)
    pe.matmul(m.banks[2][0:NS, 0:1], m.shift_on[0:NS, 0:NS], s.dst[:, SL - 1:SL], start=True, stop=True)
    s.around_in.send(pe.matmul(m.banks[2][0:NS, 1:2], m.shift_back[0:NS, 0:NS], s.dst[:, 0:1], start=True, stop=True))
    s.whole_out.receive(pe)
    pe.transpose(m.banks[3][0:H0, 0:NS], s.wide[:, 0, :], m.ident[0:NS, 0:NS])
    s.whole_in.send(pe.transpose(m.banks[3][0:H0, 128:128 + NS], s.wide[:, 1, :], m.ident[0:NS, 0:NS]))


def flags_vector(m, dve, step):
    s = m.st
    s.dst_turned.receive(dve, 2)
    step(dve.tensor_scalar(s.dst, m.banks[0][0:NS, :], 1.0, None, ALU.add))
    step.mark(dve.tensor_copy(s.given, m.banks[1][0:NS, :]))
    step.mark(dve.tensor_scalar(s.absent, m.banks[1][0:NS, :], -1.0, BIG, ALU.add, ALU.mult))
    step.mark(dve.tensor_scalar(s.first_i, s.dst[:, 0:1], -1.0, None, ALU.add))
    s.around_out.send(dve.tensor_tensor(m.goes_on[:, 1:SL], s.dst[:, 1:SL], s.dst[:, 0:SL - 1], ALU.is_equal))
    s.around_in.receive(dve)
    step.mark(dve.tensor_tensor(m.has_next[:, 0:SL - 1], s.dst[:, 1:SL], s.dst[:, 0:SL - 1], ALU.is_equal))
    step.mark(dve.tensor_tensor(m.goes_on[:, 0:1], s.dst[:, 0:1], m.banks[2][0:NS, 0:1], ALU.is_equal))
    step(dve.tensor_tensor(m.has_next[:, SL - 1:SL], s.dst[:, SL - 1:SL], m.banks[2][0:NS, 1:2], ALU.is_equal))
    step.mark(dve.tensor_scalar(m.at_start, m.goes_on, -1.0, BIG, ALU.add, ALU.mult))
    step.mark(dve.tensor_reduce(s.whole[:, 0:1], m.goes_on, AX.X, ALU.min))
    step(dve.tensor_reduce(s.whole[:, 1:2], m.has_next, AX.X, ALU.min))
    s.whole_out.send(dve.tensor_copy(s.wide, s.whole.unsqueeze(2).to_broadcast([NS, 2, H0])))
    s.whole_in.receive(dve)
    step.mark(dve.tensor_scalar(s.through[:, 0, 0:NS], m.banks[3][0:H0, 0:NS], -1.0, BIG, ALU.add, ALU.mult))
    step.mark(dve.tensor_copy(s.through[:, 1, 0:NS], m.banks[3][0:H0, 0:NS]))
    step(dve.tensor_copy(s.through[:, 2, 0:NS], m.banks[3][0:H0, 128:128 + NS]))


def strips_tensor(m, pe, heads):
    s = m.st
    s.scores_there.receive(pe)
    scores = m.edge[:, 0:T * heads].rearrange("p (t h) -> p t h", h=heads)
    for h in range(heads):
        for b in range(FB):
            last = pe.transpose(m.banks[h][0:NS, b * P:(b + 1) * P], scores[:, b::FB, h], m.ident)
        s.turned.send(last)
    for n in range(4):
        s.ends_out.receive(pe)
        s.ends_in.send(pe.transpose(m.banks[0][0:heads, 0:NS], s.ends[:, 0:heads], m.ident[0:NS, 0:NS]))
        s.scans_out.receive(pe)
        moved = s.scanned[0:heads, 0:NS] if n % 2 == 0 else s.scanned[0:heads, 1:NS + 1]
        s.scans_in.send(pe.transpose(m.banks[1][0:NS, 0:heads], moved, m.ident[0:heads, 0:heads]))
    x = s.arrays[heads][0]
    for h in range(heads):
        s.attention.receive(pe)
        for b in range(FB):
            last = pe.transpose(m.banks[h][:, b * NS:(b + 1) * NS], x[:, h, b * P:(b + 1) * P], m.ident[0:NS, 0:NS])
        s.back.send(last)


def strips_scalar(m, act, heads):
    s = m.st
    x = s.arrays[heads][0]
    for h in range(heads):
        s.turned.receive(act)
        s.taken.send(act.activation(x[:, h, :], m.banks[h][0:NS, :], ACT.Copy))
    for h in range(heads):
        s.shifted.receive(act)
        s.grown.send(act.activation(x[:, h], x[:, h], ACT.Exp))
    edges = m.edge[:, 0:T * heads].rearrange("p (s b h) -> p h b s", b=FB, h=heads)
    for h in range(heads):
        s.back.receive(act)
        s.back_in.send(act.activation(edges[:, h], m.banks[h][:, 0:FB * NS].rearrange("p (b s) -> p b s", b=FB),
                                      ACT.Copy))


def strips_vector(m, dve, step, heads, slope=None, least=None, more=None):
    s = m.st
    x, on, back = s.arrays[heads][0:3]
    wide = [NS, heads, SL]

    def each(flag):
        return flag.unsqueeze(1).to_broadcast(wide)

    def run(out, x, flag, ops, start, rev=False):
        way = slice(None, None, -1) if rev else slice(None)
        for h in range(heads):
            first = start if isinstance(start, float) else start[:, h:h + 1]
            step.mark(dve.tensor_tensor_scan(out[:, h, way], flag[:, way], x[:, h, way], first, *ops))
        step.wait()

    def starts(values, through, ops, zero, rev=False):
        s.ends_out.send(dve.tensor_copy(s.ends[:, 0:heads], values))
        s.ends_in.receive(dve)
        step(dve.tensor_copy(s.ended[0:heads, 0:NS], m.banks[0][0:heads, 0:NS]))
        through = through[0:heads, 0:NS]
        if rev:
            step(dve.memset(s.scanned[0:heads, NS:NS + 1], zero))
            s.scans_out.send(dve.tensor_tensor_scan(s.scanned[0:heads, 0:NS][:, ::-1], through[:, ::-1],
                                                    s.ended[0:heads, 0:NS][:, ::-1], zero, *ops))
        else:
            step(dve.memset(s.scanned[0:heads, 0:1], zero))
            s.scans_out.send(dve.tensor_tensor_scan(s.scanned[0:heads, 1:NS + 1], through,
                                                    s.ended[0:heads, 0:NS], zero, *ops))
        s.scans_in.receive(dve)
        step(dve.tensor_copy(s.start[:, 0:heads], m.banks[1][0:NS, 0:heads]))
        return s.start

    def over_runs(x, flag, ops, through, zero):
        run(on, x, flag, ops, zero)
        run(on, x, flag, ops, starts(on[:, :, SL - 1], through, ops, zero))
        step(dve.scalar_tensor_tensor(on, each(m.has_next), 0.0, on, ALU.is_equal, ALU.mult))
        ops = (ALU.mult, ALU.add)
        run(back, on, m.has_next, ops, 0.0, rev=True)
        run(back, on, m.has_next, ops, starts(back[:, :, 0], s.through[:, 2], ops, 0.0, rev=True), rev=True)

    if heads == H0:
        s.taken.receive(dve, heads)
        step(dve.tensor_tensor(x, x, each(s.given), ALU.mult))
        step(dve.tensor_tensor(x, x, each(s.absent), ALU.add))
    else:
        s.fill_in.receive(dve, 16)
        s.first_filled.receive(dve, 16)
        filled = s.arrays[heads][3].rearrange("p h c -> p (h c)").rearrange("p (c h) -> p h c", h=heads)
        run(on, filled, m.goes_on, (ALU.mult, ALU.add), s.fill0)
        s.taken.receive(dve, heads)
        step(dve.tensor_tensor(x, x, on, ALU.add))
        step(dve.scalar_tensor_tensor(x, x, slope, x, ALU.mult, ALU.max))
    over_runs(x, m.at_start, (ALU.add, ALU.max), s.through[:, 0], -BIG)
    for h in range(heads):
        s.shifted.send(dve.tensor_tensor(x[:, h], x[:, h], back[:, h], ALU.subtract))
    s.grown.receive(dve, heads)
    if heads == H0:
        step(dve.tensor_tensor(x, x, each(s.given), ALU.mult))
    over_runs(x, m.goes_on, (ALU.mult, ALU.add), s.through[:, 1], 0.0)
    if least is not None:
        step(dve.tensor_scalar(back, back, least, None, ALU.max))
    if more is not None:
        step(dve.tensor_scalar(back, back, more, None, ALU.add))
    for h in range(heads):
        step(dve.reciprocal(back[:, h], back[:, h]))
        s.attention.send(dve.tensor_tensor(x[:, h], x[:, h], back[:, h], ALU.mult))



AGGREGATES = ["values"] + [f"rows{i}" for i in range(4)]


def plan_aggregates(m):
    a = m.ag = Memory()
    a.chosen = Signal(m.sem("aggregate_chosen"))
    a.weighted = Signal(m.sem("aggregate_weighted"))
    a.added = Signal(m.sem("aggregate_added"))
    a.products = Signal(m.sem("aggregate_products"))
    a.added.total = 4
    for stage in AGGREGATES:
        a.chosen.plan(stage, G)
        a.weighted.plan(stage, G)
        a.added.plan(stage, 4 * G)
        a.products.plan(stage, 4 * G)
    a.begun = Turns(m.sem("aggregate_begun"))
    w = m.w1[:, :, :].rearrange("p a c -> p (a c)")
    a.loc = w[:, W2:W2 + T]
    a.iota = w[:, 1024:1024 + W2]
    wide = K * W2
    sel = m.sel[:, :, :].rearrange("p a c -> p (a c)")
    rest = 2 * ACOLS
    assert 2 * wide <= J * K * P and rest + 3 * wide <= SUMS
    a.sel = [(sel[:, j * wide:(j + 1) * wide] if j < 2 else m.sums[:, rest + (j - 2) * wide:rest + (j - 1) * wide])
             .rearrange("p (k c) -> p k c", c=W2) for j in range(J)]


def numbers_vector(m, dve, step):
    a = m.ag
    step(dve.tensor_copy(a.loc, m.loc[:, 0:T]))
    step(dve.tensor_copy(a.iota[:, 0:P], m.iota))
    a.begun.send(dve.tensor_scalar(a.iota[:, P:W2], m.iota, float(P), None, ALU.add))


def aggregate_vector(m, dve, step, stage, heads):
    a = m.ag
    bw, bp, ba = a.weighted.base[stage], a.products.base[stage], a.added.base[stage]
    m.st.back_in.receive(dve, heads)
    edges = m.edge[:, 0:T * heads].rearrange("p (t h) -> p t h", h=heads)
    if stage == AGGREGATES[0]:
        dve.sem_inc(a.added.sem, 4)

    def weigh(it, j):
        g = it * J + j
        landed(m, dve, stage, it, j)
        rows = m.rows[:, j * K:(j + 1) * K, :].rearrange("p k (h d) -> p k h d", h=heads)
        dve.tensor_tensor(rows, rows, edges[:, bass.ds(g * K, K), :].unsqueeze(3)
                          .to_broadcast([P, K, heads, D // heads]), ALU.mult).then_inc(a.weighted.sem, 1)

    def add(it, j):
        g = it * J + j
        first = windows(m, ENGINE.DVE, g)
        for b in range(K // 2):
            dve.wait_ge(a.products.sem, bp + 4 * g + b + 1)
            w = m.acc[:, :, bass.ds(first[2 * b], W2)]
            dve.tensor_tensor(w, w, m.banks[b][:, :].rearrange("p (f c) -> p f c", f=2), ALU.add
                              ).then_inc(a.added.sem, 1)
            dve.wait_ge(a.added.sem, ba + 4 * g + b + 1)

    weigh(0, 0)
    step(dve.memset(m.sums[:, 0:2 * ACOLS], 0.0))
    with dve.Fori(0, IT - 1) as it:
        for j in range(J):
            weigh(it + (j + 1) // J, (j + 1) % J)
            add(it, j)
    for j in range(J):
        if j + 1 < J:
            weigh(IT - 1, j + 1)
        add(IT - 1, j)


def aggregate_scalar(m, act, step, stage):
    a = m.ag
    a.begun.receive(act)
    free = m.rows_free.base[stage] - J
    with step.loop(IT, J) as it:
        for j in range(J):
            g = it * J + j
            act.wait_ge(m.rows_free.sem, free + g + 1)
            for k in range(K):
                last = act.activation(a.sel[j][:, k, :], a.iota, ACT.Abs, scale=-1.0,
                                      bias=a.loc[:, bass.ds(g * K + k, 1)])
            step(last)
            act.activation(a.sel[j], a.sel[j], ACT.Relu, scale=-1.0, bias=1.0).then_inc(a.chosen.sem, 1)


def aggregate_tensor(m, pe, stage):
    a = m.ag
    bc, bw, bp, ba = (x.base[stage] for x in (a.chosen, a.weighted, a.products, a.added))
    with pe.Fori(0, IT) as it:
        for j in range(J):
            g = it * J + j
            pe.wait_ge(a.chosen.sem, bc + g + 1)
            pe.wait_ge(a.weighted.sem, bw + g + 1)
            for b in range(K // 2):
                pe.wait_ge(a.added.sem, ba - 4 + 4 * g + b + 1)
                for f in range(2):
                    for i in range(2):
                        k = 2 * b + i
                        last = pe.matmul(m.banks[b][:, f * W2:(f + 1) * W2], m.rows[:, j * K + k, f * P:(f + 1) * P],
                                         a.sel[j][:, k, :], start=i == 0, stop=i == 1)
                last.then_inc(a.products.sem, 1)
            pe.wait_ge(a.products.sem, bp + 4 * g + 4)
            pe.sem_inc(m.rows_free.sem, 1)



class Marks:

    def __init__(self, sem, plan):
        self.sem, self.plan, self.at, self.n = sem, plan, {}, 0
        total = 0
        for label, count in plan:
            total += count
            self.at[label] = total

    def reach(self, label, ins):
        assert self.plan[self.n][0] == label, (self.plan[self.n], label)
        self.n += 1
        return ins.then_inc(self.sem, 1)

    def wait(self, eng, label):
        eng.wait_ge(self.sem, self.at[label])


def norm_labels(stage):
    return [(stage + " variance", 1), (stage + " norm", 1)]


LAYERS = range(3)
VECTOR_MARKS = ([("zeros", 1)] + norm_labels("A") + norm_labels("A2") + [("B sum", 1), ("B rows", NL)]
                + norm_labels("C") + [("C rows", NL)]
                + norm_labels("D") + [("D ratio", 1), ("D factor", 1), ("D product", NL), ("D2 square", 1),
                                      ("D sum", 1), ("D3 ratio", 1), ("D rows", 1), ("D terms", 1)]
                + [("F sum", 1), ("F product", NL), ("F relu", 1), ("F rows", NL)]
                + [("G turns", 1)] + norm_labels("G") + [("G weights", 1), ("G rows", NL)] + norm_labels("H")
                + [(f"H{i} {what}", n) for i in LAYERS
                   for what, n in (("sum" if i else "weights", 1), ("rows", NL))]
                + [("J sum", 1), ("J rows", NL)])
SCALAR_MARKS = ([("A deviation", 1), ("A rows", NL), ("A2 deviation", 1), ("C deviation", 1)]
                + [("D deviation", 1), ("D rows", NL), ("D squares", NL), ("D root", 1), ("D log", 1),
                   ("D2 squares", NL), ("D2 root", 1), ("D2 tanh", 1), ("D3 squares", NL), ("D3 root", 1),
                   ("D3 log", 1)]
                + [("F squares", NL), ("F root", 1), ("F tanh", 1)]
                + [("G deviation", 1), ("H deviation", 1), ("H1 sum", 1), ("H2 sum", 1), ("J sum", 1)])
SYNC_MARKS = ([("inputs", 16 * 6), ("zeros", 32), ("B weights", 48), ("C weights", 32), ("D weights", 64),
               ("D flat", 32), ("D rows", 128), ("D table", 32), ("D tables", 16),
               ("F flat", 128), ("F rows", 32)]
              + [(f"H{i} {what}", n) for i in LAYERS for what, n in (("weights", 32), ("tables", 48))]
              )
TURNING = ["A", "C", "D", "G", "H0"]
PASSES = ["A", "B", "C", "D", "F", "G", "H0", "H1", "H2", "J"]


def place_nodes(m):
    n = m.n = Memory()
    r = m.rows[:, :, :].rearrange("p t d -> p (t d)")
    n.z = r[0:NP, 0:J * D].rearrange("p (j d) -> p j d", j=J)
    n.lhs = r[:, 1280:1280 + J * 2 * NP].rearrange("p (j f n) -> p j f n", j=J, f=2)
    n.lhs_c = r[:, 1280:1280 + 2 * J * NP].rearrange("p (f c) -> p f c", f=2)
    n.out = r[0:NP, 2560:2560 + J * 3 * D].rearrange("p (j d) -> p j d", j=J)
    n.spare = r[:, 6400:10240]
    n.hidden = m.sel[:, :, :].rearrange("p a b -> p (a b)")[:, 0:FF // P * J * NP].rearrange(
        "p (c n) -> p c n", c=FF // P)
    n.squares = m.sums[0:NP, 0:NL * D].rearrange("p (l d) -> p l d", l=NL)
    e = m.edge
    n.stats = e[0:NP, 0:6 * NL].rearrange("p (l s) -> p l s", s=6)
    n.wide = [e[0:NP, 150 + (NL + 1) * i:150 + (NL + 1) * (i + 1)] for i in range(16)]
    n.v = [v[:, 0:NL] for v in n.wide]
    n.mean, n.rs, n.nb, n.sq = n.v[0:4]
    n.cols = m.sb("cols", [P, 30])
    n.g1, n.b1, n.g2, n.b2 = (n.cols[:, 2 * i:2 * i + 2] for i in range(4))
    n.hidden_bias = n.cols[:, 8:16]
    n.b3 = [n.cols[:, 18 + 2 * i:20 + 2 * i] for i in LAYERS]
    n.alpha, n.beta = n.cols[0:NP, 24:25], n.cols[0:NP, 25:26]
    n.qkv = m.w1[:, :, 0:3 * D]
    n.qkv_bias = m.w2[0:NP, 0:3, :].rearrange("p a d -> p (a d)")
    n.wo = n.spare[:, 0:2 * D].rearrange("p (f d) -> p f d", f=2)
    n.bo = n.spare[0:NP, 2 * D:3 * D]
    n.b_ff = n.spare[0:NP, 3 * D:4 * D]
    w = m.w2[:, :, :].rearrange("p a d -> p (a d)")
    n.w = w[:, 0:2 * (D + 2 * H1)].rearrange("p (f d) -> p f d", f=2)
    n.att = w[:, 528:528 + 2 * D].rearrange("p (a d) -> p a d", a=2)
    n.b_lin = w[0:NP, 1040:1040 + D]
    n.b_conv = w[0:NP, 1296:1296 + D]
    n.scratch = w[:, 1296:1296 + 2 * D].rearrange("p (f d) -> p f d", f=2)
    m.terms = m.w1[0:NP, 0, 0:NL * 2 * H1].rearrange("p (a l h) -> p a l h", a=2, l=NL)
    n.vector = Marks(m.sem("vector_reached"), VECTOR_MARKS)
    n.scalar = Marks(m.sem("scalar_reached"), SCALAR_MARKS)
    n.sync = Marks(m.sem("loaded"), SYNC_MARKS)
    n.z_in = Signal(m.sem("node_z_in"))
    n.turned = Signal(m.sem("node_turned"))
    n.lhs_in = Signal(m.sem("node_lhs_in"))
    n.out_ready = Signal(m.sem("node_out_ready"))
    n.out_read = Signal(m.sem("node_out_read"))
    n.turned.total = n.out_ready.total = n.out_read.total = J
    for p in TURNING:
        if p != "C":
            n.z_in.plan(p, NL)
            n.turned.plan(p, NL)
    for p in PASSES:
        if p != "C":
            for signal in (n.lhs_in, n.out_ready, n.out_read):
                signal.plan(p, NL)
    n.stored = [m.sem(f"tables_stored{j}") for j in range(J)]
    n.output_stored = m.sem("output_stored")
    n.ff_z_in = m.sem("ff_z_in")
    n.ff_turned = m.sem("ff_turned")
    n.ff_lhs_in = m.sem("ff_lhs_in")
    n.ff_hidden_out = m.sem("ff_hidden_out")
    n.ff_hidden_read = m.sem("ff_hidden_read")
    n.ff_out_ready = m.sem("ff_out_ready")
    n.ff_out_read = m.sem("ff_out_read")


def done(eng, signal, p, l):
    eng.wait_ge(signal.sem, signal.base[p] + l + 1)


def free(eng, signal, p, l):
    eng.wait_ge(signal.sem, signal.base[p] - J + l + 1)


def pass_scalar(m, act, p, z, lhs):
    n = m.n
    with act.Fori(0, NL // J) as it:
        def first(k):
            l = it * J + k
            free(act, n.turned, p, l)
            z(l, k).then_inc(n.z_in.sem, 1)

        def second(k):
            l = it * J + k
            done(act, n.turned, p, l)
            free(act, n.out_ready, p, l)
            lhs(l, k).then_inc(n.lhs_in.sem, 1)

        for k in range(J):
            first(k)
            if k:
                second(k - 1)
        second(J - 1)


def turn_back(m, act, k, scale=None, bias=None):
    n = m.n
    for f in range(2):
        bank = m.banks[k][:, f * P:f * P + NP]
        if scale is None:
            last = act.activation(n.lhs[:, k, f, :], bank, ACT.Copy)
        else:
            last = act.activation(n.lhs[:, k, f, :], bank, ACT.Identity, bias=bias[:, f:f + 1],
                                  scale=scale[:, f:f + 1])
    return last


def sums_scalar(m, act, p):
    n = m.n
    columns = m.acc[:, :, 0:N].rearrange("p f (n l) -> p l f n", l=NL)
    with act.Fori(0, NL // J) as it:
        for k in range(J):
            l = it * J + k
            free(act, n.out_ready, p, l)
            act.activation(n.lhs[:, k, :, :], columns[:, bass.ds(l, 1)].rearrange("p o f n -> p (o f) n"),
                           ACT.Copy).then_inc(n.lhs_in.sem, 1)


def pass_tensor(m, pe, p, product):
    n = m.n
    turning = p in TURNING
    with pe.Fori(0, NL // J) as it:
        def turn(k):
            l = it * J + k
            done(pe, n.z_in, p, l)
            free(pe, n.out_read, p, l)
            for f in range(2):
                last = pe.transpose(m.banks[k][:, f * P:f * P + NP], n.z[:, k, f * P:(f + 1) * P], m.ident[0:NP, 0:NP])
            last.then_inc(n.turned.sem, 1)

        def multiply(k):
            l = it * J + k
            done(pe, n.lhs_in, p, l)
            free(pe, n.out_read, p, l + J - 2)
            product(k).then_inc(n.out_ready.sem, 1)

        for k in range(J):
            if turning:
                turn(k)
                if k:
                    multiply(k - 1)
            else:
                multiply(k)
        if turning:
            multiply(J - 1)


def product_of(m, pe, weights, width):
    def product(k):
        for first in range(0, width, 512):
            bank = m.banks[k] if not first else m.banks[J + k % 3]
            end = min(first + 512, width)
            for f in range(2):
                last = pe.matmul(bank[0:NP, 0:end - first], m.n.lhs[:, k, f, :], weights[:, f, first:end],
                                 start=f == 0, stop=f == 1)
        return last
    return product


def rows_of(m, pe):
    def product(k):
        for f in range(2):
            last = pe.transpose(m.banks[k][0:NP, f * P:(f + 1) * P], m.n.lhs[:, k, f, :], m.ident)
        return last
    return product


def norm_vector(m, dve, step, stage, rows):
    n = m.n
    with step.loop(NL // J, J) as it:
        for k in range(J):
            l = it * J + k
            step.mark(dve.bn_stats(n.stats[:, bass.ds(l, 1), :].rearrange("p l s -> p (l s)"),
                                   rows[0:NP, bass.ds(l, 1), :].rearrange("p l d -> p (l d)")))
    step.wait()
    st = n.stats
    step.mark(dve.tensor_tensor(n.v[4], st[:, :, 1], st[:, :, 4], ALU.add))
    step.mark(dve.tensor_tensor(n.v[5], st[:, :, 1], st[:, :, 4], ALU.subtract))
    step(dve.tensor_tensor(n.v[6], st[:, :, 2], st[:, :, 5], ALU.add))
    step.mark(dve.tensor_scalar(n.mean, n.v[4], 0.5, None, ALU.mult))
    step.mark(dve.tensor_tensor(n.v[7], n.v[5], n.v[5], ALU.mult))
    step(dve.tensor_scalar(n.v[8], n.v[6], 1.0 / D, LN_EPS, ALU.mult, ALU.add))
    n.vector.reach(stage + " variance", dve.scalar_tensor_tensor(n.v[9], n.v[7], 0.25, n.v[8], ALU.mult, ALU.add))
    n.scalar.wait(dve, stage + " deviation")
    step(dve.reciprocal(n.rs, n.v[10]))
    n.vector.reach(stage + " norm", dve.scalar_tensor_tensor(n.nb, n.mean, -1.0, n.rs, ALU.mult, ALU.mult))


def norm_scalar(m, act, stage):
    n = m.n
    n.vector.wait(act, stage + " variance")
    n.scalar.reach(stage + " deviation", act.activation(n.v[10], n.v[9], ACT.Sqrt))
    n.vector.wait(act, stage + " norm")


def row(rows, l):
    return rows[0:NP, bass.ds(l, 1), :].rearrange("p l d -> p (l d)")


def normed(m, act, rows, func):
    n = m.n
    return lambda l, k: act.activation(n.z[:, k, :], row(rows, l), func, bias=n.nb[:, bass.ds(l, 1)],
                                       scale=n.rs[:, bass.ds(l, 1)])


def each_node(eng, signal, body):
    with eng.Fori(0, NL // J) as it:
        for k in range(J):
            body(it * J + k, k).then_inc(signal.sem, 1)
    signal.n += 1



def a_sync(m, io, sp):
    n = m.n
    for out, in_ in two_parts(m.x[0:NP, :, :], io["x"].rearrange("(p l) d -> p l d", l=NL)):
        sp.dma_start(out, in_).then_inc(n.sync.sem, 16)
    sp.dma_start(n.cols[:, :], io["cols"]).then_inc(n.sync.sem, 16)
    sp.dma_start(n.qkv, io["qkv"]).then_inc(n.sync.sem, 16)
    sp.dma_start(n.qkv_bias, io["qkv_bias"][0:1, :].to_broadcast([NP, 3 * D])).then_inc(n.sync.sem, 16)
    sp.dma_start(m.consts[:, :, :], io["consts"]).then_inc(n.sync.sem, 16)
    n.vector.wait(sp, "zeros")
    n.sync.wait(sp, "inputs")
    zeros = m.zeros
    sp.dma_start(m.q_table[N:N + P, :], zeros[:, 0:D]).then_inc(n.sync.sem, 16)
    sp.dma_start(m.at_starts.rearrange("(s c) h -> s (c h)", s=NS), zeros[0:NS, :]).then_inc(n.sync.sem, 16)
    n.sync.wait(sp, "zeros")
    sort_inputs(m, io, sp)
    with sp.Fori(0, NL // J) as it:
        for k in range(J):
            l = it * J + k
            done(sp, n.out_read, "A", l)
            for i, table in enumerate((m.q_table, m.k_table, m.row_table)):
                sp.dma_start(node_rows(table, D)[:, bass.ds(l, 1), :].rearrange("p l d -> p (l d)"),
                             n.out[:, k, i * D:(i + 1) * D]).then_inc(n.stored[k], 16)
    for k in range(J):
        sp.wait_ge(n.stored[k], 48 * NL // J)
    n.sync.n = 2


def a_vector(m, dve, step):
    n = m.n
    dve.sem_inc(n.out_read.sem, J)
    n.vector.reach("zeros", dve.memset(m.zeros, 0.0))
    n.sync.wait(dve, "inputs")
    norm_vector(m, dve, step, "A", m.x)
    n.scalar.wait(dve, "A rows")
    norm_vector(m, dve, step, "A2", m.h)
    with dve.Fori(0, NL // J) as it:
        for k in range(J):
            l = it * J + k
            done(dve, n.out_ready, "A", l)
            dve.wait_ge(n.stored[k], 48 * it)
            dve.tensor_tensor(n.out[:, k, 0:2 * D], m.banks[k][0:NP, :], n.qkv_bias[:, 0:2 * D], ALU.add)
            dve.tensor_tensor(n.out[:, k, 2 * D:3 * D], m.banks[J + k % 3][0:NP, 0:D], n.qkv_bias[:, 2 * D:3 * D],
                              ALU.add).then_inc(n.out_read.sem, 1)


def a_scalar(m, act):
    n = m.n
    norm_scalar(m, act, "A")
    each_node(act, n.scalar, lambda l, k: act.activation(row(m.h, l), row(m.x, l), ACT.Relu,
                                                         bias=n.nb[:, bass.ds(l, 1)], scale=n.rs[:, bass.ds(l, 1)]))
    norm_scalar(m, act, "A2")
    pass_scalar(m, act, "A", normed(m, act, m.h, ACT.Identity), lambda l, k: turn_back(m, act, k, n.g1, n.b1))


def a_tensor(m, pe):
    n = m.n
    pe.sem_inc(n.turned.sem, J)
    pe.sem_inc(n.out_ready.sem, J)
    n.sync.wait(pe, "inputs")
    pass_tensor(m, pe, "A", product_of(m, pe, n.qkv, 3 * D))



MOST = NP // 16 * 16


def two_parts(out, in_):
    return [(out[0:MOST], in_[0:MOST]), (out[MOST:NP], in_[MOST:NP])]


def load(m, sp, parts):
    m.n.sync.wait(sp, m.n.sync.plan[m.n.sync.n - 1][0])
    for out, in_ in parts:
        sp.dma_start(out, in_).then_inc(m.n.sync.sem, 16)
    m.n.sync.n += 1


def spread(source, rows, width):
    return source[0:1, :].to_broadcast([rows, width])


def b_sync(m, io, sp):
    n = m.n
    n.vector.wait(sp, "B sum")
    load(m, sp, [(n.wo, io["wo"]), (n.bo, spread(io["bo"], NP, D)), (n.b_ff, spread(io["b_ff"], NP, D))])
    load(m, sp, [(m.w1[:, :, :], io["w1"]), (m.w2[:, :, :], io["w2"])])


def sums_there(m, dve, label):
    n = m.n
    assert n.vector.plan[n.vector.n][0] == label
    dve.sem_inc(n.vector.sem, 1)
    n.vector.n += 1


def b_vector(m, dve, step):
    n = m.n
    sums_there(m, dve, "B sum")
    n.sync.wait(dve, "B weights")
    with step.loop(NL // J, J) as it:
        for k in range(J):
            l = it * J + k
            done(dve, n.out_ready, "B", l)
            step(dve.tensor_tensor(n.out[:, k, 0:D], m.banks[k][0:NP, 0:D], n.bo, ALU.add))
            dve.sem_inc(n.out_read.sem, 1)
            dve.scalar_tensor_tensor(row(m.h, l), n.out[:, k, 0:D], n.alpha, row(m.h, l), ALU.mult, ALU.add
                                     ).then_inc(n.vector.sem, 1)
    n.vector.n += 1
    n.vector.wait(dve, "B rows")


def b_scalar(m, act):
    m.n.vector.wait(act, "B sum")
    sums_scalar(m, act, "B")


def b_tensor(m, pe):
    m.n.sync.wait(pe, "B weights")
    pass_tensor(m, pe, "B", product_of(m, pe, m.n.wo, D))



def c_vector(m, dve, step):
    n = m.n
    norm_vector(m, dve, step, "C", m.h)
    with step.loop(NL // J, 2 * J) as it:
        for k in range(J):
            l = it * J + k
            dve.wait_ge(n.ff_out_ready, l + 1)
            step(dve.tensor_tensor(n.out[:, k, 0:D], m.banks[k][0:NP, 0:D], n.b_ff, ALU.add))
            dve.sem_inc(n.ff_out_read, 1)
            step(dve.scalar_tensor_tensor(n.out[:, k, D:2 * D], n.out[:, k, 0:D], n.beta, row(m.h, l),
                                          ALU.mult, ALU.add))
            dve.tensor_tensor(row(m.x, l), n.out[:, k, D:2 * D], row(m.x, l), ALU.add).then_inc(n.vector.sem, 1)
    n.vector.n += 1
    n.vector.wait(dve, "C rows")


HIDDEN = FF // P
CUTS = [(0, 313), (313, J * NP)]


def c_scalar(m, act):
    n = m.n
    norm_scalar(m, act, "C")
    z = normed(m, act, m.h, ACT.Identity)

    def rows(it):
        for k in range(J):
            act.wait_ge(n.ff_turned, J * it)
            z(it * J + k, k).then_inc(n.ff_z_in, 1)

    def columns(it):
        for k in range(J):
            act.wait_ge(n.ff_turned, J * it + k + 1)
            act.wait_ge(n.ff_hidden_out, 2 * HIDDEN * it)
            for f in range(2):
                last = act.activation(n.lhs_c[:, f, k * NP:(k + 1) * NP], m.banks[k][:, f * P:f * P + NP],
                                      ACT.Identity, bias=n.b2[:, f:f + 1], scale=n.g2[:, f:f + 1])
            last.then_inc(n.ff_lhs_in, 1)

    def units(it):
        for i in range(2 * HIDDEN):
            c, (a, b) = i // 2, CUTS[i % 2]
            act.wait_ge(n.ff_hidden_out, 2 * HIDDEN * it + i + 1)
            act.wait_ge(n.ff_out_ready, J * it)
            act.activation(n.hidden[:, c, a:b], m.banks[5 + i % 3][:, 0:b - a], ACT.Gelu,
                           bias=n.hidden_bias[:, c:c + 1]).then_inc(n.ff_hidden_read, 1)

    rows(0)
    columns(0)
    with act.Fori(0, NL // J - 1) as it:
        rows(it + 1)
        units(it)
        columns(it + 1)
    units(NL // J - 1)


def c_tensor(m, pe):
    n = m.n
    n.sync.wait(pe, "C weights")

    def turn(it, ahead):
        for k in range(J):
            pe.wait_ge(n.ff_z_in, J * it + k + 1)
            if ahead:
                pe.wait_ge(n.ff_out_read, J * (it - 1))
            for f in range(2):
                last = pe.transpose(m.banks[k][:, f * P:f * P + NP], n.z[:, k, f * P:(f + 1) * P],
                                    m.ident[0:NP, 0:NP])
            last.then_inc(n.ff_turned, 1)

    def to_hidden(it):
        for i in range(2 * HIDDEN):
            c, (a, b) = i // 2, CUTS[i % 2]
            if i == 0:
                pe.wait_ge(n.ff_lhs_in, J * it + J)
                pe.wait_ge(n.ff_hidden_read, 2 * HIDDEN * it)
            elif i >= 3:
                pe.wait_ge(n.ff_hidden_read, 2 * HIDDEN * it + i - 2)
            for f in range(2):
                last = pe.matmul(m.banks[5 + i % 3][:, 0:b - a], m.w1[:, f, c * P:(c + 1) * P], n.lhs_c[:, f, a:b],
                                 start=f == 0, stop=f == 1)
            last.then_inc(n.ff_hidden_out, 1)

    def from_hidden(it, ahead):
        pe.wait_ge(n.ff_hidden_read, 2 * HIDDEN * it + 2 * HIDDEN)
        pe.wait_ge(n.ff_out_read, J * it)
        for k in range(J):
            if ahead:
                pe.wait_ge(n.ff_lhs_in, J * it + J + k + 1)
            for c in range(HIDDEN):
                last = pe.matmul(m.banks[k][0:NP, 0:D], n.hidden[:, c, k * NP:(k + 1) * NP], m.w2[:, c, :],
                                 start=c == 0, stop=c == HIDDEN - 1)
            last.then_inc(n.ff_out_ready, 1)

    turn(0, False)
    with pe.Fori(0, NL // J - 1) as it:
        to_hidden(it)
        turn(it + 1, True)
        from_hidden(it, True)
    to_hidden(NL // J - 1)
    from_hidden(NL // J - 1, False)



MIN_NORM = 1e-15
EDGE_OF_BALL = 1.0 - 0.004
SMALL = 0.1


def squares_scalar(m, act, stage, width=NL):
    n = m.n
    each_node(act, n.scalar, lambda l, k: act.activation(row(n.squares, l), row(m.h, l), ACT.Square,
                                                         accum_out=n.sq[:, bass.ds(l, 1)]))
    n.scalar.wait(act, stage + " squares")
    if width > NL:
        n.vector.wait(act, stage + " square")
    n.scalar.reach(stage + " root", act.activation(n.wide[4][:, 0:width], n.wide[3][:, 0:width], ACT.Sqrt))


def atanh_ratio_vector(m, dve, step, stage, cap, label):
    n, v = m.n, m.n.v
    n.scalar.wait(dve, stage + " root")
    step(dve.tensor_scalar(v[6], v[4], MIN_NORM, None, ALU.max))
    step(dve.tensor_scalar(v[7], v[6], cap, None, ALU.min))
    step.mark(dve.tensor_scalar(v[8], v[7], 1.0, None, ALU.add))
    step(dve.tensor_scalar(v[9], v[7], -1.0, 1.0, ALU.mult, ALU.add))
    step(dve.reciprocal(v[9], v[9]))
    n.vector.reach(stage + " ratio", dve.tensor_tensor(v[10], v[8], v[9], ALU.mult))
    step(dve.tensor_tensor(v[11], v[7], v[7], ALU.mult))
    step(dve.tensor_scalar(v[12], v[11], 1.0 / 7, 1.0 / 5, ALU.mult, ALU.add))
    step(dve.tensor_tensor(v[12], v[12], v[11], ALU.mult))
    step(dve.tensor_scalar(v[12], v[12], 1.0 / 3, None, ALU.add))
    step(dve.tensor_tensor(v[12], v[12], v[11], ALU.mult))
    step(dve.tensor_scalar(v[12], v[12], 1.0, None, ALU.add))
    step(dve.tensor_tensor(v[12], v[12], v[7], ALU.mult))
    n.scalar.wait(dve, stage + " log")
    step(dve.scalar_tensor_tensor(v[13], v[5], 0.5, v[12], ALU.mult, ALU.subtract))
    step(dve.tensor_scalar(v[8], v[7], SMALL, None, ALU.is_ge))
    step(dve.tensor_tensor(v[13], v[13], v[8], ALU.mult))
    step(dve.tensor_tensor(v[13], v[13], v[12], ALU.add))
    step(dve.reciprocal(v[6], v[6]))
    last = dve.tensor_tensor(v[14], v[13], v[6], ALU.mult)
    if label:
        n.vector.reach(label, last)
    else:
        step(last)


def atanh_scalar(m, act, stage):
    n = m.n
    squares_scalar(m, act, stage)
    n.vector.wait(act, stage + " ratio")
    n.scalar.reach(stage + " log", act.activation(n.v[5], n.v[10], ACT.Ln))


def tanh_scalar(m, act, stage, width=NL):
    n = m.n
    squares_scalar(m, act, stage, width)
    n.scalar.wait(act, stage + " root")
    n.scalar.reach(stage + " tanh", act.activation(n.wide[5][:, 0:width], n.wide[4][:, 0:width], ACT.Tanh))


def tanh_ratio_vector(m, dve, step, stage, width=NL):
    n, v = m.n, [w[:, 0:width] for w in m.n.wide]
    n.scalar.wait(dve, stage + " tanh")
    step.mark(dve.tensor_scalar(v[6], v[4], MIN_NORM, None, ALU.max))
    step(dve.tensor_scalar(v[7], v[5], MIN_NORM, EDGE_OF_BALL, ALU.max, ALU.min))
    step(dve.reciprocal(v[8], v[6]))
    step(dve.tensor_tensor(v[14], v[7], v[8], ALU.mult))


def by_heads(m):
    heads = m.flat.rearrange("(h p l d) -> h p l d", h=H1, p=NP, l=NL)
    return [(m.h[0:NP, :, i * D // H1:(i + 1) * D // H1], heads[i]) for i in range(H1)]


def d_sync(m, io, sp):
    n = m.n
    n.vector.wait(sp, "C rows")
    load(m, sp, [(n.w[:, :, 0:D], io["w_hyp"]), (n.b_lin, spread(io["b_lin"], NP, D)), (n.b_conv, spread(io["b_conv"], NP, D)),
                 (n.att, spread(io["att_hyp"], P, 2 * D).rearrange("p (a d) -> p a d", a=2))])
    n.vector.wait(sp, "D rows")
    rows = m.h[0:NP, :, :].rearrange("p l d -> p (l d)")
    load(m, sp, two_parts(m.flat.rearrange("(p c) -> p c", p=NP), rows))
    load(m, sp, [part for pair in by_heads(m) for part in two_parts(*pair)])
    flat = "p l d -> p (l d)"
    load(m, sp, two_parts(node_rows(m.row_table, D).rearrange(flat), m.h[0:NP, :, :].rearrange(flat)))
    n.vector.wait(sp, "D terms")
    load(m, sp, [(node_rows(m.dst_table, H1).rearrange(flat), m.terms[:, 1].rearrange(flat))])


def tables_sync(m, sp, label):
    m.n.vector.wait(sp, label)
    flat = "p l d -> p (l d)"
    load(m, sp, two_parts(node_rows(m.row_table, D).rearrange(flat), m.h[0:NP, :, :].rearrange(flat))
         + [(node_rows(m.dst_table, H1).rearrange(flat), m.terms[:, 1].rearrange(flat))])


def d_vector(m, dve, step):
    n = m.n
    norm_vector(m, dve, step, "D", m.x)
    atanh_ratio_vector(m, dve, step, "D", 1.0 - 1e-7, "D factor")
    n.sync.wait(dve, "D weights")

    read_products(m, dve, "D", lambda l, k: dve.tensor_copy(row(m.h, l), m.banks[k][0:NP, 0:D]))
    n.vector.wait(dve, "D product")
    b2, hb = n.out[:, 0, 0:D], n.out[:, 0, D:2 * D]
    step(dve.tensor_tensor(b2, n.b_lin, n.b_lin, ALU.mult))
    n.vector.reach("D2 square", dve.tensor_reduce(n.wide[3][:, NL:NL + 1], b2, AX.X, ALU.add))
    tanh_ratio_vector(m, dve, step, "D2", NL + 1)
    v, one = n.v, lambda i: n.wide[i][:, NL:NL + 1]
    step(dve.tensor_scalar(hb, n.b_lin, one(14), None, ALU.mult))
    big = [NP, NL, D]
    t = m.sums[0:NP, NL * D:2 * NL * D].rearrange("p (l d) -> p l d", l=NL)
    h = m.h[0:NP, :, :]

    def along(value):
        return value.unsqueeze(2).to_broadcast(big)

    step(dve.tensor_tensor(t, h, hb.unsqueeze(1).to_broadcast(big), ALU.mult))
    step(dve.tensor_reduce(v[9], t, AX.X, ALU.add))
    step(dve.tensor_tensor(v[9], v[9], v[14], ALU.mult))
    step.mark(dve.tensor_tensor(v[10], v[7], v[7], ALU.mult))
    step.mark(dve.tensor_tensor(one(10), one(7), one(7), ALU.mult))
    step(dve.tensor_scalar(v[11], v[9], 2.0, 1.0, ALU.mult, ALU.add))
    step(dve.tensor_scalar(v[12], v[10], one(10), None, ALU.mult))
    step(dve.tensor_tensor(v[12], v[12], v[11], ALU.add))
    step(dve.tensor_scalar(v[12], v[12], MIN_NORM, None, ALU.max))
    step(dve.reciprocal(v[12], v[12]))
    step(dve.tensor_scalar(v[11], v[11], one(10), None, ALU.add))
    step(dve.tensor_tensor(v[11], v[11], v[14], ALU.mult))
    step(dve.tensor_tensor(v[11], v[11], v[12], ALU.mult))
    step(dve.tensor_scalar(v[10], v[10], -1.0, 1.0, ALU.mult, ALU.add))
    step(dve.tensor_tensor(v[10], v[10], v[12], ALU.mult))
    step(dve.tensor_tensor(t, h, along(v[11]), ALU.mult))
    step(dve.tensor_tensor(h, hb.unsqueeze(1).to_broadcast(big), along(v[10]), ALU.mult))
    n.vector.reach("D sum", dve.tensor_tensor(h, t, h, ALU.add))
    atanh_ratio_vector(m, dve, step, "D3", EDGE_OF_BALL, None)
    n.vector.reach("D rows", dve.tensor_tensor(h, h, along(v[14]), ALU.mult))
    n.sync.wait(dve, "D rows")
    for a in range(2):
        step(dve.tensor_tensor(t, h, n.att[0:NP, a, :].unsqueeze(1).to_broadcast(big), ALU.mult))
        last = dve.tensor_reduce(m.terms[:, a].rearrange("p l h -> p (l h)"),
                                 t.rearrange("p l (h d) -> p (l h) d", h=H1), AX.X, ALU.add)
        if a == 0:
            step(last)
    n.vector.reach("D terms", last)


def read_products(m, dve, p, read):
    n = m.n
    with dve.Fori(0, NL // J) as it:
        for k in range(J):
            l = it * J + k
            done(dve, n.out_ready, p, l)
            read(l, k).then_inc(n.out_read.sem, 1)
    done(dve, n.out_read, p, NL - 1)
    dve.sem_inc(n.vector.sem, NL)
    n.vector.n += 1


def d_scalar(m, act):
    n = m.n
    norm_scalar(m, act, "D")
    each_node(act, n.scalar, lambda l, k: act.activation(row(m.h, l), row(m.x, l), ACT.Relu,
                                                         bias=n.nb[:, bass.ds(l, 1)], scale=n.rs[:, bass.ds(l, 1)]))
    n.scalar.wait(act, "D rows")
    atanh_scalar(m, act, "D")
    n.vector.wait(act, "D factor")
    pass_scalar(m, act, "D", lambda l, k: act.activation(n.z[:, k, :], row(m.h, l), ACT.Copy,
                                                         scale=n.v[14][:, bass.ds(l, 1)]),
                lambda l, k: turn_back(m, act, k))
    n.vector.wait(act, "D product")
    tanh_scalar(m, act, "D2", NL + 1)
    n.vector.wait(act, "D sum")
    atanh_scalar(m, act, "D3")


def d_tensor(m, pe):
    m.n.sync.wait(pe, "D weights")
    pass_tensor(m, pe, "D", product_of(m, pe, m.n.w, D))


def keys_pool(m, pool):
    for j in range(J):
        pool.wait_ge(m.n.stored[j], 48 * NL // J)
    pool.memset(m.src_i[:, T:TP], 0).then_inc(m.pool_step, 1)
    pool.wait_ge(m.pool_step, 2)
    gather(m, pool, "keys", m.k_table, D, lambda it, j: pool.wait_ge(m.sc.sources_in, it + 1))



def terms_pool(m, pool, i, tables):
    n, s = m.n, m.st
    n.sync.wait(pool, tables)
    for l in range(NL):
        pool.indirect_dma_start(out=m.at_starts[:, :],
                                out_offset=bass.IndirectOffsetOnAxis(ap=m.start_i[0:NP, l:l + 1], axis=0),
                                in_=m.terms[:, 1, l, :], in_offset=None).then_inc(s.scattered.sem, 16)
    s.scattered.sent += 16 * NL
    s.first_filled.send(pool.indirect_dma_start(out=s.fill0, out_offset=None, in_=m.dst_table[:, :],
                                                in_offset=bass.IndirectOffsetOnAxis(ap=s.first_i, axis=0)), 16)
    gather(m, pool, f"rows{i}", m.row_table, D)



def place_lookup(m):
    s = m.lk = Memory()
    wide = K * P
    z = m.sums
    s.digits = z[:, 0:J * wide // 2].bitcast(BF16).rearrange("p (j c) -> p j c", j=J)
    at = J * wide // 2
    s.one_low = z[:, at:at + J * K * NL].rearrange("p (j k l) -> p j k l", j=J, l=NL)
    at += J * K * NL
    s.masked = z[:, at:at + 3 * K * NL * H1].rearrange("p (j k l h) -> p j k l h", j=3, k=K, l=NL)
    at += 3 * K * NL * H1
    above = 4 * H1 * SL
    s.high, s.sum = z[:, above:above + TP], z[:, above + TP:above + 2 * TP]
    assert at <= 3 * H1 * SL
    s.low = m.w1[:, :, :].rearrange("p a c -> p (a c)")[:, 1300:1300 + TP]
    s.one_high = m.sel[0:NP, :, :].rearrange("p (j k) c -> p j (k c)", j=J)
    s.digits_in = [m.sem(f"lookup_digits_in{j}") for j in range(J)]
    s.told = m.sem("lookup_distances")
    s.chosen = m.sem("lookup_chosen")
    s.found = m.sem("lookup_found")
    s.masks = m.sem("lookup_masked")
    s.copied = m.sem("lookup_copied")
    s.place = m.n.cols[0:NP, 16:17]


def terms_sync(m, sp, i):
    s, st = m.lk, m.st
    with sp.Fori(0, IT) as it:
        for j in range(J):
            sp.wait_ge(s.chosen, it * J + j + G * i + 1)
            sp.dma_start(s.digits[:, j, :], m.digit_rows[0:1, bass.ds((it * J + j) * K * P, K * P)]
                         .to_broadcast([P, K * P])).then_inc(s.digits_in[j], 16)
    st.scattered.receive(sp, 16 * NL)
    st.fill_in.send(sp.dma_start(st.arrays[H1][3].rearrange("p h c -> p (h c)"),
                                 m.at_starts.rearrange("(s c) h -> s (c h)", s=NS)), 16)


def terms_scalar(m, act, i):
    s = m.lk
    if not i:
        act.sem_inc(s.chosen, J)
    with act.Fori(0, IT) as it:
        for j in range(J):
            g = it * J + j + G * i
            act.wait_ge(s.digits_in[j], 16 * (it + IT * i + 1))
            act.wait_ge(s.found, g + 1)
            act.activation(s.one_high[:, j, :], s.digits[0:NP, j, :], ACT.Abs, scale=-1.0, bias=s.place
                           ).then_inc(s.told, 1)
            act.wait_ge(s.told, g + 1)
            act.activation(s.one_high[:, j, :], s.one_high[:, j, :], ACT.Relu, scale=-1.0, bias=1.0
                           ).then_inc(s.chosen, 1)


def terms_tensor(m, pe, i):
    s = m.lk
    if not i:
        pe.sem_inc(s.found, J)
    terms = m.terms[:, 0].rearrange("p l h -> p (l h)")
    width = NL * H1
    with pe.Fori(0, IT) as it:
        for j in range(J):
            g = it * J + j + G * i
            pe.wait_ge(s.chosen, J + g + 1)
            pe.wait_ge(s.masks, 2 * g + 2)
            for k in range(K):
                last = pe.matmul(m.banks[2 * (j % 3) + k // 4][:, k % 4 * width:(k % 4 + 1) * width],
                                 s.one_high[:, j, k * P:(k + 1) * P], terms, start=True, stop=True)
            last.then_inc(s.found, 1)


def terms_vector(m, dve, step, i):
    s = m.lk
    if not i:
        dve.sem_inc(s.masks, 4)
    m.n.vector.wait(dve, f"H{i - 1} rows" if i else "D terms")
    step(dve.tensor_scalar(s.sum, m.src_i[:, :], 1.0 / NL, -(0.5 - 0.5 / NL), ALU.mult, ALU.add))
    step(dve.tensor_scalar(s.sum, s.sum, 12582912.0, None, ALU.add))
    step(dve.tensor_scalar(s.high, s.sum, -12582912.0, None, ALU.add))
    step(dve.scalar_tensor_tensor(s.low, s.high, -float(NL), m.src_i[:, :], ALU.mult, ALU.add))
    half = K // 2

    def choose_low(g, j):
        return dve.tensor_tensor(s.one_low[:, j], m.iota[:, 0:NL].unsqueeze(1).to_broadcast([P, K, NL]),
                                 s.low[:, bass.ds(g * K, K)].unsqueeze(2).to_broadcast([P, K, NL]), ALU.is_equal)

    step(choose_low(0, 0))
    with step.loop(IT, J) as it:
        for j in range(J):
            g = it * J + j + G * i
            dve.wait_ge(s.found, J + g + 1)
            for b in range(2):
                dve.tensor_tensor(s.masked[:, j % 3, b * half:(b + 1) * half],
                                  m.banks[2 * (j % 3) + b][:, 0:half * NL * H1]
                                  .rearrange("p (k l h) -> p k l h", k=half, l=NL),
                                  s.one_low[:, j, b * half:(b + 1) * half].unsqueeze(3)
                                  .to_broadcast([P, half, NL, H1]), ALU.mult).then_inc(s.masks, 1)
            step(choose_low(it * J + j + 1, (j + 1) % J))
            dve.tensor_reduce(m.edge[:, bass.ds((it * J + j) * K * H1, K * H1)].rearrange("p (k h) -> p k h", h=H1),
                              s.masked[:, j % 3].rearrange("p k l h -> p k h l"), AX.X, ALU.add).then_inc(s.copied, 1)
    dve.wait_ge(s.copied, G * (i + 1))
    dve.sem_inc(m.st.scores_there.sem, 1)
    m.st.scores_there.sent += 1



def bias_scalar(m, act, label, bias, func=ACT.Identity):
    n = m.n
    n.vector.wait(act, label)
    for f in range(2):
        last = act.activation(m.acc[:, f, 0:N], m.acc[:, f, 0:N], func, bias=bias[:, f:f + 1])
    n.scalar.reach(label, last)
    n.scalar.wait(act, label)


def f_scalar(m, act):
    m.n.vector.wait(act, "F sum")
    sums_scalar(m, act, "F")
    m.n.vector.wait(act, "F relu")
    tanh_scalar(m, act, "F")


def f_sync(m, sp):
    m.n.vector.wait(sp, "F product")
    load(m, sp, [part for rows, flat in by_heads(m) for part in two_parts(flat, rows)])
    load(m, sp, two_parts(m.h[0:NP, :, :].rearrange("p l d -> p (l d)"), m.flat.rearrange("(p c) -> p c", p=NP)))


def f_tensor(m, pe):
    pass_tensor(m, pe, "F", rows_of(m, pe))


def f_vector(m, dve, step):
    n = m.n
    sums_there(m, dve, "F sum")
    read_products(m, dve, "F", lambda l, k: dve.tensor_copy(row(m.h, l), m.banks[k][0:NP, 0:D]))
    n.sync.wait(dve, "F rows")
    h = m.h[0:NP, :, :]
    step(dve.tensor_tensor(h, h, n.b_conv.unsqueeze(1).to_broadcast([NP, NL, D]), ALU.add))
    n.vector.reach("F relu", dve.tensor_scalar(h, h, 0.0, None, ALU.max))
    tanh_ratio_vector(m, dve, step, "F")
    each_node(dve, n.vector, lambda l, k: dve.scalar_tensor_tensor(
        row(m.x, l), row(m.h, l), n.v[14][:, bass.ds(l, 1)], row(m.x, l), ALU.mult, ALU.add))
    n.vector.wait(dve, "F rows")



def place_masked(m):
    s = m.mk = Memory()
    s.sources = m.rows
    s.weighted = m.sums[:, 2 * ACOLS:2 * ACOLS + J * K * P].rearrange("p (t c) -> p t c", c=P)
    w = m.w2[:, :, :].rearrange("p a d -> p (a d)")
    s.fields = w[:, 0:J * K * 4].rearrange("p (j k f) -> p j k f", j=J, k=K)
    s.key = w[:, 160:168]
    s.later = w[:, 168:176]
    s.source = w[:, 176:192].rearrange("p (f k) -> p f k", f=2)
    s.shift = w[:, 192:200]
    s.junk = w[:, 256:256 + K * P]
    s.turns = w[:, 200:201]
    s.turns_i = w[:, 201:202].bitcast(I32)
    s.step = m.sem("masked_step")
    s.base_out = m.sem("masked_base_out")
    s.loc = m.w1[:, :, :].rearrange("p a c -> p (a c)")[:, 1300:1300 + T]
    s.fields_free = m.sem("masked_fields_free")
    s.keys = m.sem("masked_keys")
    s.keys_out = m.sem("masked_keys_out")
    s.chosen = m.sem("masked_chosen")
    s.products = m.sem("masked_products")
    s.merged = m.sem("masked_merged")
    s.fields_in = [m.sem(f"masked_fields_in{j}") for j in range(J)]


MASKED_TURN = J * K * P


def masked_turns(m, engine):
    at = D // NL
    _, turns = m.nc.values_load_multi_w_load_instructions(
        m.mk.turns_i[at:at + 1, 0:1], engines=[engine], min_val=1, max_val=IT,
        skip_runtime_bounds_check_because="it is at least 1, and no more than all edges take")
    return turns[0]


def g_sync(m, sp):
    s = m.mk
    m.n.vector.wait(sp, "G turns")
    with sp.Fori(0, masked_turns(m, ENGINE.SP)) as it:
        for j in range(J):
            g = it * J + j
            sp.wait_ge(s.fields_free, g + 1)
            sp.dma_start(s.fields[:, j], m.sorted.rearrange("(g k p) r -> p g k r", k=K, p=P)
                         [:, bass.ds(g, 1), :, 0:4].rearrange("p g k r -> p (g k) r")).then_inc(s.fields_in[j], 16)


def g_vector(m, dve, step):
    n, s = m.n, m.mk
    place = m.start_i[0:NP, D % NL:D % NL + 1]
    step(dve.tensor_copy(s.turns[0:NP, :], place))
    step(dve.tensor_scalar(s.turns[0:NP, :], s.turns[0:NP, :], 1.0 / MASKED_TURN, 0.5 - 0.5 / MASKED_TURN,
                           ALU.mult, ALU.add))
    step(dve.tensor_scalar(s.turns[0:NP, :], s.turns[0:NP, :], 12582912.0, None, ALU.add))
    step(dve.tensor_scalar(s.turns[0:NP, :], s.turns[0:NP, :], -12582912.0, 1.0, ALU.add, ALU.max))
    n.vector.reach("G turns", dve.tensor_copy(s.turns_i[0:NP, :], s.turns[0:NP, :]))
    norm_vector(m, dve, step, "G", m.x)
    dve.sem_inc(s.fields_free, J)
    step(dve.memset(m.acc, 0.0))
    dve.wait_ge(s.base_out, 1)
    step(dve.tensor_tensor(s.loc, m.ag.loc, m.banks[6][:, 0:T], ALU.subtract))
    step = Chain(dve, s.step)
    tile = [P, K, P]
    with step.loop(masked_turns(m, ENGINE.DVE), J * 26) as it:
        for j in range(J):
            g = it * J + j
            dve.wait_ge(s.fields_in[j], 16 * it + 16)
            source, weight, given = (s.fields[:, j, :, f] for f in (0, 2, 3))
            step(dve.tensor_scalar(s.shift, s.loc[:, bass.ds(g * K, K)], 1.0, None, ALU.add))
            step(dve.scalar_tensor_tensor(s.key, source, float(P), s.shift, ALU.mult, ALU.add))
            dve.tensor_tensor(s.key, s.key, given, ALU.mult).then_inc(s.keys, 1)
            slots = slice(j * K, (j + 1) * K)
            step(dve.tensor_tensor(m.sel[:, slots, :], m.iota.unsqueeze(1).to_broadcast(tile),
                                   s.loc[:, bass.ds(g * K, K)].unsqueeze(2).to_broadcast(tile), ALU.is_equal))
            step.mark(dve.tensor_tensor(s.weighted[:, slots, :], m.sel[:, slots, :],
                                        weight.unsqueeze(2).to_broadcast(tile), ALU.mult))
            dve.wait_ge(s.keys_out, g + 1)
            for k in range(K):
                ins = dve.scalar_tensor_tensor(s.junk[:, k * P:(k + 1) * P],
                                               m.banks[4 + k // 4][:, (k % 4) * P:(k % 4 + 1) * P],
                                               s.key[:, k:k + 1], m.after, ALU.is_equal, ALU.mult,
                                               accum_out=s.later[:, k:k + 1])
            step(ins)
            step(dve.scalar_tensor_tensor(s.later, s.later, 0.0, given, ALU.is_equal, ALU.mult))
            step(dve.tensor_scalar(s.source[:, 0], source, 1.0, None, ALU.add))
            step(dve.tensor_tensor(s.source[:, 0], s.source[:, 0], s.later, ALU.mult))
            step(dve.tensor_scalar(s.source[:, 1], s.source[:, 0], -1.0 - P, None, ALU.add))
            step(dve.tensor_scalar(s.source[:, 0], s.source[:, 0], -1.0, None, ALU.add))
            for f in range(2):
                dve.tensor_tensor(s.sources[:, slots, f * P:(f + 1) * P], m.iota.unsqueeze(1).to_broadcast(tile),
                                  s.source[:, f].unsqueeze(2).to_broadcast(tile), ALU.is_equal).then_inc(s.chosen, 1)
            dve.wait_ge(s.chosen, 2 * g + 2)
            dve.sem_inc(s.fields_free, 1)
            first = windows(m, ENGINE.DVE, g)
            for k in range(K):
                dve.wait_ge(s.products, K * g + k + 1)
                bank = m.banks[k % 4][:, :].rearrange("p (f c) -> p f c", f=2)
                old = s.junk[:, 0:2 * P].rearrange("p (f c) -> p f c", f=2)
                w = m.acc[:, :, bass.ds(first[k], P)]
                step(dve.tensor_tensor(old, w, bank[:, :, 0:P], ALU.mult))
                step(dve.tensor_tensor(w, w, old, ALU.subtract))
                dve.tensor_tensor(w, w, bank[:, :, P:2 * P], ALU.add).then_inc(s.merged, 1)
                dve.wait_ge(s.merged, 4 + K * g + k + 1)
    n.vector.reach("G weights", dve.memset(s.later, 0.0))
    read_products(m, dve, "G", lambda l, k: dve.tensor_tensor(row(m.x, l), m.banks[k][0:NP, 0:D], row(m.x, l),
                                                              ALU.add))
    n.vector.wait(dve, "G rows")


def g_tensor(m, pe):
    s = m.mk
    pe.sem_inc(s.merged, 4)
    m.n.vector.wait(pe, "G turns")
    pe.matmul(m.banks[6][:, 0:T], m.first_row, m.ag.loc, start=True, stop=True).then_inc(s.base_out, 1)
    with pe.Fori(0, masked_turns(m, ENGINE.PE)) as it:
        for j in range(J):
            g = it * J + j
            pe.wait_ge(s.keys, g + 1)
            pe.wait_ge(s.chosen, 2 * g)
            for k in range(K):
                last = pe.matmul(m.banks[4 + k // 4][:, (k % 4) * P:(k % 4 + 1) * P],
                                 s.key[:, k:k + 1].to_broadcast([P, P]), m.ident, start=True, stop=True)
            last.then_inc(s.keys_out, 1)
            pe.wait_ge(s.chosen, 2 * g + 2)
            for k in range(K):
                pe.wait_ge(s.merged, K * g + k + 1)
                for f in range(2):
                    for i, side in enumerate((m.sel, s.weighted)):
                        last = pe.matmul(m.banks[k % 4][:, (2 * f + i) * P:(2 * f + i + 1) * P],
                                         s.sources[:, j * K + k, f * P:(f + 1) * P], side[:, j * K + k, :],
                                         start=True, stop=True)
                last.then_inc(s.products, 1)
    m.n.vector.wait(pe, "G weights")
    pass_tensor(m, pe, "G", product_of(m, pe, m.acc, D))


def g_scalar(m, act):
    norm_scalar(m, act, "G")
    m.n.vector.wait(act, "G weights")
    pass_scalar(m, act, "G", normed(m, act, m.x, ACT.Relu), lambda l, k: turn_back(m, act, k))



def h_sync(m, io, sp, i):
    n = m.n
    n.vector.wait(sp, f"H{i - 1} rows" if i else "G rows")
    load(m, sp, [(n.w[:, :, 0:D], io[f"w3_{i}"]),
                 (n.att, spread(io[f"att3_{i}"], P, 2 * D).rearrange("p (a d) -> p a d", a=2))])
    tables_sync(m, sp, f"H{i} rows")


def h_vector(m, dve, step, i):
    n = m.n
    if i == 0:
        norm_vector(m, dve, step, "H", m.x)
    n.sync.wait(dve, f"H{i} weights")
    for a in range(2):
        step(dve.tensor_tensor(n.scratch, n.w[:, :, 0:D], n.att[:, a].unsqueeze(1).to_broadcast([P, 2, D]), ALU.mult))
        at = D + a * H1
        last = dve.tensor_reduce(n.w[:, :, at:at + H1], n.scratch.rearrange("p f (h d) -> p f h d", h=H1),
                                 AX.X, ALU.add)
        if a == 0 or i:
            step(last)
    if i == 0:
        n.vector.reach(f"H{i} weights", last)
    else:
        sums_there(m, dve, f"H{i} sum")
    with dve.Fori(0, NL // J) as it:
        for k in range(J):
            l = it * J + k
            done(dve, n.out_ready, f"H{i}", l)
            dve.tensor_copy(row(m.h, l), m.banks[k][0:NP, 0:D])
            dve.tensor_copy(m.terms[:, :, bass.ds(l, 1), :].rearrange("p a l h -> p a (l h)"),
                            m.banks[k][0:NP, D:D + 2 * H1].rearrange("p (a h) -> p a h", a=2)
                            ).then_inc(n.out_read.sem, 1)
    done(dve, n.out_read, f"H{i}", NL - 1)
    dve.sem_inc(n.vector.sem, NL)
    n.vector.n += 1


def h_scalar(m, act, i):
    n = m.n
    if i == 0:
        norm_scalar(m, act, "H")
        pass_scalar(m, act, "H0", normed(m, act, m.x, ACT.Relu), lambda l, k: turn_back(m, act, k))
    else:
        bias_scalar(m, act, f"H{i} sum", n.b3[i - 1])
        sums_scalar(m, act, f"H{i}")


def h_tensor(m, pe, i):
    m.n.vector.wait(pe, f"H{i} sum" if i else "H0 weights")
    pass_tensor(m, pe, f"H{i}", product_of(m, pe, m.n.w, D + 2 * H1))


def j_vector(m, dve):
    sums_there(m, dve, "J sum")
    read_products(m, dve, "J", lambda l, k: dve.tensor_tensor(row(m.x, l), m.banks[k][0:NP, 0:D], row(m.x, l),
                                                              ALU.add))


def j_scalar(m, act):
    bias_scalar(m, act, "J sum", m.n.b3[2])
    sums_scalar(m, act, "J")


def j_tensor(m, pe):
    pass_tensor(m, pe, "J", rows_of(m, pe))


def j_sync(m, out, sp):
    n = m.n
    rows = out.rearrange("(p l) d -> p l d", l=NL)
    with sp.Fori(0, NL // J) as it:
        done(sp, n.out_read, "J", it * J + J - 1)
        for to, of in two_parts(rows[:, bass.ds(it * J, J), :], m.x[0:NP, bass.ds(it * J, J), :]):
            sp.dma_start(to, of).then_inc(n.output_stored, 16)
    sp.wait_ge(n.output_stored, 32 * NL // J)


def build(nc, io, out):
    with ExitStack() as ctx:
        m = place_memory(nc, ctx)
        place_nodes(m)
        place_sort(m)
        place_scores(m)
        place_strips(m)
        place_masked(m)
        place_lookup(m)
        plan_gathers(m)
        plan_aggregates(m)
        block = ctx.enter_context(nc.Block())

        @block.sync
        def _(sp):
            a_sync(m, io, sp)
            sort_sync(m, io, sp)
            fields_sync(m, sp)
            scores_sync(m, sp)
            b_sync(m, io, sp)
            d_sync(m, io, sp)
            terms_sync(m, sp, 0)
            f_sync(m, sp)
            g_sync(m, sp)
            for i in LAYERS:
                h_sync(m, io, sp, i)
                terms_sync(m, sp, i + 1)
            j_sync(m, out, sp)

        @block.vector
        def _(dve):
            step = Chain(dve, m.vector_step)
            a_vector(m, dve, step)
            sort_vector(m, dve, step)
            fields_vector(m, dve, step)
            flags_vector(m, dve, step)
            scores_vector(m, dve, step)
            numbers_vector(m, dve, step)
            strips_vector(m, dve, step, H0, least=MIN_NORM)
            aggregate_vector(m, dve, step, "values", H0)
            b_vector(m, dve, step)
            c_vector(m, dve, step)
            d_vector(m, dve, step)
            terms_vector(m, dve, step, 0)
            numbers_vector(m, dve, step)
            strips_vector(m, dve, step, H1, slope=0.2, least=MIN_NORM)
            aggregate_vector(m, dve, step, "rows0", H1)
            f_vector(m, dve, step)
            g_vector(m, dve, step)
            for i in LAYERS:
                h_vector(m, dve, step, i)
                terms_vector(m, dve, step, i + 1)
                numbers_vector(m, dve, step)
                strips_vector(m, dve, step, H1, slope=0.2, more=1e-16)
                aggregate_vector(m, dve, step, f"rows{i + 1}", H1)
            j_vector(m, dve)

        @block.tensor
        def _(pe):
            a_tensor(m, pe)
            sort_tensor(m, pe)
            fields_tensor(m, pe)
            flags_tensor(m, pe)
            scores_tensor(m, pe)
            strips_tensor(m, pe, H0)
            aggregate_tensor(m, pe, "values")
            b_tensor(m, pe)
            c_tensor(m, pe)
            d_tensor(m, pe)
            terms_tensor(m, pe, 0)
            strips_tensor(m, pe, H1)
            aggregate_tensor(m, pe, "rows0")
            f_tensor(m, pe)
            g_tensor(m, pe)
            for i in LAYERS:
                h_tensor(m, pe, i)
                terms_tensor(m, pe, i + 1)
                strips_tensor(m, pe, H1)
                aggregate_tensor(m, pe, f"rows{i + 1}")
            j_tensor(m, pe)

        @block.scalar
        def _(act):
            step = Chain(act, m.scalar_step)
            a_scalar(m, act)
            sort_scalar(m, act)
            fields_scalar(m, act)
            scores_scalar(m, act, step)
            strips_scalar(m, act, H0)
            aggregate_scalar(m, act, step, "values")
            b_scalar(m, act)
            c_scalar(m, act)
            d_scalar(m, act)
            terms_scalar(m, act, 0)
            strips_scalar(m, act, H1)
            aggregate_scalar(m, act, step, "rows0")
            f_scalar(m, act)
            g_scalar(m, act)
            for i in LAYERS:
                h_scalar(m, act, i)
                terms_scalar(m, act, i + 1)
                strips_scalar(m, act, H1)
                aggregate_scalar(m, act, step, f"rows{i + 1}")
            j_scalar(m, act)

        @block.gpsimd
        def _(pool):
            sort_pool(m, pool)
            keys_pool(m, pool)
            gather(m, pool, "values", m.row_table, D)
            terms_pool(m, pool, 0, "D tables")
            for i in LAYERS:
                terms_pool(m, pool, i + 1, f"H{i} tables")


def layout(a):
    f = np.float32
    loop = np.arange(N, dtype=np.int32)
    src = np.concatenate([a["src"], loop, np.zeros(EP - EL, np.int32)]).astype(np.int32)
    dst = np.concatenate([a["dst"], loop, np.full(EP - EL, N, np.int32)]).astype(np.int32)
    weight = np.concatenate([a["edge_weight"], np.zeros(EP - E, f)])
    given = np.concatenate([np.ones(E, f), np.zeros(EP - E, f)])

    def tiles(v):
        return np.ascontiguousarray(v.reshape(T, P).T)

    ef = np.zeros((ED + 1, EP), f)
    ef[0:ED, 0:E] = a["edge_attr_64"].T
    ef[ED, :] = 1.0
    row, col = np.indices((P, P))
    consts = np.stack([col, col < row, col > row, col == row, row == 0, row == col - 1, row == col + 1], 1).astype(f)
    out = dict(x=a["x"], src_tiles=tiles(src), dst_tiles=tiles(dst), weight_tiles=tiles(weight),
               given_tiles=tiles(given), dst_row=dst[None, :], efT=ef, consts=consts,
               We=np.concatenate([a["L0_gnn_We"], a["L0_gnn_be"][None, :]]))
    return {k: np.ascontiguousarray(v) for k, v in out.items()}
def node_inputs(a):
    f = np.float32

    def halves(w):
        return np.ascontiguousarray(w.reshape(2, P, -1).transpose(1, 0, 2))

    def col(v):
        return v.reshape(-1, P).T

    cols = [col(a["L0_gnn_" + k]) for k in ("ln1_g", "ln1_b", "ln2_g", "ln2_b", "b1")]
    place = np.arange(P)
    cols += [np.stack([place, place // H1], 1)] + [col(a[f"L3_gnn_b{i}"]) for i in range(3)]
    cols += [np.broadcast_to(a["L0_gnn_alpha"], (P, 1)), np.broadcast_to(a["L0_gnn_beta"], (P, 1)),
             place[:, None] % H1 == np.arange(H1)]
    out = dict(cols=np.concatenate(cols, 1),
               qkv=halves(np.concatenate([a["L0_gnn_Wq"], a["L0_gnn_Wk"], a["L0_gnn_Wv"]], 1)),
               qkv_bias=np.concatenate([a["L0_gnn_bq"], a["L0_gnn_bk"], a["L0_gnn_bv"]])[None],
               wo=halves(a["L0_gnn_Wo"]), bo=a["L0_gnn_bo"][None], b_ff=a["L0_gnn_b2"][None],
               w1=halves(a["L0_gnn_W1"]), w2=a["L0_gnn_W2"].reshape(FF // P, P, D).transpose(1, 0, 2),
               w_hyp=halves(a["L1_gnn_W"].T), b_lin=a["L1_gnn_b_lin"][None], b_conv=a["L1_gnn_b_conv"][None],
               att_hyp=np.concatenate([a["L1_gnn_att"][:, 64:].reshape(-1), a["L1_gnn_att"][:, :64].reshape(-1)])[None])
    for i in range(3):
        out[f"w3_{i}"] = halves(a[f"L3_gnn_W{i}"])
        out[f"att3_{i}"] = np.concatenate([a[f"L3_gnn_as{i}"].reshape(-1), a[f"L3_gnn_ad{i}"].reshape(-1)])[None]
    return {k: np.ascontiguousarray(v, dtype=f) for k, v in out.items()}


def kernel(**a):
    from concourse import bacc
    from concourse.bass_utils import run_bass_kernel_spmd

    nc = bacc.Bacc("TRN2", target_bir_lowering=False, num_devices=1)
    a = {k: np.asarray(v) for k, v in a.items()}
    arrays = {"in_" + k: v for k, v in {**layout(a), **node_inputs(a)}.items()}
    io = {k[3:]: nc.dram_tensor(k, v.shape, mybir.dt.from_np(v.dtype), kind="ExternalInput").ap()
          for k, v in arrays.items()}
    out = nc.dram_tensor("out", (N, D), F32, kind="ExternalOutput").ap()
    build(nc, io, out)
    result = run_bass_kernel_spmd(nc, [arrays], core_ids=[0])
    return result.results[0]["out"]
```
